# Optimizing a Trainium2 kernel written in Bass

```python
import numpy as np
import jax
import jax.numpy as jnp

def _softmax(x, axis=-1):
    return jax.nn.softmax(x, axis=axis)

def _gelu(x):
    return jax.nn.gelu(x, approximate=True)

def _silu(x):
    return jax.nn.silu(x)

def _sigmoid(x):
    return jax.nn.sigmoid(x)

def _layernorm(x, axis=-1, eps=1e-05):
    m = jnp.mean(x, axis=axis, keepdims=True)
    v = jnp.var(x, axis=axis, keepdims=True)
    return (x - m) / jnp.sqrt(v + eps)

def _scatter_add(tgt, idx, src, axis=0):
    return tgt.at[idx].add(src)

def _segment_sum(src, seg, n):
    return jax.ops.segment_sum(src, seg, n)
kernel_name = 'mk_recurrent_d1_jaxref_r4_57ef6a'

def setup_inputs(seed: int=0):
    np.random.seed(seed)
    _w = jnp.asarray

    def _L0_attn_setup():
        import jax, jax.numpy as jnp
        import numpy as np
        import math
        NUM_HEADS = 8
        EMB = 256
        HEAD_DIM = 128
        B, T = (1, 1024)

        def sinusoidal_pe(T, d, dtype=jnp.float32):
            pos = jnp.arange(T, dtype=dtype)[:, None]
            inv_freq = jnp.exp(-math.log(10000.0) * jnp.arange(0, d, 2, dtype=dtype) / d)
            ang = pos * inv_freq[None, :]
            pe = jnp.zeros((T, d), dtype=dtype)
            pe = pe.at[:, 0::2].set(jnp.sin(ang))
            pe = pe.at[:, 1::2].set(jnp.cos(ang))
            return pe
        key = jax.random.key(seed)
        ks = jax.random.split(key, 6)
        s = lambda fan_in: 1.0 / math.sqrt(fan_in)
        x = jax.random.normal(ks[0], (B, T, EMB), dtype=jnp.float32)
        Wq = jax.random.normal(ks[1], (EMB, NUM_HEADS * HEAD_DIM), dtype=jnp.float32) * s(EMB)
        bq = jax.random.normal(ks[2], (NUM_HEADS * HEAD_DIM,), dtype=jnp.float32) * s(EMB)
        Wkv = jax.random.normal(ks[3], (EMB, 2 * HEAD_DIM), dtype=jnp.float32) * s(EMB)
        bkv = jax.random.normal(ks[4], (2 * HEAD_DIM,), dtype=jnp.float32) * s(EMB)
        Wo = jax.random.normal(ks[5], (NUM_HEADS * HEAD_DIM, EMB), dtype=jnp.float32) * s(NUM_HEADS * HEAD_DIM)
        return {'x': x, 'Wq': Wq, 'bq': bq, 'Wkv': Wkv, 'bkv': bkv, 'Wo': Wo}
    _L0_attn_in = _L0_attn_setup()

    def _L0_ffn_setup():
        import jax, jax.numpy as jnp
        import numpy as np
        NEG_INF = -1e+30

        def _moe_forward(x, router_w, router_b, w1, b1, w2, b2, top_k=2):
            B, S, D = x.shape
            E = router_w.shape[1]
            logits = jnp.einsum('bsd,de->bse', x, router_w) + router_b
            top_vals, top_idx = jax.lax.top_k(logits, top_k)
            keep = jax.nn.one_hot(top_idx, E, dtype=logits.dtype).sum(-2) > 0
            sparse_logits = jnp.where(keep, logits, NEG_INF)
            gating = jax.nn.softmax(sparse_logits, axis=-1)
            xf = x.reshape(-1, D)
            gf = gating.reshape(-1, E)
            h = jax.nn.relu(jnp.einsum('td,edh->eth', xf, w1) + b1[:, None, :])
            y = jnp.einsum('eth,ehd->etd', h, w2) + b2[:, None, :]
            out = jnp.einsum('etd,te->td', y, gf)
            return out.reshape(B, S, D)
        key = jax.random.key(seed)
        ks = jax.random.split(key, 5)
        B, S, D, E, H = (2, 512, 256, 8, 1024)
        scale = 0.02
        return {'x': jax.random.normal(ks[0], (B, S, D), dtype=jnp.float32), 'router_w': jax.random.normal(ks[1], (D, E), dtype=jnp.float32) * scale, 'router_b': jnp.zeros((E,), dtype=jnp.float32), 'w1': jax.random.normal(ks[2], (E, D, H), dtype=jnp.float32) * scale, 'b1': jnp.zeros((E, H), dtype=jnp.float32), 'w2': jax.random.normal(ks[3], (E, H, D), dtype=jnp.float32) * scale, 'b2': jnp.zeros((E, D), dtype=jnp.float32)}
    _L0_ffn_in = _L0_ffn_setup()
    _d = {'L0_attn_x': _L0_attn_in['x'], 'L0_attn_Wq': _L0_attn_in['Wq'], 'L0_attn_bq': _L0_attn_in['bq'], 'L0_attn_Wkv': _L0_attn_in['Wkv'], 'L0_attn_bkv': _L0_attn_in['bkv'], 'L0_attn_Wo': _L0_attn_in['Wo'], 'L0_ffn_router_w': _L0_ffn_in['router_w'], 'L0_ffn_router_b': _L0_ffn_in['router_b'], 'L0_ffn_w1': _L0_ffn_in['w1'], 'L0_ffn_b1': _L0_ffn_in['b1'], 'L0_ffn_w2': _L0_ffn_in['w2'], 'L0_ffn_b2': _L0_ffn_in['b2']}
    _x0 = _d['L0_attn_x']
    _d['L0_attn_x'] = jax.random.normal(jax.random.fold_in(jax.random.key(seed), 1), (4, 1024, 256), dtype=_x0.dtype)
    del _x0
    return _d

def reference(L0_attn_x, L0_attn_Wq, L0_attn_bq, L0_attn_Wkv, L0_attn_bkv, L0_attn_Wo, L0_ffn_router_w, L0_ffn_router_b, L0_ffn_w1, L0_ffn_b1, L0_ffn_w2, L0_ffn_b2):

    def _L0_attn_ref(x, Wq, bq, Wkv, bkv, Wo):
        import jax, jax.numpy as jnp
        import numpy as np
        import math
        NUM_HEADS = 8
        EMB = 256
        HEAD_DIM = 128
        B, T = (1, 1024)

        def sinusoidal_pe(T, d, dtype=jnp.float32):
            pos = jnp.arange(T, dtype=dtype)[:, None]
            inv_freq = jnp.exp(-math.log(10000.0) * jnp.arange(0, d, 2, dtype=dtype) / d)
            ang = pos * inv_freq[None, :]
            pe = jnp.zeros((T, d), dtype=dtype)
            pe = pe.at[:, 0::2].set(jnp.sin(ang))
            pe = pe.at[:, 1::2].set(jnp.cos(ang))
            return pe
        Bsz, Tlen, E = x.shape
        q = (x @ Wq + bq).reshape(Bsz, Tlen, NUM_HEADS, HEAD_DIM)
        kv = x @ Wkv + bkv
        k, v = (kv[..., :HEAD_DIM], kv[..., HEAD_DIM:])
        q = jnp.transpose(q, (0, 2, 1, 3))
        pe = sinusoidal_pe(Tlen, HEAD_DIM, x.dtype)
        q = q + pe[None, None, :, :]
        k = k + pe[None, :, :]
        scale = 1.0 / math.sqrt(HEAD_DIM)
        scores = jnp.einsum('bhqd,bkd->bhqk', q, k) * scale
        causal = jnp.tril(jnp.ones((Tlen, Tlen), dtype=bool))
        scores = jnp.where(causal[None, None, :, :], scores, jnp.finfo(scores.dtype).min)
        probs = jax.nn.softmax(scores, axis=-1)
        attn = jnp.einsum('bhqk,bkd->bhqd', probs, v)
        out = jnp.transpose(attn, (0, 2, 1, 3)).reshape(Bsz, Tlen, NUM_HEADS * HEAD_DIM)
        return out @ Wo

    def _L0_ffn_ref(x, router_w, router_b, w1, b1, w2, b2):
        import jax, jax.numpy as jnp
        import numpy as np
        NEG_INF = -1e+30

        def _moe_forward(x, router_w, router_b, w1, b1, w2, b2, top_k=2):
            B, S, D = x.shape
            E = router_w.shape[1]
            logits = jnp.einsum('bsd,de->bse', x, router_w) + router_b
            top_vals, top_idx = jax.lax.top_k(logits, top_k)
            keep = jax.nn.one_hot(top_idx, E, dtype=logits.dtype).sum(-2) > 0
            sparse_logits = jnp.where(keep, logits, NEG_INF)
            gating = jax.nn.softmax(sparse_logits, axis=-1)
            xf = x.reshape(-1, D)
            gf = gating.reshape(-1, E)
            h = jax.nn.relu(jnp.einsum('td,edh->eth', xf, w1) + b1[:, None, :])
            y = jnp.einsum('eth,ehd->etd', h, w2) + b2[:, None, :]
            out = jnp.einsum('etd,te->td', y, gf)
            return out.reshape(B, S, D)
        return _moe_forward(x, router_w, router_b, w1, b1, w2, b2, top_k=2)
    x = L0_attn_x
    xn = _layernorm(x, axis=-1)
    s = _L0_attn_ref(xn, L0_attn_Wq, L0_attn_bq, L0_attn_Wkv, L0_attn_bkv, L0_attn_Wo)
    g = _silu(_L0_ffn_ref(xn, L0_ffn_router_w, L0_ffn_router_b, L0_ffn_w1, L0_ffn_b1, L0_ffn_w2, L0_ffn_b2))
    x = x + s * g
    return x

_drawn_inputs = setup_inputs


def setup_inputs(seed=0):
    import zlib

    import numpy as np

    out = dict(_drawn_inputs(seed))
    spreads = {'L0_ffn_router_b': (0.0, 0.8), 'L0_ffn_b1': (0.0, 0.8), 'L0_ffn_b2': (0.0, 0.8)}
    factors = {'L0_attn_Wq': 5.256,
     'L0_attn_bq': 8.0,
     'L0_attn_Wkv': 3.946,
     'L0_attn_bkv': 8.0,
     'L0_attn_Wo': 3.833,
     'L0_ffn_router_w': 4.453,
     'L0_ffn_w1': 5.74,
     'L0_ffn_w2': 4.607}
    for name, (base, spread) in spreads.items():
        noise = np.random.default_rng([zlib.crc32(name.encode()), seed]).standard_normal(out[name].shape)
        drawn = base * np.exp(spread * noise) if base else spread * noise
        out[name] = jnp.asarray(drawn.astype(out[name].dtype))
    for name, factor in factors.items():
        out[name] = (out[name] * factor).astype(out[name].dtype)
    return out
```

```python
from contextlib import ExitStack

import numpy as np
import concourse.bass as bass
from concourse import mybir

F32, F16, BF16, I32, U32 = (mybir.dt.float32, mybir.dt.float16, mybir.dt.bfloat16, mybir.dt.int32,
                            mybir.dt.uint32)
ALU, ACT, AX = mybir.AluOpType, mybir.ActivationFunctionType, mybir.AxisListType
ds = bass.ds

P = 128
WS = 64.0
EPS = 1e-5
MASKED = -3.0e38
FAR = -3.0e38
HEADS, HD = 8, 128
BLK = 256
PASSES = ((0, 0), (0, 1), (1, 0))
C_ID, C_MASK, C_UP, C_E = 0, P, 2 * P, 3 * P


def constants(tokens, experts, seq):
    most = tokens // BLK
    blocks = 2 * tokens // BLK + experts - 1
    q, k = np.arange(P)[:, None], np.arange(P)[None, :]
    c = np.concatenate([
        (q == k), np.where(k > q, MASKED, 0.0), (q < k),
        np.broadcast_to(np.arange(experts), (P, experts)),
        np.broadcast_to(np.arange(most) * BLK, (P, most)),
        np.broadcast_to(np.arange(blocks), (P, blocks))], axis=1).astype(np.float32)
    pos = np.arange(seq, dtype=np.float32)[:, None]
    inv = np.exp(np.float32(-np.log(10000.0)) * np.arange(0, HD, 2, dtype=np.float32) / np.float32(HD))
    ang = (pos * inv.astype(np.float32)[None, :]).astype(np.float32)
    pe = np.zeros((seq, HD), np.float32)
    pe[:, 0::2], pe[:, 1::2] = np.sin(ang), np.cos(ang)
    return c, np.ascontiguousarray((pe * np.float32(HD ** -0.25)).T.astype(np.float32))


def build(nc, x, wq, bq, wkv, bkv, wo, rw, rb, w1, b1, w2, b2, cst, pe, out):
    NB_, T, D = x.shape
    N = NB_ * T
    NT = N // P
    E, _, H = w1.shape
    DC, HT = D // P, H // P
    QT = T // P
    MOST = N // BLK
    NBLK = 2 * N // BLK + E - 1
    C_TH, C_BL, CW = C_E + E, C_E + E + MOST, C_E + E + MOST + NBLK
    SC = float(HD) ** -0.25
    ROW = D + 2
    SLOTS = NBLK * BLK
    assert D == 256 and HD == P and T == 1024 and H == 1024 and E == 8 and NBLK % 3 == 0

    xf = x.rearrange("b t d -> (b t) d").rearrange("(n p) d -> p n d", p=P)
    of = out.rearrange("b t d -> (b t) d").rearrange("(n p) d -> p n d", p=P)
    xp_d = nc.dram_tensor("xn_split", (N, 2 * D), F16, kind="Internal").ap()
    s_d = nc.dram_tensor("attention", (N, D), F32, kind="Internal").ap()
    rows_d = nc.dram_tensor("expert_rows", (SLOTS, ROW), I32, kind="Internal").ap()
    acc_d = nc.dram_tensor("mixture", (N + BLK, D), F32, kind="Internal").ap()
    xp_v = xp_d.rearrange("(n p) d -> p n d", p=P)
    s_v = s_d.rearrange("(n p) d -> p n d", p=P)
    acc_v = acc_d.rearrange("(n p) d -> p n d", p=P)
    rows_v = rows_d.rearrange("(k p) c -> p k c", p=P)

    with ExitStack() as keep:
        def tensors(ctx):
            def sb(name, shape, dt):
                return ctx.enter_context(nc.sbuf_tensor(name, shape, dt))

            def pb(name, shape, dt):
                return ctx.enter_context(nc.psum_tensor(name, shape, dt))

            def sem(name):
                return ctx.enter_context(nc.semaphore(name))
            return sb, pb, sem

        sb, _, _ = tensors(keep)
        pos = sb("pos", [P, 2, NT], U32)
        gate = sb("gate", [P, 2, NT], F32)
        tok = sb("tok", [P, NT], I32)
        blk_e = sb("blk_e", [P, NBLK], I32)
        bias = sb("bias", [P, E * HT + HEADS + 2], F32)
        B_Q, B_K = E * HT, E * HT + HEADS
        id16 = sb("id16", [P, P], F16)
        w1_p = sb("w1_p", [P, 2 * E * DC * H], F16)

        with ExitStack() as attn_mem:
            sba, _, _ = tensors(attn_mem)
            id32 = sba("id32", [P, P], F32)
            idb = sba("idb", [P, P], BF16)
            maskb = sba("maskb", [P, P], BF16)
            pe_sb = sba("pe_sb", [P, T], F32)
            bv = sba("bv", [P, HD], F32)
            wq_p = sba("wq_p", [P, 2 * DC * HEADS * HD], F16)
            wkv_p = sba("wkv_p", [P, 2, DC, 2 * HD], F16)
            wo_p = sba("wo_p", [P, 2, HEADS, D], F16)
            xT = sba("xT", [P, 2 * DC * N], F16)
            xT4 = xT[:, :].rearrange("p (c t) -> p c t", c=2 * DC)

            with ExitStack() as ctx:
                sb, pb, sem = tensors(ctx)
                x_sb = w1_p[:, 0:2 * NT * D].bitcast(F32).rearrange("p (n d) -> p n d", d=D)
                xp = w1_p[:, 2 * NT * D:4 * NT * D].rearrange("p (n h d) -> p n h d", h=2, d=D)
                c_sb = sb("c_sb", [P, CW], F32)
                up16 = sb("up16", [P, P], F16)
                one16 = sb("one16", [P, P], F16)
                zrow = sb("zrow", [P, 2, ROW], I32)
                zero = sb("zero", [P, D], F32)
                brow = sb("brow", [E * HT + HEADS + 2, P], F32)
                rbb = sb("rbb", [P, E], F32)
                eps = sb("eps", [P, 1], F32)
                wst = sb("wst", [P, 2048], F32)
                wst2 = sb("wst2", [P, 2048], F32)
                kvst = sb("kvst", [P, DC, 2 * HD], F32)
                rw_s = sb("rw_s", [P, DC, E], F32)
                rw_p = sb("rw_p", [P, 2, DC, E], F16)
                st = sb("st", [P, NT, 6], F32)
                mv = sb("mv", [P, NT, 2], F32)
                rs = sb("rs", [P, 4, NT], F32)
                L = sb("L", [P, NT, E], F32)
                L2 = sb("L2", [P, NT, E], F32)
                cand = sb("cand", [P, NT, E], F32)
                oh = [sb(f"oh{i}", [P, NT, E], F32) for i in range(2)]
                M16 = sb("M16", [P, NT * E], F16)
                m_ = [sb(f"m{i}", [P, NT], F32) for i in range(2)]
                ix = [sb(f"ix{i}", [P, NT], F32) for i in range(2)]
                ex = sb("ex", [P, 3, NT], F32)
                sc = [sb(f"scan{i}", [P, NT, E], F32) for i in range(2)]
                tot = sb("tot", [P, NT, E], F32)
                se = [sb(f"scane{i}", [P, E], F32) for i in range(2)]
                nbl = sb("nbl", [P, E], F32)
                cmpb = sb("cmpb", [P, max(NBLK, MOST) * E], F32)
                bf = sb("bf", [P, NBLK], F32)
                psT = [pb(f"psT{i}", [P, 4, 2 * P], F16) for i in range(2)]
                psL = pb("psL", [P, NT * E], F32)
                psR = pb("psR", [P, 2, NT * E], F32)
                psB = pb("psB", [P, P], F32)
                s_x = [sem(f"s_x{i}") for i in range(4)]
                s_c, s_w, s_cc, s_bn, s_ag = map(sem, ("s_c", "s_w", "s_cc", "s_bn", "s_ag"))
                s_sd, s_r, s_xn, s_xh, s_xl = map(sem, ("s_sd", "s_r", "s_xn", "s_xh", "s_xl"))
                s_z, s_st, s_tr, s_te, s_wh, s_wl = map(sem, ("s_z", "s_st", "s_tr", "s_te", "s_wh", "s_wl"))
                s_b, s_lg, s_ch, s_m, s_rk, s_e = map(sem, ("s_b", "s_lg", "s_ch", "s_m", "s_rk", "s_e"))
                s_dr = sem("s_dr")
                block = ctx.enter_context(nc.Block())
                G4 = NT // 4

                @block.sync
                def _(eng):
                    for c in range(4):
                        eng.dma_start(x_sb[:, c * G4:(c + 1) * G4, :], xf[:, c * G4:(c + 1) * G4, :]).then_inc(s_x[c], 16)
                    eng.wait_ge(s_z, 4)
                    for t in range(2):
                        eng.dma_start(rows_d.rearrange("(k t p) c -> t p k c", t=2, p=P)[t],
                                      zrow[:, t, :].unsqueeze(1).to_broadcast([P, NBLK, ROW])).then_inc(s_dr, 16)
                    eng.dma_start(acc_v, zero[:, :].unsqueeze(1).to_broadcast([P, NT + BLK // P, D])).then_inc(s_dr, 16)
                    eng.wait_ge(s_xl, NT)
                    eng.dma_start(xp_v, xp[:, :, :, :].rearrange("p n h d -> p n (h d)")).then_inc(s_dr, 16)
                    eng.wait_ge(s_dr, 64)

                @block.gpsimd
                def _(eng):
                    eng.memset(eps[:, :], EPS).then_inc(s_z, 1)
                    eng.memset(zero[:, :], 0.0).then_inc(s_z, 1)
                    eng.memset(one16[:, :], 1.0).then_inc(s_st, 1)
                    eng.memset(zrow[:, :, :], 0).then_inc(s_st, 1)
                    eng.iota(tok[:, :], [[P, NT]], base=0, channel_multiplier=1).then_inc(s_st, 1)
                    eng.wait_ge(s_st, 3)
                    for t in range(2):
                        eng.iota(zrow[:, t, D:D + 1], [[1, 1]], base=N + t * P, channel_multiplier=1).then_inc(s_z, 1)

                @block.scalar
                def _(eng):
                    for dst, src in ((c_sb[:, :], cst), (rw_s[:, :, :], rw.rearrange("(c p) e -> p c e", p=P)),
                                     (rbb[:, :], rb.partition_broadcast(P)),
                                     (brow[0:E * HT, :], b1.rearrange("e (h p) -> (e h) p", p=P)),
                                     (brow[E * HT:E * HT + HEADS, :], bq.rearrange("(h p) -> h p", p=P)),
                                     (brow[E * HT + HEADS:, :], bkv.rearrange("(h p) -> h p", p=P))):
                        eng.dma_start(dst, src).then_inc(s_c, 16)
                    for dst, src in ((wst[:, :].rearrange("p (c n) -> p c n", c=DC), wq.rearrange("(c p) n -> p c n", p=P)),
                                     (kvst[:, :, :], wkv.rearrange("(c p) n -> p c n", p=P)),
                                     (wst2[:, :].rearrange("p (h n) -> p h n", h=HEADS), wo.rearrange("(h p) n -> p h n", p=P)),
                                     (bv[:, :], bkv[HD:2 * HD].partition_broadcast(P)),
                                     (pe_sb[:, :], pe)):
                        eng.dma_start(dst, src).then_inc(s_w, 16)
                    eng.wait_ge(s_c, 96)
                    for dst, src in ((id32, C_ID), (id16, C_ID), (idb, C_ID), (maskb, C_MASK), (up16, C_UP)):
                        eng.activation(dst[:, :], c_sb[:, src:src + P], ACT.Copy).then_inc(s_cc, 1)
                    eng.activation(rw_p[:, 0], rw_s[:, :, :], ACT.Copy, scale=WS).then_inc(s_wh, 1)
                    eng.wait_ge(s_w, 80)
                    eng.activation(wq_p[:, 0:2048], wst[:, :], ACT.Copy, scale=WS).then_inc(s_wh, 1)
                    eng.activation(wkv_p[:, 0], kvst[:, :, :], ACT.Copy, scale=WS).then_inc(s_wh, 1)
                    eng.activation(wo_p[:, 0], wst2[:, :].rearrange("p (h n) -> p h n", h=HEADS), ACT.Copy,
                                   scale=WS).then_inc(s_wh, 1)
                    eng.wait_ge(s_ag, 1)
                    eng.wait_ge(s_z, 1)
                    eng.activation(rs[:, 0, :], mv[:, :, 1], ACT.Sqrt, bias=eps[:, :]).then_inc(s_sd, 1)
                    with eng.Fori(0, NT) as n:
                        eng.wait_ge(s_xn, n + 1)
                        eng.activation(xp[:, ds(n, 1), 0, :], x_sb[:, ds(n, 1), :], ACT.Copy).then_inc(s_xh, 1)
                    eng.wait_ge(s_b, 1)
                    eng.activation(bias[:, 0:E * HT], psB[:, 0:E * HT], ACT.Copy).then_inc(s_cc, 1)
                    eng.activation(bias[:, E * HT:], psB[:, E * HT:E * HT + HEADS + 2], ACT.Copy, scale=SC).then_inc(s_cc, 1)
                    with eng.Fori(0, NT // 4) as i:
                        for q in range(2):
                            eng.wait_ge(s_tr, i * 2 + (q + 1))
                            eng.activation(xT4[:, :, ds(i * 4 * P + q * 2 * P, 2 * P)], psT[q][:, :, :], ACT.Copy).then_inc(s_te, 1)
                    eng.wait_ge(s_m, 1)
                    eng.activation(ex[:, 0, :], ex[:, 2, :], ACT.Exp).then_inc(s_e, 1)

                @block.tensor
                def _(eng):
                    eng.wait_ge(s_cc, 5)
                    eng.transpose(psB[:, 0:E * HT + HEADS + 2], brow[:, :], id32[0:E * HT + HEADS + 2, 0:E * HT + HEADS + 2]).then_inc(s_b, 1)
                    with eng.Fori(0, NT // 4) as i:
                        for q in range(2):
                            eng.wait_ge(s_xl, i * 4 + (2 * q + 2))
                            if q == 0:
                                eng.wait_ge(s_te, i * 2)
                            for t in range(2):
                                for h in range(2):
                                    for c in range(DC):
                                        mm = eng.transpose(psT[q][:, 2 * h + c, t * P:(t + 1) * P],
                                                           xp[:, ds(i * 4 + 2 * q + t, 1), h, c * P:(c + 1) * P].squeeze(1),
                                                           id16[:, :])
                            mm.then_inc(s_tr, 1)
                    eng.wait_ge(s_te, NT // 2)
                    eng.wait_ge(s_wl, 1)
                    with eng.Fori(0, NT) as n:
                        first = True
                        for a, b in PASSES:
                            for c in range(DC):
                                mm = eng.matmul(psL[:, ds(n * E, E)], xT[:, ds(n * P + (2 * a + c) * N, P)],
                                                rw_p[:, b, c, :], start=first, stop=(a == 1 and c == DC - 1))
                                first = False
                        mm.then_inc(s_lg, 1)
                    eng.wait_ge(s_z, 4)
                    eng.wait_ge(s_rk, 1)
                    eng.matmul(psR[:, 0, :], up16[:, :], M16[:, :], start=True, stop=True)
                    eng.matmul(psR[:, 1, :], one16[:, :], M16[:, :], start=True, stop=True).then_inc(s_rk, 1)

                @block.vector
                def _(eng):
                    n_ch = [0]

                    def link(ins):
                        n_ch[0] += 1
                        ins.then_inc(s_ch, 1)
                        eng.wait_ge(s_ch, n_ch[0])

                    for c in range(4):
                        eng.wait_ge(s_x[c], 16)
                        with eng.Fori(c * G4, (c + 1) * G4) as n:
                            eng.bn_stats(st[:, ds(n, 1), :].squeeze(1), x_sb[:, ds(n, 1), :].squeeze(1)).then_inc(s_bn, 1)
                    eng.wait_ge(s_bn, NT)
                    link(eng.tensor_tensor(mv[:, :, 0], st[:, :, 1], st[:, :, 4], ALU.add))
                    link(eng.tensor_tensor(rs[:, 1, :], st[:, :, 1], st[:, :, 4], ALU.subtract))
                    link(eng.tensor_scalar(mv[:, :, 0], mv[:, :, 0], 0.5, None, ALU.mult))
                    link(eng.tensor_tensor(rs[:, 1, :], rs[:, 1, :], rs[:, 1, :], ALU.mult))
                    link(eng.tensor_tensor(rs[:, 2, :], st[:, :, 2], st[:, :, 5], ALU.add))
                    link(eng.tensor_scalar(rs[:, 1, :], rs[:, 1, :], 0.25, None, ALU.mult))
                    link(eng.scalar_tensor_tensor(mv[:, :, 1], rs[:, 2, :], 1.0 / D, rs[:, 1, :], ALU.mult, ALU.add))
                    eng.sem_inc(s_ag, 1)
                    eng.wait_ge(s_wh, 4)
                    for dst, src, hi in ((rw_p[:, 1], rw_s[:, :, :], rw_p[:, 0]), (wq_p[:, 2048:], wst[:, :], wq_p[:, 0:2048]),
                                         (wkv_p[:, 1], kvst[:, :, :], wkv_p[:, 0]),
                                         (wo_p[:, 1], wst2[:, :].rearrange("p (h n) -> p h n", h=HEADS), wo_p[:, 0])):
                        eng.scalar_tensor_tensor(dst, src, WS, hi, ALU.mult, ALU.subtract).then_inc(s_wl, 1)
                    eng.wait_ge(s_sd, 1)
                    link(eng.tensor_scalar(rs[:, 1, :], mv[:, :, 1], EPS, None, ALU.add))
                    link(eng.reciprocal(rs[:, 2, :], rs[:, 0, :]))
                    link(eng.tensor_tensor(rs[:, 3, :], rs[:, 2, :], rs[:, 2, :], ALU.mult))
                    link(eng.tensor_tensor(rs[:, 3, :], rs[:, 3, :], rs[:, 1, :], ALU.mult))
                    link(eng.tensor_scalar(rs[:, 3, :], rs[:, 3, :], -0.5, 1.5, ALU.mult, ALU.add))
                    link(eng.tensor_tensor(rs[:, 0, :], rs[:, 2, :], rs[:, 3, :], ALU.mult))
                    with eng.Fori(0, NT) as n:
                        eng.tensor_scalar(x_sb[:, ds(n, 1), :].squeeze(1), x_sb[:, ds(n, 1), :].squeeze(1), mv[:, ds(n, 1), 0],
                                          rs[:, 0, ds(n, 1)], ALU.subtract, ALU.mult).then_inc(s_xn, 1)
                    with eng.Fori(0, NT) as n:
                        eng.wait_ge(s_xh, n + 1)
                        eng.tensor_tensor(xp[:, ds(n, 1), 1, :], x_sb[:, ds(n, 1), :], xp[:, ds(n, 1), 0, :],
                                          ALU.subtract).then_inc(s_xl, 1)
                    ids = c_sb[:, C_E:C_E + E].unsqueeze(1).to_broadcast([P, NT, E])
                    eng.wait_ge(s_c, 96)
                    eng.wait_ge(s_lg, NT)

                    def wide(a):
                        return a.unsqueeze(2).to_broadcast([P, NT, E])

                    link(eng.scalar_tensor_tensor(L[:, :, :], psL[:, :].rearrange("p (n e) -> p n e", e=E), 1.0 / WS,
                                                  rbb[:, :].unsqueeze(1).to_broadcast([P, NT, E]), ALU.mult, ALU.add))
                    src = L
                    for i in range(2):
                        link(eng.tensor_reduce(m_[i][:, :], src[:, :, :], AX.X, ALU.max))
                        link(eng.tensor_tensor(cand[:, :, :], src[:, :, :], wide(m_[i][:, :]), ALU.is_lt))
                        link(eng.scalar_tensor_tensor(cand[:, :, :], cand[:, :, :], float(E), ids, ALU.mult, ALU.add))
                        link(eng.tensor_reduce(ix[i][:, :], cand[:, :, :], AX.X, ALU.min))
                        link(eng.tensor_tensor(oh[i][:, :, :], ids, wide(ix[i][:, :]), ALU.is_equal))
                        if i == 0:
                            link(eng.scalar_tensor_tensor(L2[:, :, :], oh[0][:, :, :], FAR, L[:, :, :], ALU.mult, ALU.add))
                            src = L2
                    link(eng.tensor_tensor(ex[:, 2, :], m_[1][:, :], m_[0][:, :], ALU.subtract))
                    eng.sem_inc(s_m, 1)
                    eng.tensor_tensor(M16[:, :].rearrange("p (n e) -> p n e", e=E), oh[0][:, :, :], oh[1][:, :, :],
                                      ALU.add).then_inc(s_rk, 1)
                    eng.wait_ge(s_e, 1)
                    link(eng.tensor_scalar(ex[:, 1, :], ex[:, 0, :], 1.0, None, ALU.add))
                    link(eng.reciprocal(gate[:, 0, :], ex[:, 1, :]))
                    link(eng.tensor_tensor(gate[:, 1, :], ex[:, 0, :], gate[:, 0, :], ALU.mult))
                    eng.wait_ge(s_rk, 2)
                    link(eng.tensor_copy(tot[:, :, :], psR[:, 1, :].rearrange("p (n e) -> p n e", e=E)))
                    link(eng.tensor_copy(sc[0][:, :, :], tot[:, :, :]))
                    cur, step = 0, 1
                    while step < NT:
                        a, b = sc[cur], sc[1 - cur]
                        eng.tensor_copy(b[:, 0:step, :], a[:, 0:step, :]).then_inc(s_ch, 1)
                        n_ch[0] += 1
                        link(eng.tensor_tensor(b[:, step:, :], a[:, step:, :], a[:, 0:NT - step, :], ALU.add))
                        cur, step = 1 - cur, 2 * step
                    cnt = sc[cur][:, NT - 1, :]
                    cm = cmpb[:, 0:MOST * E].rearrange("p (e k) -> p e k", e=E)
                    link(eng.tensor_tensor(cm, c_sb[:, C_TH:C_TH + MOST].unsqueeze(1).to_broadcast([P, E, MOST]),
                                           cnt.unsqueeze(2).to_broadcast([P, E, MOST]), ALU.is_lt))
                    link(eng.tensor_reduce(nbl[:, :], cm, AX.X, ALU.add))
                    link(eng.tensor_copy(se[0][:, :], nbl[:, :]))
                    ce, step = 0, 1
                    while step < E:
                        a, b = se[ce], se[1 - ce]
                        eng.tensor_copy(b[:, 0:step], a[:, 0:step]).then_inc(s_ch, 1)
                        n_ch[0] += 1
                        link(eng.tensor_tensor(b[:, step:], a[:, step:], a[:, 0:E - step], ALU.add))
                        ce, step = 1 - ce, 2 * step
                    ends = se[ce]
                    first = se[1 - ce]
                    link(eng.tensor_tensor(first[:, :], ends[:, :], nbl[:, :], ALU.subtract))
                    link(eng.tensor_tensor(sc[1 - cur][:, :, :], sc[cur][:, :, :], tot[:, :, :], ALU.subtract))
                    link(eng.tensor_tensor(sc[1 - cur][:, :, :], sc[1 - cur][:, :, :],
                                           psR[:, 0, :].rearrange("p (n e) -> p n e", e=E), ALU.add))
                    link(eng.scalar_tensor_tensor(sc[1 - cur][:, :, :], first[:, :].unsqueeze(1).to_broadcast([P, NT, E]), float(BLK),
                                                  sc[1 - cur][:, :, :], ALU.mult, ALU.add))
                    for i in range(2):
                        link(eng.tensor_tensor(cand[:, :, :], oh[i][:, :, :], sc[1 - cur][:, :, :], ALU.mult))
                        link(eng.tensor_reduce(ix[i][:, :], cand[:, :, :], AX.X, ALU.add))
                        link(eng.tensor_copy(pos[:, i, :], ix[i][:, :]))
                    cb = cmpb[:, 0:NBLK * E].rearrange("p (k e) -> p k e", e=E)
                    link(eng.tensor_tensor(cb, c_sb[:, C_BL:C_BL + NBLK].unsqueeze(2).to_broadcast([P, NBLK, E]),
                                           ends[:, :].unsqueeze(1).to_broadcast([P, NBLK, E]), ALU.is_ge))
                    link(eng.tensor_reduce(bf[:, :], cb, AX.X, ALU.add))
                    link(eng.tensor_scalar(blk_e[:, :], bf[:, :], float(E - 1), None, ALU.min))

            attention(nc, locals())
        experts(nc, locals())


def attention(nc, v):
    NB_, T, QT, N, D, DC, E, H = (v[k] for k in ("NB_", "T", "QT", "N", "D", "DC", "E", "H"))
    NT, SC, ROW, B_Q, B_K = (v[k] for k in ("NT", "SC", "ROW", "B_Q", "B_K"))
    pos, gate, tok, bias, id32, idb, maskb, pe_sb, bv = (v[k] for k in (
        "pos", "gate", "tok", "bias", "id32", "idb", "maskb", "pe_sb", "bv"))
    wq_p, wkv_p, wo_p, xT, w1_p = (v[k] for k in ("wq_p", "wkv_p", "wo_p", "xT", "w1_p"))
    xp_v, s_v, rows_d, w1 = v["xp_v"], v["s_v"], v["rows_d"], v["w1"]
    PRIME = 16
    CUM = [1, 2, 3, 4, 6, 8, 10, 12]
    CH = CUM[-1]
    WC = E * DC * H // NT
    with ExitStack() as ctx:
        sb, pb, sem = v["tensors"](ctx)
        qp = sb("qp", [P, 2 * HEADS * T], F16)
        kp = sb("kp", [P, 2, T], F16)
        vp = sb("vp", [P, 2, QT, HD], F16)
        prb = sb("prb", [P, 4, T], F32)
        pr = [prb[:, i, :] for i in range(4)]
        tmp = prb[:, 0:2, :].rearrange("p a (b n) -> p (a b) n", b=2)
        pT = [sb(f"pT{g}", [P, 2, 4 * (g + 1), 512], F16) for g in range(2)]
        nmax = sb("nmax", [P, 4], F32)
        rsum = sb("rsum", [P, 4], F32)
        rrec = sb("rrec", [P, 4], F32)
        wst = [sb(f"w1st{i}", [P, WC], F32) for i in range(2)]
        rowb = [sb(f"rowb{i}", [P, ROW], I32) for i in range(2)]
        idx = [sb(f"idx{i}", [P, 1], U32) for i in range(2)]
        psS = [pb(f"psS{i}", [P, 2, 512], F32) for i in range(2)]
        psP = [pb(f"psP{i}", [P, 4, P], F32) for i in range(2)]
        psO = [pb(f"psO{i}", [P, 512], F32) for i in range(2)]
        bank = [psS[0][:, 0, :], psS[0][:, 1, :], psS[1][:, 0, :], psS[1][:, 1, :]]
        names = ("a_sc", "a_max", "a_exp", "a_rec", "a_nrm", "a_tr", "a_hi", "a_lo", "a_pv", "a_ah", "a_al",
                 "j_mm", "j_t", "j_hi", "j_lo", "o_mm", "o_cp", "a_pr", "a_waited")
        (sc_, mx_, ex_, rc_, nm_, tr_, hi_, lo_, pv_, ah_, al_, jm_, jt_, jh_, jl_, om_, oc_, primed, waited) = map(sem, names)
        od_ = sem("o_dma")
        w_l = [sem(f"w_ld{i}") for i in range(2)]
        w_u, w_c = sem("w_used"), sem("w_chain")
        r_l = [sem(f"r_ld{i}") for i in range(2)]
        r_c, r_s, r_u = sem("r_copy"), sem("r_scatter"), sem("r_used")
        JOBS = 4 + 2 * HEADS
        block = ctx.enter_context(nc.Block())
        qoff = HEADS * T

        def nblk(i):
            return i + 1

        def prime(eng, sems):
            for s in sems:
                eng.sem_inc(s, PRIME)
            eng.sem_inc(primed, 1)

        @block.tensor
        def _(eng):
            prime(eng, (sc_, tr_, pv_))
            eng.wait_ge(primed, 4)

            def proj(out, lhs, rhs):
                k = 0
                for a, b in PASSES:
                    for c in range(DC):
                        mm = eng.matmul(out, lhs(a, c), rhs(b, c), start=(k == 0), stop=(k == 3 * DC - 1))
                        k += 1
                return mm

            with eng.Fori(0, NB_) as b:
                eng.wait_ge(oc_, b * 4)
                for j in range(2):
                    proj(bank[j], lambda a, c: wkv_p[:, a, c, 0:HD],
                         lambda a, c: xT[:, ds(b * T + ((2 * a + c) * N + j * 512), 512)]).then_inc(jm_, 1)
                for j in range(2):
                    for t in range(4):
                        mm = proj(bank[2 + j][:, t * P:(t + 1) * P],
                                  lambda a, c: xT[:, ds(b * T + ((2 * a + c) * N + (4 * j + t) * P), P)],
                                  lambda a, c: wkv_p[:, a, c, HD:2 * HD])
                    mm.then_inc(jm_, 1)
                with eng.Fori(0, HEADS // 2) as hh:
                    for j in range(4):
                        eng.wait_ge(jt_, b * JOBS + hh * 4 + (j + 1))
                        proj(bank[j], lambda a, c: wq_p[:, ds(hh * 2 * HD + ((2 * a + c) * HEADS * HD + (j // 2) * HD), HD)],
                             lambda a, c: xT[:, ds(b * T + ((2 * a + c) * N + (j % 2) * 512), 512)]).then_inc(jm_, 1)

                def scores(h, i):
                    eng.wait_ge(ex_, b * 64 + h * 8 + (i - 1 + PRIME))
                    n = nblk(i) * P
                    for lo in range(0, n, 512):
                        w = min(512, n - lo)
                        last = lo + w == n
                        o = psS[i % 2][:, lo // 512, 0:w]
                        for k, (a, c) in enumerate(PASSES):
                            mm = eng.matmul(o, qp[:, ds(h * T + (a * qoff + i * P), P)], kp[:, c, lo:lo + w],
                                            start=(k == 0), stop=(k == 2 and not last))
                        if last:
                            mm = eng.matmul(o[:, w - P:w], idb[:, :], maskb[:, :], start=False, stop=True)
                    mm.then_inc(sc_, 1)

                def turn(h, i):
                    eng.wait_ge(nm_, b * 64 + h * 8 + (i + 1 + PRIME))
                    for k in range(CUM[i] - CUM[i - 1] if i else 1):
                        c = (CUM[i - 1] if i else 0) + k
                        eng.wait_ge(lo_, b * 8 * CH + h * CH + (c - 1 + PRIME))
                        for t in range(min(4, nblk(i) - 4 * k)):
                            mm = eng.transpose(psP[c % 2][:, t, :], pr[i % 4][:, (4 * k + t) * P:(4 * k + t + 1) * P], id32[:, :])
                        mm.then_inc(tr_, 1)

                def values(h, g):
                    eng.wait_ge(lo_, b * 8 * CH + h * CH + (CUM[4 * g + 3] + PRIME))
                    eng.wait_ge(al_, b * 16 + h * 2 + (g - 1 + PRIME))
                    last = 4 * g + 3
                    for j in range(last + 1):
                        q0 = max(0, j - 4 * g) * P
                        for k, (a, c) in enumerate(PASSES):
                            mm = eng.matmul(psO[g][:, q0:512], vp[:, a, j, :], pT[g][:, c, j, q0:512],
                                            start=(j == 0 and k == 0), stop=(j == last and k == 2))
                    mm.then_inc(pv_, 1)

                def head(h, first, last):
                    for i in range(8):
                        if i < 6:
                            scores(h, i + 2)
                        elif not last:
                            scores(h + 1, i - 6)
                        if i:
                            turn(h, i - 1)
                        elif not first:
                            turn(h - 1, 7)
                        if i == 5:
                            values(h, 0)
                        if i == 1 and not first:
                            values(h - 1, 1)

                eng.wait_ge(jl_, b * JOBS + JOBS)
                scores(0, 0)
                scores(0, 1)
                head(0, True, False)
                with eng.Fori(1, HEADS - 1) as h:
                    head(h, False, False)
                head(HEADS - 1, False, True)
                turn(HEADS - 1, 7)
                values(HEADS - 1, 1)
                eng.wait_ge(al_, b * 16 + (16 + PRIME))
                for i in range(QT):
                    o = bank[i // 2][:, (i % 2) * D:(i % 2 + 1) * D]
                    for h in range(HEADS):
                        for k, (a, c) in enumerate(PASSES):
                            mm = eng.matmul(o, qp[:, a * qoff + h * T + i * P:a * qoff + h * T + (i + 1) * P], wo_p[:, c, h, :],
                                            start=(h == 0 and k == 0), stop=(h == HEADS - 1 and k == 2))
                    if i % 2:
                        mm.then_inc(om_, 1)

        @block.scalar
        def _(eng):
            prime(eng, (ex_, hi_, ah_))
            eng.wait_ge(primed, 4)
            with eng.Fori(0, NB_) as b:
                def job(kind, j, jj, h):
                    eng.wait_ge(jt_, b * JOBS + jj)
                    if kind == "v":
                        eng.activation(vp[:, 0, 4 * (j % 2):4 * (j % 2) + 4, :],
                                       tmp[:, j, :].rearrange("p (t n) -> p t n", n=P), ACT.Copy).then_inc(jh_, 1)
                    elif kind == "k":
                        eng.activation(kp[:, 0, j * 512:(j + 1) * 512], tmp[:, j, :], ACT.Identity,
                                       bias=bias[:, B_K:B_K + 1]).then_inc(jh_, 1)
                    else:
                        eng.activation(qp[:, ds(h * T + (j % 2) * 512, 512)], tmp[:, j, :], ACT.Identity,
                                       bias=bias[:, ds(h + B_Q, 1)]).then_inc(jh_, 1)

                for j in range(4):
                    job("kkvv"[j], j, j + 1, None)
                with eng.Fori(0, HEADS // 2) as hh:
                    for j in range(4):
                        job("q", j, hh * 4 + (4 + j + 1), hh * 2 + j // 2)

                def expo(h, i):
                    n = nblk(i) * P
                    eng.wait_ge(mx_, b * 64 + h * 8 + (i + 1 + PRIME))
                    eng.wait_ge(tr_, b * 8 * CH + h * CH + ((CUM[i - 4] if i >= 4 else CUM[i + 4] - CH) + PRIME))
                    eng.activation(pr[i % 4][:, 0:n], psS[i % 2][:, :, :].rearrange("p a n -> p (a n)")[:, 0:n], ACT.Exp,
                                   bias=nmax[:, i % 4:i % 4 + 1], accum_out=rsum[:, i % 4:i % 4 + 1]).then_inc(ex_, 1)

                def his(h, i):
                    g, qi = i // 4, i % 4
                    eng.wait_ge(pv_, b * 16 + h * 2 + (g - 1 + PRIME))
                    for k in range(CUM[i] - CUM[i - 1] if i else 1):
                        c = (CUM[i - 1] if i else 0) + k
                        n = min(4, nblk(i) - 4 * k)
                        eng.wait_ge(tr_, b * 8 * CH + h * CH + (c + 1 + PRIME))
                        eng.activation(pT[g][:, 0, 4 * k:4 * k + n, qi * P:(qi + 1) * P], psP[c % 2][:, 0:n, :], ACT.Copy).then_inc(hi_, 1)

                def outs(h, g):
                    eng.wait_ge(pv_, b * 16 + h * 2 + (g + 1 + PRIME))
                    eng.activation(qp[:, ds(h * T + g * 512, 512)], psO[g][:, :], ACT.Copy).then_inc(ah_, 1)

                def head(h, first, last):
                    for i in range(8):
                        if i < 7:
                            expo(h, i + 1)
                        elif not last:
                            expo(h + 1, 0)
                        if i:
                            his(h, i - 1)
                        elif not first:
                            his(h - 1, 7)
                        if i == 6:
                            outs(h, 0)
                        if i == 2 and not first:
                            outs(h - 1, 1)

                expo(0, 0)
                head(0, True, False)
                with eng.Fori(1, HEADS - 1) as h:
                    head(h, False, False)
                head(HEADS - 1, False, True)
                his(HEADS - 1, 7)
                outs(HEADS - 1, 1)
                eng.wait_ge(jl_, b * JOBS + JOBS)
                for j in range(4):
                    eng.wait_ge(om_, b * 4 + (j + 1))
                    eng.activation(tmp[:, j, :], bank[j], ACT.Copy, scale=1.0 / WS).then_inc(oc_, 1)

        @block.vector
        def _(eng):
            prime(eng, (mx_, rc_, lo_, al_))
            eng.wait_ge(primed, 4)
            with eng.Fori(0, NB_) as b:
                def unscale(kind, j, jj, lojj):
                    eng.wait_ge(jm_, b * JOBS + jj)
                    eng.wait_ge(jl_, b * JOBS + lojj)
                    if kind == "v":
                        eng.scalar_tensor_tensor(tmp[:, j, :].rearrange("p (t n) -> p t n", n=P),
                                                 bank[j].rearrange("p (t n) -> p t n", n=P), 1.0 / WS,
                                                 bv[:, :].unsqueeze(1).to_broadcast([P, 4, P]), ALU.mult, ALU.add).then_inc(jt_, 1)
                    else:
                        eng.scalar_tensor_tensor(tmp[:, j, :], bank[j], SC / WS, pe_sb[:, (j % 2) * 512:(j % 2 + 1) * 512],
                                                 ALU.mult, ALU.add).then_inc(jt_, 1)

                def rest(kind, j, jj, h):
                    eng.wait_ge(jh_, b * JOBS + jj)
                    if kind == "v":
                        sl = slice(4 * (j % 2), 4 * (j % 2) + 4)
                        eng.tensor_tensor(vp[:, 1, sl, :], tmp[:, j, :].rearrange("p (t n) -> p t n", n=P), vp[:, 0, sl, :],
                                          ALU.subtract).then_inc(jl_, 1)
                    elif kind == "k":
                        eng.scalar_tensor_tensor(kp[:, 1, j * 512:(j + 1) * 512], tmp[:, j, :], bias[:, B_K:B_K + 1],
                                                 kp[:, 0, j * 512:(j + 1) * 512], ALU.add, ALU.subtract).then_inc(jl_, 1)
                    else:
                        eng.scalar_tensor_tensor(qp[:, ds(h * T + (qoff + (j % 2) * 512), 512)], tmp[:, j, :],
                                                 bias[:, ds(h + B_Q, 1)], qp[:, ds(h * T + (j % 2) * 512, 512)],
                                                 ALU.add, ALU.subtract).then_inc(jl_, 1)

                eng.wait_ge(od_, b * 16)
                for j in range(4):
                    unscale("kkvv"[j], j, j + 1, 0)
                    if j:
                        rest("kkvv"[j - 1], j - 1, j, None)
                rest("v", 3, 4, None)
                with eng.Fori(0, HEADS // 2) as hh:
                    for j in range(4):
                        unscale("q", j, hh * 4 + (4 + j + 1), hh * 4 + (j + 1))
                        if j:
                            rest("q", j - 1, hh * 4 + (4 + j), hh * 2 + (j - 1) // 2)
                    rest("q", 3, hh * 4 + 8, hh * 2 + 1)

                def maxi(h, i):
                    n = nblk(i) * P
                    eng.wait_ge(sc_, b * 64 + h * 8 + (i + 1 + PRIME))
                    eng.tensor_reduce(nmax[:, i % 4:i % 4 + 1], psS[i % 2][:, :, :].rearrange("p a n -> p (a n)")[:, 0:n],
                                      AX.X, ALU.max, negate=True).then_inc(mx_, 1)

                def rec(h, i):
                    eng.wait_ge(ex_, b * 64 + h * 8 + (i + 1 + PRIME))
                    eng.wait_ge(nm_, b * 64 + h * 8 + (i - 3 + PRIME))
                    eng.reciprocal(rrec[:, i % 4:i % 4 + 1], rsum[:, i % 4:i % 4 + 1]).then_inc(rc_, 1)

                def los(h, i):
                    g, qi = i // 4, i % 4
                    for k in range(CUM[i] - CUM[i - 1] if i else 1):
                        c = (CUM[i - 1] if i else 0) + k
                        n = min(4, nblk(i) - 4 * k)
                        eng.wait_ge(hi_, b * 8 * CH + h * CH + (c + 1 + PRIME))
                        o = pT[g][:, :, 4 * k:4 * k + n, qi * P:(qi + 1) * P]
                        eng.tensor_tensor(o[:, 1], psP[c % 2][:, 0:n, :], o[:, 0], ALU.subtract).then_inc(lo_, 1)

                def outs(h, g):
                    eng.wait_ge(ah_, b * 16 + h * 2 + (g + 1 + PRIME))
                    eng.tensor_tensor(qp[:, ds(h * T + (qoff + g * 512), 512)], psO[g][:, :], qp[:, ds(h * T + g * 512, 512)],
                                      ALU.subtract).then_inc(al_, 1)

                def head(h, first, last):
                    for i in range(8):
                        rec(h, i)
                        if i < 6:
                            maxi(h, i + 2)
                        elif not last:
                            maxi(h + 1, i - 6)
                        if i:
                            los(h, i - 1)
                        elif not first:
                            los(h - 1, 7)
                        if i == 6:
                            outs(h, 0)
                        if i == 2 and not first:
                            outs(h - 1, 1)

                maxi(0, 0)
                maxi(0, 1)
                head(0, True, False)
                with eng.Fori(1, HEADS - 1) as h:
                    head(h, False, False)
                head(HEADS - 1, False, True)
                los(HEADS - 1, 7)
                outs(HEADS - 1, 1)

        @block.gpsimd
        def _(eng):
            def wait(sem, value):
                eng.wait_ge(sem, value)
                eng.sem_inc(waited, 1)

            prime(eng, (nm_,))
            wait(primed, 4)
            with eng.Fori(0, NB_) as b:
                with eng.Fori(0, HEADS // 2) as hh:
                    for par in range(2):
                        U = b * 64 + hh * 16 + par * 8
                        n = b * HEADS + hh * 2 + par
                        for i in range(8):
                            w = nblk(i) * P
                            wait(rc_, U + (i + 1 + PRIME))
                            eng.tensor_scalar(pr[i % 4][:, 0:w], pr[i % 4][:, 0:w], rrec[:, i % 4:i % 4 + 1], 1.0,
                                              ALU.mult, ALU.mult).then_inc(nm_, 1)
                            if i == 0:
                                wait(r_s, (b * (HEADS // 2) + hh) * 64 + par * 32)
                                for s in range(2):
                                    eng.tensor_copy(rowb[s][:, D:D + 1], tok[:, ds(n, 1)]).then_inc(r_c, 1)
                                    eng.tensor_copy(rowb[s][:, D + 1:D + 2].bitcast(F32), gate[:, s, ds(n, 1)]).then_inc(r_c, 1)
                                    eng.tensor_copy(idx[s][:, :], pos[:, s, ds(n, 1)]).then_inc(r_c, 1)
                            if i == 2:
                                wait(r_c, n * 6 + 6)
                                for s in range(2):
                                    wait(r_l[s], n * 16 + 16)
                                    eng.indirect_dma_start(rows_d, bass.IndirectOffsetOnAxis(ap=idx[s][:, 0:1], axis=0),
                                                           rowb[s][:, :], None).then_inc(r_s, 16)
                            if i == 4:
                                wait(w_l[par], (b * (HEADS // 2) + hh) * 16 + 16)
                                eng.tensor_scalar(wst[par][:, :], wst[par][:, :], WS, 1.0, ALU.mult, ALU.mult).then_inc(w_c, 1)
                                wait(w_c, n * 2 + 1)
                                eng.tensor_copy(w1_p[:, ds(n * WC, WC)], wst[par][:, :]).then_inc(w_c, 1)
                            if i == 5:
                                wait(w_c, n * 2 + 2)
                                eng.tensor_tensor(w1_p[:, ds(n * WC + E * DC * H, WC)], wst[par][:, :], w1_p[:, ds(n * WC, WC)],
                                                  ALU.subtract).then_inc(w_u, 1)
            wait(r_s, NT * 32)

        @block.sync
        def _(eng):
            w1v = w1.rearrange("e (c p) n -> (e c) p n", p=P)
            assert H == 2 * WC
            with eng.Fori(0, NB_) as b:
                with eng.Fori(0, HEADS // 2) as hh:
                    for par in range(2):
                        n = b * HEADS + hh * 2 + par
                        m = b * (HEADS // 2) + hh
                        eng.wait_ge(w_u, m * 2 + par + (-1 if par else 0))
                        eng.dma_start(wst[par][:, :], w1v[ds(m, 1), :, par * WC:(par + 1) * WC].squeeze(0)).then_inc(w_l[par], 16)
                        eng.wait_ge(r_s, m * 64 + par * 32)
                        for s in range(2):
                            eng.dma_start(rowb[s][:, 0:D].bitcast(F16), xp_v[:, ds(n, 1), :].squeeze(1)).then_inc(r_l[s], 16)
                eng.wait_ge(oc_, b * 4 + 4)
                eng.dma_start(s_v[:, ds(b * QT, QT), :], tmp[:, :, :].rearrange("p j (i d) -> p (j i) d", d=D)).then_inc(od_, 16)
            eng.wait_ge(od_, NB_ * 16)


def experts(nc, v):
    N, D, DC, E, H, HT, NT, NBLK, ROW = (v[k] for k in ("N", "D", "DC", "E", "H", "HT", "NT", "NBLK", "ROW"))
    blk_e, bias, id16, w1_p, w2, b2, rows_v, acc_d = (v[k] for k in (
        "blk_e", "bias", "id16", "w1_p", "w2", "b2", "rows_v", "acc_d"))
    W1, W2 = E * DC * H, E * HT * D
    R = 3
    UPS = HT // 2
    with ExitStack() as ctx:
        sb, pb, sem = v["tensors"](ctx)
        w2_p = sb("w2_p", [P, 2 * W2], F16)
        w2st = [sb(f"w2st{i}", [P, HT * D], F32) for i in range(2)]
        b2b = sb("b2b", [P, E * D], F32)
        rowx = [sb(f"rowx{i}", [P, 2, ROW], I32) for i in range(R)]
        bxT = [sb(f"bxT{i}", [P, 2 * DC, BLK], F16) for i in range(R)]
        h32 = [sb(f"h32_{i}", [P, 2, BLK], F32) for i in range(UPS)]
        hp = [sb(f"hp{i}", [P, 2, HT, BLK], F16) for i in range(R)]
        y = [sb(f"y{i}", [P, 2, D], F32) for i in range(R)]
        psX = pb("psX", [P, 2 * DC, BLK], F16)
        psU = [pb(f"psU{i}", [P, 2, BLK], F32) for i in range(UPS)]
        psY = [pb(f"psY{i}", [P, 2, D], F32) for i in range(R)]
        ws_l = [sem(f"ws_l{i}") for i in range(2)]
        ws_h, ws_o, b_l = sem("ws_h"), sem("ws_o"), sem("b_l")
        ld = [sem(f"ld{i}") for i in range(R)]
        (xt_, xc_, up_, rl_, hh_, hl_, dn_, yb_, yg_, sc_) = map(sem, (
            "e_xt", "e_xc", "e_up", "e_relu", "e_hi", "e_lo", "e_down", "e_yb", "e_yg", "e_add"))
        primed, waited = sem("e_primed"), sem("e_waited")
        PR = 16

        def prime(eng, sems):
            for s in sems:
                eng.sem_inc(s, PR)
            eng.sem_inc(primed, 1)

        ctx2 = ctx.enter_context(ExitStack())
        block = ctx2.enter_context(nc.Block())

        @block.sync
        def _(eng):
            w2v = w2.rearrange("e (h p) d -> e p h d", p=P)
            eng.dma_start(b2b[:, :], b2.rearrange("e d -> (e d)").partition_broadcast(P)).then_inc(b_l, 16)
            for e in range(E):
                if e >= 2:
                    eng.wait_ge(ws_o, e - 1)
                eng.dma_start(w2st[e % 2][:, :].rearrange("p (h d) -> p h d", h=HT), w2v[e]).then_inc(ws_l[e % 2], 16)
            eng.wait_ge(primed, 4)

            def load(m, j):
                eng.wait_ge(xt_, m * R + (j - 2 + PR))
                eng.sem_inc(waited, 1)
                if not (isinstance(m, int) and m == 0):
                    eng.wait_ge(sc_, m * R * 32 + (j - 2) * 32)
                    eng.sem_inc(waited, 1)
                eng.dma_start(rowx[j][:, :, :], rows_v[:, ds(m * R * 2 + 2 * j, 2), :]).then_inc(ld[j], 16)

            for j in range(R):
                load(0, j)
            with eng.Fori(1, NBLK // R) as m:
                for j in range(R):
                    load(m, j)

        @block.tensor
        def _(eng):
            prime(eng, (xt_, up_, dn_))
            eng.wait_ge(primed, 4)
            eng.wait_ge(ws_o, E)

            def expert(m, j):
                return eng.value_load(blk_e[0:1, ds(m * R + j, 1)], min_val=0, max_val=E - 1)

            def turn(m, j):
                eng.wait_ge(ld[j % R], m * 16 + 16 * (j // R + 1))
                eng.wait_ge(xc_, m * R + (j + PR))
                for t in range(2):
                    for h in range(2):
                        for c in range(DC):
                            mm = eng.transpose(psX[:, 2 * h + c, t * P:(t + 1) * P],
                                               rowx[j % R][:, t, 0:D].bitcast(F16)[:, h * D + c * P:h * D + (c + 1) * P], id16[:, :])
                mm.then_inc(xt_, 1)

            def up(m, j):
                e = expert(m, j)
                eng.wait_ge(xc_, m * R + (j + 1 + PR))
                for u in range(UPS):
                    eng.wait_ge(rl_, m * R * UPS + ((j - 1) * UPS + u + 1 + PR))
                    for g in range(2):
                        n = 0
                        for a, b in PASSES:
                            for c in range(DC):
                                mm = eng.matmul(psU[u][:, g, :], w1_p[:, ds(e * (DC * H) + (a * W1 + c * H + (2 * u + g) * P), P)],
                                                bxT[j][:, 2 * b + c, :], start=(n == 0), stop=(n == 3 * DC - 1))
                                n += 1
                    mm.then_inc(up_, 1)

            def down(m, j):
                e = expert(m, j)
                eng.wait_ge(hl_, m * R * UPS + ((j + 1) * UPS + PR))
                eng.wait_ge(yb_, m * R * 2 + ((j - 2) * 2 + PR))
                for t in range(2):
                    n = 0
                    for g in range(HT):
                        for a, b in PASSES:
                            mm = eng.matmul(psY[j % R][:, t, :], hp[j % R][:, a, g, t * P:(t + 1) * P],
                                            w2_p[:, ds(e * (HT * D) + (b * W2 + g * D), D)],
                                            start=(n == 0), stop=(n == 3 * HT - 1))
                            n += 1
                mm.then_inc(dn_, 1)

            def blocks(m, first, last):
                for j in range(R):
                    up(m, j)
                    if not (last and j == R - 1):
                        turn(m, j + 1)
                    if not (first and j == 0):
                        down(m, j - 1)

            turn(0, 0)
            blocks(0, True, False)
            with eng.Fori(1, NBLK // R - 1) as m:
                blocks(m, False, False)
            blocks(NBLK // R - 1, False, True)
            down(NBLK // R - 1, R - 1)

        @block.scalar
        def _(eng):
            prime(eng, (xc_, rl_))
            for e in range(E):
                eng.wait_ge(ws_l[e % 2], 16 * (e // 2 + 1))
                eng.activation(w2_p[:, e * HT * D:(e + 1) * HT * D], w2st[e % 2][:, :], ACT.Copy, scale=WS).then_inc(ws_h, 1)
            eng.wait_ge(primed, 4)
            with eng.Fori(0, NBLK // R) as m:
                for j in range(R):
                    e = eng.value_load(blk_e[0:1, ds(m * R + j, 1)], min_val=0, max_val=E - 1)
                    eng.wait_ge(xt_, m * R + (j + 1 + PR))
                    eng.wait_ge(up_, m * R * UPS + ((j - 2) * UPS + PR))
                    eng.activation(bxT[j][:, :, :], psX[:, :, :], ACT.Copy).then_inc(xc_, 1)
                    for u in range(UPS):
                        eng.wait_ge(up_, m * R * UPS + (j * UPS + u + 1 + PR))
                        eng.wait_ge(hl_, m * R * UPS + ((j - 1) * UPS + u + 1 + PR))
                        for g in range(2):
                            a = eng.activation(h32[u][:, g, :], psU[u][:, g, :], ACT.Relu,
                                               bias=bias[:, ds(e * HT + (2 * u + g), 1)], scale=1.0 / WS)
                        a.then_inc(rl_, 1)

        @block.vector
        def _(eng):
            prime(eng, (hh_, hl_, yb_))
            for e in range(E):
                eng.wait_ge(ws_h, e + 1)
                eng.scalar_tensor_tensor(w2_p[:, W2 + e * HT * D:W2 + (e + 1) * HT * D], w2st[e % 2][:, :], WS,
                                         w2_p[:, e * HT * D:(e + 1) * HT * D], ALU.mult, ALU.subtract).then_inc(ws_o, 1)
            eng.wait_ge(primed, 4)
            eng.wait_ge(b_l, 16)

            def hidden(m, j):
                def hi(u):
                    eng.wait_ge(rl_, m * R * UPS + (j * UPS + u + 1 + PR))
                    if u == 0:
                        eng.wait_ge(dn_, m * R + (j - 2 + PR))
                    eng.tensor_copy(hp[j][:, 0, 2 * u:2 * u + 2, :], h32[u][:, :, :]).then_inc(hh_, 1)

                def lo(u):
                    eng.wait_ge(hh_, m * R * UPS + (j * UPS + u + 1 + PR))
                    eng.tensor_tensor(hp[j][:, 1, 2 * u:2 * u + 2, :], h32[u][:, :, :], hp[j][:, 0, 2 * u:2 * u + 2, :],
                                      ALU.subtract).then_inc(hl_, 1)
                for u in range(UPS):
                    hi(u)
                    if u:
                        lo(u - 1)
                lo(UPS - 1)

            def rows(m, j):
                e = eng.value_load(blk_e[0:1, ds(m * R + j, 1)], min_val=0, max_val=E - 1)
                eng.wait_ge(dn_, m * R + (j + 1 + PR))
                if not isinstance(m, int) or m * R + j > 2:
                    eng.wait_ge(sc_, m * R * 32 + (j - 2) * 32)
                for t in range(2):
                    eng.scalar_tensor_tensor(y[j % R][:, t, :], psY[j % R][:, t, :], 1.0 / WS, b2b[:, ds(e * D, D)],
                                             ALU.mult, ALU.add).then_inc(yb_, 1)

            for j in range(R):
                hidden(0, j)
                if j:
                    rows(0, j - 1)
            with eng.Fori(1, NBLK // R) as m:
                for j in range(R):
                    hidden(m, j)
                    rows(m, j - 1)
            rows(NBLK // R - 1, R - 1)

        @block.gpsimd
        def _(eng):
            def wait(sem, value):
                eng.wait_ge(sem, value)
                eng.sem_inc(waited, 1)

            prime(eng, (yg_,))
            wait(primed, 4)
            with eng.Fori(0, NBLK // R) as m:
                for j in range(R):
                    wait(yb_, m * R * 2 + (2 * j + 2 + PR))
                    for t in range(2):
                        eng.tensor_scalar(y[j][:, t, :], y[j][:, t, :], rowx[j][:, t, D + 1:D + 2].bitcast(F32), 1.0,
                                          ALU.mult, ALU.mult).then_inc(yg_, 1)
                    wait(yg_, m * R * 2 + (2 * j + 2 + PR))
                    wait(sc_, m * R * 32 + j * 32)
                    for t in range(2):
                        eng.indirect_dma_start(acc_d, bass.IndirectOffsetOnAxis(ap=rowx[j][:, t, D:D + 1].bitcast(U32), axis=0),
                                               y[j][:, t, :], None, compute_op=ALU.add).then_inc(sc_, 16)
            wait(sc_, NBLK * 32)

    xf, of, s_v, acc_v = (v[k] for k in ("xf", "of", "s_v", "acc_v"))
    G, B = 2, 4
    STEPS = NT // G
    with ExitStack() as ctx:
        sb, pb, sem = v["tensors"](ctx)
        fb = [sb(f"fb{i}", [P, G, D], F32) for i in range(B)]
        gb = [sb(f"gb{i}", [P, G, D], F32) for i in range(B)]
        sbf = [sb(f"sbf{i}", [P, G, D], F32) for i in range(B)]
        xb = [sb(f"xb{i}", [P, G, D], F32) for i in range(B)]
        f_l = [sem(f"f_ld{i}") for i in range(B)]
        f_o = [sem(f"f_out{i}") for i in range(B)]
        f_g, f_m, f_a, f_w = sem("f_silu"), sem("f_mul"), sem("f_add"), sem("f_waited")
        block = ctx.enter_context(nc.Block())

        @block.sync
        def _(eng):
            with eng.Fori(0, STEPS // B) as m:
                for j in range(B):
                    eng.wait_ge(f_o[j], m * 16)
                    for dst, src in ((fb, acc_v), (sbf, s_v), (xb, xf)):
                        eng.dma_start(dst[j][:, :, :], src[:, ds(m * B * G + j * G, G), :]).then_inc(f_l[j], 16)

        @block.scalar
        def _(eng):
            with eng.Fori(0, STEPS // B) as m:
                for j in range(B):
                    eng.wait_ge(f_l[j], m * 48 + 48)
                    eng.activation(gb[j][:, :, :], fb[j][:, :, :], ACT.Silu).then_inc(f_g, 1)

        @block.vector
        def _(eng):
            with eng.Fori(0, STEPS // B) as m:
                for j in range(B):
                    eng.wait_ge(f_g, m * B + (j + 1))
                    eng.tensor_tensor(gb[j][:, :, :], gb[j][:, :, :], sbf[j][:, :, :], ALU.mult).then_inc(f_m, 1)
                    eng.wait_ge(f_m, m * B + (j + 1))
                    eng.tensor_tensor(xb[j][:, :, :], gb[j][:, :, :], xb[j][:, :, :], ALU.add).then_inc(f_a, 1)

        @block.gpsimd
        def _(eng):
            with eng.Fori(0, STEPS // B) as m:
                for j in range(B):
                    eng.wait_ge(f_a, m * B + (j + 1))
                    eng.sem_inc(f_w, 1)
                    eng.dma_start(of[:, ds(m * B * G + j * G, G), :], xb[j][:, :, :]).then_inc(f_o[j], 16)
            for j in range(B):
                eng.wait_ge(f_o[j], STEPS // B * 16)


_INS = ["L0_attn_x", "L0_attn_Wq", "L0_attn_bq", "L0_attn_Wkv", "L0_attn_bkv", "L0_attn_Wo", "L0_ffn_router_w",
        "L0_ffn_router_b", "L0_ffn_w1", "L0_ffn_b1", "L0_ffn_w2", "L0_ffn_b2"]


def kernel(**inputs):
    import concourse.bacc as _bacc
    from concourse.bass_utils import run_bass_kernel_spmd as _run

    nc = _bacc.Bacc("TRN2", target_bir_lowering=False, num_devices=1)
    arrays, args = {}, []

    def given(name, a):
        arrays[name] = a
        args.append(nc.dram_tensor(name, a.shape, mybir.dt.from_np(a.dtype), kind="ExternalInput").ap())

    for name in _INS:
        given(f"in_{name}", np.ascontiguousarray(inputs[name]))
    shape = tuple(inputs["L0_attn_x"].shape)
    for name, a in zip(("tables", "positions"), constants(shape[0] * shape[1], inputs["L0_ffn_w1"].shape[0], shape[1])):
        given(name, a)
    args.append(nc.dram_tensor("out", shape, F32, kind="ExternalOutput").ap())
    build(nc, *args)
    r = _run(nc, [arrays], core_ids=[0])
    return r.results[0]["out"]
```

```python
from contextlib import ExitStack

import numpy as np
import concourse.bass as bass
from concourse import mybir

F32, F16, BF16, I32, U32 = (mybir.dt.float32, mybir.dt.float16, mybir.dt.bfloat16, mybir.dt.int32,
                            mybir.dt.uint32)
ALU, ACT, AX = mybir.AluOpType, mybir.ActivationFunctionType, mybir.AxisListType
ds = bass.ds

P = 128
WS = 64.0
EPS = 1e-5
MASKED = -3.0e38
FAR = -3.0e38
HEADS, HD = 8, 128
BLK = 256
PASSES = ((0, 0), (0, 1), (1, 0))
C_ID, C_MASK, C_UP, C_E = 0, P, 2 * P, 3 * P


def constants(tokens, experts, seq):
    most = tokens // BLK
    blocks = 2 * tokens // BLK + experts - 1
    q, k = np.arange(P)[:, None], np.arange(P)[None, :]
    c = np.concatenate([
        (q == k), np.where(k > q, MASKED, 0.0), (q < k),
        np.broadcast_to(np.arange(experts), (P, experts)),
        np.broadcast_to(np.arange(most) * BLK, (P, most)),
        np.broadcast_to(np.arange(blocks), (P, blocks)),
        np.arange(blocks * BLK // P - 2 * tokens // P)[None, :] * P + q], axis=1).astype(np.float32)
    pos = np.arange(seq, dtype=np.float32)[:, None]
    inv = np.exp(np.float32(-np.log(10000.0)) * np.arange(0, HD, 2, dtype=np.float32) / np.float32(HD))
    ang = (pos * inv.astype(np.float32)[None, :]).astype(np.float32)
    pe = np.zeros((seq, HD), np.float32)
    pe[:, 0::2], pe[:, 1::2] = np.sin(ang), np.cos(ang)
    return c, np.ascontiguousarray((pe * np.float32(HD ** -0.25)).T.astype(np.float32))


class Arena:

    def __init__(self, nc, at):
        self.nc, self.at = nc, -(-at // 64) * 64

    def take(self, name, shape, dt):
        size = mybir.dt.size(dt)
        for n in shape[1:]:
            size *= n
        assert self.at + size <= self.nc.sbuf_usable_end, (name, self.at, size)
        t = self.nc.alloc_sbuf_tensor_at(name, shape, dt, offset=self.at)
        self.at += -(-size // 64) * 64
        return t


def build(nc, x, wq, bq, wkv, bkv, wo, rw, rb, w1, b1, w2, b2, cst, pe, out):
    NB_, T, D = x.shape
    N = NB_ * T
    NT = N // P
    E, _, H = w1.shape
    DC, HT = D // P, H // P
    QT = T // P
    MOST = N // BLK
    NBLK = 2 * N // BLK + E - 1
    FREE = NBLK * BLK // P - 2 * NT
    C_TH, C_BL, C_FR = C_E + E, C_E + E + MOST, C_E + E + MOST + NBLK
    CW = C_FR + FREE
    SC = float(HD) ** -0.25
    ROW = D + 2
    SLOTS = NBLK * BLK
    EARLY = 3
    W1, W2 = DC * H, HT * D
    assert D == 256 and HD == P and T == 1024 and H == 1024 and E == 8 and NBLK % 3 == 0

    xf = x.rearrange("b t d -> (b t) d").rearrange("(n p) d -> p n d", p=P)
    of = out.rearrange("b t d -> (b t) d").rearrange("(n p) d -> p n d", p=P)
    xp_d = nc.dram_tensor("xn_split", (N, 2 * D), F16, kind="Internal").ap()
    s_d = nc.dram_tensor("attention", (N, D), F32, kind="Internal").ap()
    rows_d = nc.dram_tensor("expert_rows", (SLOTS, ROW), I32, kind="Internal").ap()
    acc_d = nc.dram_tensor("mixture", (N + BLK, D), F32, kind="Internal").ap()
    xp_v = xp_d.rearrange("(n p) d -> p n d", p=P)
    s_v = s_d.rearrange("(n p) d -> p n d", p=P)
    acc_v = acc_d.rearrange("(n p) d -> p n d", p=P)
    rows_v = rows_d.rearrange("(k p) c -> p k c", p=P)
    xT_d = nc.dram_tensor("xn_transposed", (P, 2 * DC, N), F16, kind="Internal").ap()

    def tensors(ctx):
        def pb(name, shape, dt):
            return ctx.enter_context(nc.psum_tensor(name, shape, dt))

        def sem(name):
            return ctx.enter_context(nc.semaphore(name))
        return pb, sem

    kept = Arena(nc, nc.sbuf_base)
    pos = kept.take("pos", [P, 2, NT], U32)
    free = kept.take("free", [P, FREE], U32)
    gate = kept.take("gate", [P, 2, NT], F32)
    tok = kept.take("tok", [P, NT], I32)
    blk_e = kept.take("blk_e", [P, NBLK], I32)
    bias = kept.take("bias", [P, E * HT + HEADS + 2], F32)
    B_Q, B_K = E * HT, E * HT + HEADS
    id16 = kept.take("id16", [P, P], F16)
    w1_p = kept.take("w1_p", [P, 2 * E * W1], F16)
    w2_at = kept.at
    w2_p = kept.take("w2_p", [P, 2 * E * W2], F16)
    rest_at = kept.at

    area = Arena(nc, rest_at)
    id32 = area.take("id32", [P, P], F32)
    idb = area.take("idb", [P, P], BF16)
    maskb = area.take("maskb", [P, P], BF16)
    pe_sb = area.take("pe_sb", [P, T], F32)
    bv = area.take("bv", [P, HD], F32)
    wq_p = area.take("wq_p", [P, 2 * DC * HEADS * HD], F16)
    wkv_p = area.take("wkv_p", [P, 2, DC, 2 * HD], F16)
    wo_p = area.take("wo_p", [P, 2, HEADS, D], F16)
    xTb = area.take("xTb", [P, 2 * DC, T], F16)
    attn_at = area.at

    with ExitStack() as ctx:
        pb, sem = tensors(ctx)
        x_sb = w1_p[:, 0:2 * NT * D].bitcast(F32).rearrange("p (n d) -> p n d", d=D)
        xp = w1_p[:, 2 * NT * D:4 * NT * D].rearrange("p (n h d) -> p n h d", h=2, d=D)
        low = Arena(nc, w2_at)
        xT = low.take("xT", [P, 2 * DC, N - T], F16)
        wst = low.take("wst", [P, 2048], F32)
        wst2 = low.take("wst2", [P, 2048], F32)
        kvst = low.take("kvst", [P, DC, 2 * HD], F32)
        high = Arena(nc, attn_at)
        sb = high.take
        c_sb = sb("c_sb", [P, CW], F32)
        up16 = sb("up16", [P, P], F16)
        one16 = sb("one16", [P, P], F16)
        brow = sb("brow", [E * HT + HEADS + 2, P], F32)
        rbb = sb("rbb", [P, E], F32)
        eps = sb("eps", [P, 1], F32)
        rw_s = sb("rw_s", [P, DC, E], F32)
        rw_p = sb("rw_p", [P, 2, DC, E], F16)
        st = sb("st", [P, NT, 6], F32)
        mv = sb("mv", [P, NT, 2], F32)
        rs = sb("rs", [P, 4, NT], F32)
        L = sb("L", [P, NT, E], F32)
        L2 = sb("L2", [P, NT, E], F32)
        cand = sb("cand", [P, NT, E], F32)
        oh = [sb(f"oh{i}", [P, NT, E], F32) for i in range(2)]
        M16 = sb("M16", [P, NT * E], F16)
        m_ = [sb(f"m{i}", [P, NT], F32) for i in range(2)]
        ix = [sb(f"ix{i}", [P, NT], F32) for i in range(2)]
        ex = sb("ex", [P, 3, NT], F32)
        sc = [sb(f"scan{i}", [P, NT, E], F32) for i in range(2)]
        tot = sb("tot", [P, NT, E], F32)
        se = [sb(f"scane{i}", [P, 2, E], F32) for i in range(2)]
        nbl = sb("nbl", [P, 2, E], F32)
        fre = sb("fre", [P, E], F32)
        frs = sb("frs", [P, FREE], F32)
        cmpb = sb("cmpb", [P, max(NBLK, MOST, FREE) * E], F32)
        bf = sb("bf", [P, NBLK], F32)
        psT = [pb(f"psT{i}", [P, 4, 2 * P], F16) for i in range(2)]
        psL = pb("psL", [P, NT * E], F32)
        psR = pb("psR", [P, 2, NT * E], F32)
        psB = pb("psB", [P, P], F32)
        s_x = [sem(f"x_loaded{i}") for i in range(4)]
        (s_c, s_w, s_cc, s_bn, s_var, s_sd, s_xn, s_xh, s_xl, s_z, s_one, s_tr, s_te, s_td, s_wh, s_wl, s_b, s_lg, s_ch,
         s_diff, s_pick, s_cnt, s_e, s_dr) = map(sem, (
             "tables", "weights", "tables_cast", "stats", "variance", "std", "xn", "xn_hi", "xn_lo", "zeroed", "ones",
             "transposed", "copied_act", "copied_dve", "w_hi", "w_lo", "bias_turned", "logits", "chain", "top_diff",
             "picked", "counted", "exp_diff", "stored"))
        block = ctx.enter_context(nc.Block())
        G4 = NT // 4

        def rowsT(job):
            t = job * 2 * P
            return xTb[:, :, t:t + 2 * P] if t < T else xT[:, :, t - T:t - T + 2 * P]

        @block.sync
        def _(eng):
            for g in range(4):
                eng.dma_start(x_sb[:, g * G4:(g + 1) * G4, :], xf[:, g * G4:(g + 1) * G4, :]).then_inc(s_x[g], 16)
            for g in range(4):
                eng.wait_ge(s_xl, g + 1)
                eng.dma_start(xp_v[:, g * G4:(g + 1) * G4, :],
                              xp[:, g * G4:(g + 1) * G4].rearrange("p n h d -> p n (h d)")).then_inc(s_dr, 16)
            eng.wait_ge(s_te, NT // 4)
            eng.wait_ge(s_td, NT // 4)
            eng.dma_start(xT_d[:, :, T:N], xT[:, :, :]).then_inc(s_dr, 16)
            eng.wait_ge(s_dr, 80)

        @block.gpsimd
        def _(eng):
            eng.memset(eps[:, :], EPS).then_inc(s_z, 1)
            eng.memset(one16[:, :], 1.0).then_inc(s_one, 1)
            eng.iota(tok[:, :], [[P, NT]], base=0, channel_multiplier=1)
            for g in range(4):
                eng.wait_ge(s_xh, g + 1)
                sl = slice(g * G4, (g + 1) * G4)
                eng.tensor_tensor(xp[:, sl, 1, :], x_sb[:, sl, :], xp[:, sl, 0, :], ALU.subtract).then_inc(s_xl, 1)

        @block.scalar
        def _(eng):
            for dst, src in ((c_sb[:, :], cst), (rw_s[:, :, :], rw.rearrange("(c p) e -> p c e", p=P)),
                             (rbb[:, :], rb.partition_broadcast(P)),
                             (brow[0:E * HT, :], b1.rearrange("e (h p) -> (e h) p", p=P)),
                             (brow[E * HT:E * HT + HEADS, :], bq.rearrange("(h p) -> h p", p=P)),
                             (brow[E * HT + HEADS:, :], bkv.rearrange("(h p) -> h p", p=P))):
                eng.dma_start(dst, src).then_inc(s_c, 16)
            for dst, src in ((wst[:, :].rearrange("p (c n) -> p c n", c=DC), wq.rearrange("(c p) n -> p c n", p=P)),
                             (kvst[:, :, :], wkv.rearrange("(c p) n -> p c n", p=P)),
                             (wst2[:, :].rearrange("p (h n) -> p h n", h=HEADS), wo.rearrange("(h p) n -> p h n", p=P)),
                             (bv[:, :], bkv[HD:2 * HD].partition_broadcast(P)),
                             (pe_sb[:, :], pe)):
                eng.dma_start(dst, src).then_inc(s_w, 16)
            eng.wait_ge(s_c, 96)
            for dst, src in ((id32, C_ID), (id16, C_ID), (idb, C_ID), (maskb, C_MASK), (up16, C_UP)):
                eng.activation(dst[:, :], c_sb[:, src:src + P], ACT.Copy).then_inc(s_cc, 1)
            eng.wait_ge(s_b, 1)
            eng.activation(bias[:, 0:E * HT], psB[:, 0:E * HT], ACT.Copy)
            eng.activation(bias[:, E * HT:], psB[:, E * HT:E * HT + HEADS + 2], ACT.Copy, scale=SC)
            eng.wait_ge(s_z, 1)

            def std(k, sl):
                eng.wait_ge(s_var, k)
                eng.activation(rs[:, 0, sl], mv[:, sl, 1], ACT.Sqrt, bias=eps[:, :]).then_inc(s_sd, 1)

            def his(g):
                sl = slice(g * G4, (g + 1) * G4)
                eng.wait_ge(s_xn, g + 1)
                eng.activation(xp[:, sl, 0, :], x_sb[:, sl, :], ACT.Copy).then_inc(s_xh, 1)

            def weights():
                eng.activation(rw_p[:, 0], rw_s[:, :, :], ACT.Copy, scale=WS).then_inc(s_wh, 1)
                eng.wait_ge(s_w, 80)
                eng.activation(wkv_p[:, 0], kvst[:, :, :], ACT.Copy, scale=WS).then_inc(s_wh, 1)
                eng.activation(wq_p[:, 0:2048], wst[:, :], ACT.Copy, scale=WS).then_inc(s_wh, 1)
                eng.activation(wo_p[:, 0], wst2[:, :].rearrange("p (h n) -> p h n", h=HEADS), ACT.Copy,
                               scale=WS).then_inc(s_wh, 1)

            def out_of_psum(g):
                for i in range(2 * g, 2 * g + 2):
                    eng.wait_ge(s_tr, 2 * i + 1)
                    eng.activation(rowsT(2 * i), psT[0][:, :, :], ACT.Copy).then_inc(s_te, 1)

            std(1, slice(0, G4))
            his(0)
            std(2, slice(G4, NT))
            weights()
            his(1)
            out_of_psum(0)
            his(2)
            out_of_psum(1)
            his(3)
            out_of_psum(2)
            out_of_psum(3)
            eng.wait_ge(s_diff, 1)
            eng.activation(ex[:, 0, :], ex[:, 2, :], ACT.Exp).then_inc(s_e, 1)

        @block.tensor
        def _(eng):
            eng.wait_ge(s_cc, 5)
            eng.transpose(psB[:, 0:E * HT + HEADS + 2], brow[:, :], id32[0:E * HT + HEADS + 2, 0:E * HT + HEADS + 2]).then_inc(s_b, 1)
            with eng.Fori(0, 4) as g:
                eng.wait_ge(s_xl, g + 1)
                for j in range(4):
                    q = j % 2
                    eng.wait_ge((s_te, s_td)[q], g * 2 + j // 2)
                    for t in range(2):
                        for h in range(2):
                            for c in range(DC):
                                mm = eng.transpose(psT[q][:, 2 * h + c, t * P:(t + 1) * P],
                                                   xp[:, ds(g * 8 + 2 * j + t, 1), h, c * P:(c + 1) * P].squeeze(1),
                                                   id16[:, :])
                    mm.then_inc(s_tr, 1)
            eng.wait_ge(s_te, NT // 4)
            eng.wait_ge(s_td, NT // 4)
            eng.wait_ge(s_wl, 1)
            for lo, hi, src, width in ((0, G4, xTb[:, :, :], T), (G4, NT, xT[:, :, :], N - T)):
                flat = src.rearrange("p c t -> p (c t)")
                with eng.Fori(0, (hi - lo) // 4) as n:
                    for t in range(4):
                        k = 0
                        for a, b in PASSES:
                            for c in range(DC):
                                mm = eng.matmul(psL[:, ds(n * 4 * E + (lo + t) * E, E)], flat[:, ds(n * 4 * P + ((2 * a + c) * width + t * P), P)],
                                                rw_p[:, b, c, :], start=(k == 0), stop=(k == 3 * DC - 1))
                                k += 1
                    mm.then_inc(s_lg, 1)
            eng.wait_ge(s_one, 1)
            eng.wait_ge(s_pick, 1)
            eng.matmul(psR[:, 0, :], up16[:, :], M16[:, :], start=True, stop=True)
            eng.matmul(psR[:, 1, :], one16[:, :], M16[:, :], start=True, stop=True).then_inc(s_cnt, 1)

        @block.vector
        def _(eng):
            n_ch = [0]

            def step(ins):
                n_ch[0] += 1
                ins.then_inc(s_ch, 1)

            def link(ins):
                step(ins)
                eng.wait_ge(s_ch, n_ch[0])

            def stats(g):
                eng.wait_ge(s_x[g], 16)
                for n in range(g * G4, (g + 1) * G4):
                    eng.bn_stats(st[:, n, :], x_sb[:, n, :]).then_inc(s_bn, 1)

            def variance(g, sl):
                eng.wait_ge(s_bn, g * G4)
                step(eng.tensor_tensor(mv[:, sl, 0], st[:, sl, 1], st[:, sl, 4], ALU.add))
                step(eng.tensor_tensor(rs[:, 1, sl], st[:, sl, 1], st[:, sl, 4], ALU.subtract))
                link(eng.tensor_tensor(rs[:, 2, sl], st[:, sl, 2], st[:, sl, 5], ALU.add))
                step(eng.tensor_scalar(mv[:, sl, 0], mv[:, sl, 0], 0.5, None, ALU.mult))
                link(eng.tensor_tensor(rs[:, 1, sl], rs[:, 1, sl], rs[:, 1, sl], ALU.mult))
                link(eng.tensor_scalar(rs[:, 1, sl], rs[:, 1, sl], 0.25, None, ALU.mult))
                eng.scalar_tensor_tensor(mv[:, sl, 1], rs[:, 2, sl], 1.0 / D, rs[:, 1, sl], ALU.mult, ALU.add).then_inc(s_var, 1)

            def rstd(k, sl):
                eng.wait_ge(s_sd, k)
                step(eng.tensor_scalar(rs[:, 1, sl], mv[:, sl, 1], EPS, None, ALU.add))
                link(eng.reciprocal(rs[:, 2, sl], rs[:, 0, sl]))
                link(eng.tensor_tensor(rs[:, 3, sl], rs[:, 2, sl], rs[:, 2, sl], ALU.mult))
                link(eng.tensor_tensor(rs[:, 3, sl], rs[:, 3, sl], rs[:, 1, sl], ALU.mult))
                link(eng.tensor_scalar(rs[:, 3, sl], rs[:, 3, sl], -0.5, 1.5, ALU.mult, ALU.add))
                link(eng.tensor_tensor(rs[:, 0, sl], rs[:, 2, sl], rs[:, 3, sl], ALU.mult))

            def normalise(g):
                for n in range(g * G4, (g + 1) * G4):
                    a = eng.tensor_scalar(x_sb[:, n, :], x_sb[:, n, :], mv[:, n, 0:1], rs[:, 0, n:n + 1], ALU.subtract, ALU.mult)
                a.then_inc(s_xn, 1)

            stats(0)
            variance(1, slice(0, G4))
            stats(1)
            rstd(1, slice(0, G4))
            normalise(0)
            stats(2)
            stats(3)
            variance(4, slice(G4, NT))
            rstd(2, slice(G4, NT))
            normalise(1)
            normalise(2)
            normalise(3)
            eng.wait_ge(s_wh, 4)
            for dst, src, hi in ((rw_p[:, 1], rw_s[:, :, :], rw_p[:, 0]), (wkv_p[:, 1], kvst[:, :, :], wkv_p[:, 0]),
                                 (wq_p[:, 2048:], wst[:, :], wq_p[:, 0:2048]),
                                 (wo_p[:, 1], wst2[:, :].rearrange("p (h n) -> p h n", h=HEADS), wo_p[:, 0])):
                eng.scalar_tensor_tensor(dst, src, WS, hi, ALU.mult, ALU.subtract).then_inc(s_wl, 1)
            for i in range(NT // 4):
                eng.wait_ge(s_tr, 2 * i + 2)
                eng.tensor_copy(rowsT(2 * i + 1), psT[1][:, :, :]).then_inc(s_td, 1)

            ids = c_sb[:, C_E:C_E + E].unsqueeze(1).to_broadcast([P, NT, E])
            eng.wait_ge(s_c, 96)
            eng.wait_ge(s_lg, NT // 4)

            def wide(a):
                return a.unsqueeze(2).to_broadcast([P, NT, E])

            link(eng.scalar_tensor_tensor(L[:, :, :], psL[:, :].rearrange("p (n e) -> p n e", e=E), 1.0 / WS,
                                          rbb[:, :].unsqueeze(1).to_broadcast([P, NT, E]), ALU.mult, ALU.add))
            src = L
            for i in range(2):
                link(eng.tensor_reduce(m_[i][:, :], src[:, :, :], AX.X, ALU.max))
                link(eng.tensor_tensor(cand[:, :, :], src[:, :, :], wide(m_[i][:, :]), ALU.is_lt))
                link(eng.scalar_tensor_tensor(cand[:, :, :], cand[:, :, :], float(E), ids, ALU.mult, ALU.add))
                link(eng.tensor_reduce(ix[i][:, :], cand[:, :, :], AX.X, ALU.min))
                link(eng.tensor_tensor(oh[i][:, :, :], ids, wide(ix[i][:, :]), ALU.is_equal))
                if i == 0:
                    link(eng.scalar_tensor_tensor(L2[:, :, :], oh[0][:, :, :], FAR, L[:, :, :], ALU.mult, ALU.add))
                    src = L2
            eng.tensor_tensor(M16[:, :].rearrange("p (n e) -> p n e", e=E), oh[0][:, :, :], oh[1][:, :, :],
                              ALU.add).then_inc(s_pick, 1)
            eng.tensor_tensor(ex[:, 2, :], m_[1][:, :], m_[0][:, :], ALU.subtract).then_inc(s_diff, 1)
            eng.wait_ge(s_e, 1)
            link(eng.tensor_scalar(ex[:, 1, :], ex[:, 0, :], 1.0, None, ALU.add))
            link(eng.reciprocal(gate[:, 0, :], ex[:, 1, :]))
            step(eng.tensor_tensor(gate[:, 1, :], ex[:, 0, :], gate[:, 0, :], ALU.mult))
            eng.wait_ge(s_cnt, 1)
            step(eng.tensor_copy(tot[:, :, :], psR[:, 1, :].rearrange("p (n e) -> p n e", e=E)))
            link(eng.tensor_copy(sc[0][:, :, :], psR[:, 1, :].rearrange("p (n e) -> p n e", e=E)))
            cur, by = 0, 1
            while by < NT:
                a, b = sc[cur], sc[1 - cur]
                step(eng.tensor_copy(b[:, 0:by, :], a[:, 0:by, :]))
                link(eng.tensor_tensor(b[:, by:, :], a[:, by:, :], a[:, 0:NT - by, :], ALU.add))
                cur, by = 1 - cur, 2 * by
            cnt = sc[cur][:, NT - 1, :]
            cm = cmpb[:, 0:MOST * E].rearrange("p (e k) -> p e k", e=E)
            step(eng.tensor_copy(nbl[:, 1, :], cnt))
            link(eng.tensor_tensor(cm, c_sb[:, C_TH:C_TH + MOST].unsqueeze(1).to_broadcast([P, E, MOST]),
                                   cnt.unsqueeze(2).to_broadcast([P, E, MOST]), ALU.is_lt))
            link(eng.tensor_reduce(nbl[:, 0, :], cm, AX.X, ALU.add))
            link(eng.tensor_copy(se[0][:, :, :], nbl[:, :, :]))
            ce, by = 0, 1
            while by < E:
                a, b = se[ce], se[1 - ce]
                step(eng.tensor_copy(b[:, :, 0:by], a[:, :, 0:by]))
                link(eng.tensor_tensor(b[:, :, by:], a[:, :, by:], a[:, :, 0:E - by], ALU.add))
                ce, by = 1 - ce, 2 * by
            ends = se[ce][:, 0, :]
            first = se[1 - ce]
            link(eng.tensor_tensor(first[:, :, :], se[ce][:, :, :], nbl[:, :, :], ALU.subtract))
            rank = sc[1 - cur]
            link(eng.tensor_tensor(rank[:, :, :], sc[cur][:, :, :], tot[:, :, :], ALU.subtract))
            link(eng.tensor_tensor(rank[:, :, :], rank[:, :, :], psR[:, 0, :].rearrange("p (n e) -> p n e", e=E), ALU.add))
            link(eng.scalar_tensor_tensor(rank[:, :, :], first[:, 0, :].unsqueeze(1).to_broadcast([P, NT, E]), float(BLK),
                                          rank[:, :, :], ALU.mult, ALU.add))
            for i in range(2):
                link(eng.tensor_tensor(cand[:, :, :], oh[i][:, :, :], rank[:, :, :], ALU.mult))
                link(eng.tensor_reduce(ix[i][:, :], cand[:, :, :], AX.X, ALU.add))
                step(eng.tensor_copy(pos[:, i, :], ix[i][:, :]))
            cb = cmpb[:, 0:NBLK * E].rearrange("p (k e) -> p k e", e=E)
            link(eng.tensor_tensor(cb, c_sb[:, C_BL:C_BL + NBLK].unsqueeze(2).to_broadcast([P, NBLK, E]),
                                   ends.unsqueeze(1).to_broadcast([P, NBLK, E]), ALU.is_ge))
            link(eng.tensor_reduce(bf[:, :], cb, AX.X, ALU.add))
            step(eng.tensor_scalar(blk_e[:, :], bf[:, :], float(E - 1), None, ALU.min))
            link(eng.scalar_tensor_tensor(fre[:, :], first[:, 0, :], float(BLK), first[:, 1, :], ALU.mult, ALU.subtract))
            jj = c_sb[:, C_FR:C_FR + FREE]
            cf = cmpb[:, 0:FREE * E].rearrange("p (k e) -> p k e", e=E)
            link(eng.tensor_tensor(cf, jj.unsqueeze(2).to_broadcast([P, FREE, E]), fre[:, :].unsqueeze(1).to_broadcast([P, FREE, E]),
                                   ALU.is_ge))
            link(eng.tensor_tensor(cf, cf, nbl[:, 1, :].unsqueeze(1).to_broadcast([P, FREE, E]), ALU.mult))
            link(eng.tensor_reduce(frs[:, :], cf, AX.X, ALU.add))
            step(eng.tensor_tensor(free[:, :], frs[:, :], jj, ALU.add))

    attention(nc, locals())
    experts(nc, locals())


def attention(nc, v):
    NB_, T, QT, N, D, DC, E, H = (v[k] for k in ("NB_", "T", "QT", "N", "D", "DC", "E", "H"))
    NT, HT, SC, ROW, B_Q, B_K, FREE, EARLY, W1, W2 = (v[k] for k in (
        "NT", "HT", "SC", "ROW", "B_Q", "B_K", "FREE", "EARLY", "W1", "W2"))
    pos, free, gate, tok, bias, id32, idb, maskb, pe_sb, bv = (v[k] for k in (
        "pos", "free", "gate", "tok", "bias", "id32", "idb", "maskb", "pe_sb", "bv"))
    wq_p, wkv_p, wo_p, xTb, w1_p, w2_p, xT_d = (v[k] for k in ("wq_p", "wkv_p", "wo_p", "xTb", "w1_p", "w2_p", "xT_d"))
    xp_v, s_v, rows_d, acc_v, w1, w2 = (v[k] for k in ("xp_v", "s_v", "rows_d", "acc_v", "w1", "w2"))
    PRIME = 16
    ORDER = (0, 4, 1, 5, 2, 6, 3, 7)
    CHUNKS = [1 if u < 4 else 2 for u in ORDER]
    CUM = [sum(CHUNKS[:p]) for p in range(9)]
    CH = CUM[8]
    WC = E * W1 // NT
    LATE = E - EARLY
    LATE_TMP = 3
    PIECES = EARLY * W2 // WC // NB_
    assert WC == 512 and T == 2 * WC and EARLY * W2 == PIECES * WC * NB_
    with ExitStack() as ctx:
        pb, sem = v["tensors"](ctx)
        sb = Arena(nc, v["attn_at"]).take
        qp = sb("qp", [P, 2 * HEADS * T], F16)
        kp = sb("kp", [P, 2, T], F16)
        vp = sb("vp", [P, 2, QT, HD], F16)
        nmax = sb("nmax", [P, 4], F32)
        rsum = sb("rsum", [P, 4], F32)
        rrec = sb("rrec", [P, 4], F32)
        wst = [sb(f"wpiece{i}", [P, WC], F32) for i in range(2)]
        rowb = [sb(f"rowb{i}", [P, ROW], I32) for i in range(2)]
        idx = [sb(f"idx{i}", [P, 1], U32) for i in range(2)]
        over = Arena(nc, v["w2_at"] + EARLY * 2 * W2 * 2)
        pT = [over.take(f"pT{g}", [P, 2, 4 * (g + 1), 512], F16) for g in range(2)]
        tmp_at = over.at
        wide = [max(ORDER[p], ORDER[p + 4]) + 1 for p in range(4)]
        pr = [over.take(f"pr{i}", [P, wide[i] * P], F32) for i in range(4)]
        tmp = Arena(nc, tmp_at).take("tmp", [P, 4, 512], F32)
        zrow = over.take("zrow", [P, 2, ROW], I32)
        w2st = [xTb[:, :, :].rearrange("p c t -> p (c t)").bitcast(F32), wq_p[:, :].bitcast(F32)]
        psS = [pb("psS0", [P, 1, 512], F32), pb("psS1", [P, 2, 512], F32)]
        psP = [pb(f"psP{i}", [P, 4, P], F32) for i in range(3)]
        psO = [pb(f"psO{i}", [P, 512], F32) for i in range(2)]
        bank = [psS[0][:, 0, :], psS[1][:, 0, :], psS[1][:, 1, :], psP[2][:, :, :].rearrange("p a n -> p (a n)")]
        names = ("a_sc", "a_max", "a_exp", "a_rec", "a_nrm", "a_tr", "a_hi", "a_lo", "a_pv", "a_ah", "a_al",
                 "j_mm", "j_t", "j_hi", "j_lo", "o_mm", "o_cp", "a_pr", "a_waited")
        (sc_, mx_, ex_, rc_, nm_, tr_, hi_, lo_, pv_, ah_, al_, jm_, jt_, jh_, jl_, om_, oc_, primed, waited) = map(sem, names)
        od_, xl_, z_, zi_, fr_, za_ = map(sem, ("o_dma", "x_next", "zero_rows", "zero_ids", "free_rows", "zero_acc"))
        w_l = [sem(f"w_ld{i}") for i in range(2)]
        w_u = [sem(f"w_used{i}") for i in range(2)]
        w_c = sem("w_chain")
        l_l = [sem(f"late_ld{i}") for i in range(2)]
        l_h, l_o = sem("late_hi"), sem("late_lo")
        r_l = [sem(f"r_ld{i}") for i in range(2)]
        r_c, r_s = sem("r_copy"), sem("r_scatter")
        JOBS = 4 + 2 * HEADS
        USES = [(PIECES + 1) // 2 + HEADS // 2, PIECES // 2 + HEADS // 2]
        block = ctx.enter_context(nc.Block())
        qoff = HEADS * T

        def prime(eng, sems):
            for s in sems:
                eng.sem_inc(s, PRIME)
            eng.sem_inc(primed, 1)

        def at(h, p):
            return h + p // 8, p % 8

        @block.tensor
        def _(eng):
            prime(eng, (sc_, tr_, pv_))
            eng.wait_ge(primed, 4)

            def proj(out, lhs, rhs):
                k = 0
                for a, b in PASSES:
                    for c in range(DC):
                        mm = eng.matmul(out, lhs(a, c), rhs(b, c), start=(k == 0), stop=(k == 3 * DC - 1))
                        k += 1
                return mm

            with eng.Fori(0, NB_) as b:
                eng.wait_ge(oc_, b * 4)
                eng.wait_ge(xl_, b * 16)
                for j in range(2):
                    proj(bank[j], lambda a, c: wkv_p[:, a, c, 0:HD],
                         lambda a, c: xTb[:, 2 * a + c, j * 512:(j + 1) * 512]).then_inc(jm_, 1)
                for j in range(2):
                    for t in range(4):
                        mm = proj(bank[2 + j][:, t * P:(t + 1) * P],
                                  lambda a, c: xTb[:, 2 * a + c, (4 * j + t) * P:(4 * j + t + 1) * P],
                                  lambda a, c: wkv_p[:, a, c, HD:2 * HD])
                    mm.then_inc(jm_, 1)
                with eng.Fori(0, HEADS // 2) as hh:
                    for j in range(4):
                        eng.wait_ge(jt_, b * JOBS + hh * 4 + (j + 1))
                        proj(bank[j], lambda a, c: wq_p[:, ds(hh * 2 * HD + ((2 * a + c) * HEADS * HD + (j // 2) * HD), HD)],
                             lambda a, c: xTb[:, 2 * a + c, (j % 2) * 512:(j % 2 + 1) * 512]).then_inc(jm_, 1)

                def scores(h, p):
                    u = ORDER[p]
                    eng.wait_ge(ex_, b * 64 + h * 8 + (p - 1 + PRIME))
                    n = (u + 1) * P
                    for lo in range(0, n, 512):
                        w = min(512, n - lo)
                        last = lo + w == n
                        o = psS[p % 2][:, lo // 512, 0:w]
                        for k, (a, c) in enumerate(PASSES):
                            mm = eng.matmul(o, qp[:, ds(h * T + (a * qoff + u * P), P)], kp[:, c, lo:lo + w],
                                            start=(k == 0), stop=(k == 2 and not last))
                        if last:
                            mm = eng.matmul(o[:, w - P:w], idb[:, :], maskb[:, :], start=False, stop=True)
                    mm.then_inc(sc_, 1)

                def turn(h, p):
                    u = ORDER[p]
                    eng.wait_ge(nm_, b * 64 + h * 8 + (p + 1 + PRIME))
                    for k in range(CHUNKS[p]):
                        c = CUM[p] + k
                        eng.wait_ge(lo_, b * 8 * CH + h * CH + (c - 2 + PRIME))
                        for t in range(min(4, u + 1 - 4 * k)):
                            mm = eng.transpose(psP[c % 3][:, t, :], pr[p % 4][:, (4 * k + t) * P:(4 * k + t + 1) * P], id32[:, :])
                        mm.then_inc(tr_, 1)

                def values(h, g):
                    eng.wait_ge(lo_, b * 8 * CH + h * CH + (CUM[7 + g] + PRIME))
                    eng.wait_ge(al_, b * 16 + h * 2 + (g - 1 + PRIME))
                    last = 4 * g + 3
                    for j in range(last + 1):
                        q0 = max(0, j - 4 * g) * P
                        for k, (a, c) in enumerate(PASSES):
                            mm = eng.matmul(psO[g][:, q0:512], vp[:, a, j, :], pT[g][:, c, j, q0:512],
                                            start=(j == 0 and k == 0), stop=(j == last and k == 2))
                    mm.then_inc(pv_, 1)

                def head(h, first, last):
                    for p in range(8):
                        if p > 1 or not first:
                            turn(*at(h, p - 2))
                        if p in (1, 2) and not first:
                            values(h - 1, p - 1)
                        if p < 6 or not last:
                            scores(*at(h, p + 2))

                eng.wait_ge(jl_, b * JOBS + JOBS)
                scores(0, 0)
                scores(0, 1)
                head(0, True, False)
                with eng.Fori(1, HEADS - 1) as h:
                    head(h, False, False)
                head(HEADS - 1, False, True)
                turn(HEADS - 1, 6)
                turn(HEADS - 1, 7)
                values(HEADS - 1, 0)
                values(HEADS - 1, 1)
                eng.wait_ge(al_, b * 16 + (16 + PRIME))
                for i in range(QT):
                    o = bank[i // 2][:, (i % 2) * D:(i % 2 + 1) * D]
                    for h in range(HEADS):
                        for k, (a, c) in enumerate(PASSES):
                            mm = eng.matmul(o, qp[:, a * qoff + h * T + i * P:a * qoff + h * T + (i + 1) * P], wo_p[:, c, h, :],
                                            start=(h == 0 and k == 0), stop=(h == HEADS - 1 and k == 2))
                    if i % 2:
                        mm.then_inc(om_, 1)

        @block.scalar
        def _(eng):
            prime(eng, (ex_, hi_, ah_))
            eng.wait_ge(primed, 4)
            with eng.Fori(0, NB_) as b:
                def job(kind, j, jj, h):
                    eng.wait_ge(jt_, b * JOBS + jj)
                    if kind == "v":
                        eng.activation(vp[:, 0, 4 * (j % 2):4 * (j % 2) + 4, :],
                                       tmp[:, j, :].rearrange("p (t n) -> p t n", n=P), ACT.Copy).then_inc(jh_, 1)
                    elif kind == "k":
                        eng.activation(kp[:, 0, j * 512:(j + 1) * 512], tmp[:, j, :], ACT.Identity,
                                       bias=bias[:, B_K:B_K + 1]).then_inc(jh_, 1)
                    else:
                        eng.activation(qp[:, ds(h * T + (j % 2) * 512, 512)], tmp[:, j, :], ACT.Identity,
                                       bias=bias[:, ds(h + B_Q, 1)]).then_inc(jh_, 1)

                for j in range(4):
                    job("kkvv"[j], j, j + 1, None)
                with eng.Fori(0, HEADS // 2) as hh:
                    for j in range(4):
                        job("q", j, hh * 4 + (4 + j + 1), hh * 2 + j // 2)

                def expo(h, p):
                    n = (ORDER[p] + 1) * P
                    eng.wait_ge(mx_, b * 64 + h * 8 + (p + 1 + PRIME))
                    eng.wait_ge(tr_, b * 8 * CH + h * CH + ((CUM[p - 3] if p > 3 else CUM[p + 5] - CH) + PRIME))
                    eng.activation(pr[p % 4][:, 0:n], psS[p % 2][:, :, :].rearrange("p a n -> p (a n)")[:, 0:n], ACT.Exp,
                                   bias=nmax[:, p % 4:p % 4 + 1], accum_out=rsum[:, p % 4:p % 4 + 1]).then_inc(ex_, 1)

                def his(h, p):
                    g, qi = ORDER[p] // 4, ORDER[p] % 4
                    eng.wait_ge(pv_, b * 16 + h * 2 + (g - 1 + PRIME))
                    for k in range(CHUNKS[p]):
                        c = CUM[p] + k
                        n = min(4, ORDER[p] + 1 - 4 * k)
                        eng.wait_ge(tr_, b * 8 * CH + h * CH + (c + 1 + PRIME))
                        eng.activation(pT[g][:, 0, 4 * k:4 * k + n, qi * P:(qi + 1) * P], psP[c % 3][:, 0:n, :], ACT.Copy).then_inc(hi_, 1)

                def outs(h, g):
                    eng.wait_ge(pv_, b * 16 + h * 2 + (g + 1 + PRIME))
                    eng.activation(qp[:, ds(h * T + g * 512, 512)], psO[g][:, :], ACT.Copy).then_inc(ah_, 1)

                def head(h, first, last):
                    for p in range(8):
                        if p < 7 or not last:
                            expo(*at(h, p + 1))
                        if p > 1 or not first:
                            his(*at(h, p - 2))
                        if p in (2, 3) and not first:
                            outs(h - 1, p - 2)

                expo(0, 0)
                head(0, True, False)
                with eng.Fori(1, HEADS - 1) as h:
                    head(h, False, False)
                head(HEADS - 1, False, True)
                his(HEADS - 1, 6)
                his(HEADS - 1, 7)
                outs(HEADS - 1, 0)
                outs(HEADS - 1, 1)
                eng.wait_ge(jl_, b * JOBS + JOBS)
                for j in range(4):
                    eng.wait_ge(om_, b * 4 + (j + 1))
                    eng.activation(tmp[:, j, :], bank[j], ACT.Copy, scale=1.0 / WS).then_inc(oc_, 1)

        @block.vector
        def _(eng):
            prime(eng, (mx_, rc_, lo_, al_))
            eng.wait_ge(primed, 4)
            with eng.Fori(0, NB_) as b:
                def unscale(kind, j, jj, lojj):
                    eng.wait_ge(jm_, b * JOBS + jj)
                    eng.wait_ge(jl_, b * JOBS + lojj)
                    if kind == "v":
                        eng.scalar_tensor_tensor(tmp[:, j, :].rearrange("p (t n) -> p t n", n=P),
                                                 bank[j].rearrange("p (t n) -> p t n", n=P), 1.0 / WS,
                                                 bv[:, :].unsqueeze(1).to_broadcast([P, 4, P]), ALU.mult, ALU.add).then_inc(jt_, 1)
                    else:
                        eng.scalar_tensor_tensor(tmp[:, j, :], bank[j], SC / WS, pe_sb[:, (j % 2) * 512:(j % 2 + 1) * 512],
                                                 ALU.mult, ALU.add).then_inc(jt_, 1)

                def rest(kind, j, jj, h):
                    eng.wait_ge(jh_, b * JOBS + jj)
                    if kind == "v":
                        sl = slice(4 * (j % 2), 4 * (j % 2) + 4)
                        eng.tensor_tensor(vp[:, 1, sl, :], tmp[:, j, :].rearrange("p (t n) -> p t n", n=P), vp[:, 0, sl, :],
                                          ALU.subtract).then_inc(jl_, 1)
                    elif kind == "k":
                        eng.scalar_tensor_tensor(kp[:, 1, j * 512:(j + 1) * 512], tmp[:, j, :], bias[:, B_K:B_K + 1],
                                                 kp[:, 0, j * 512:(j + 1) * 512], ALU.add, ALU.subtract).then_inc(jl_, 1)
                    else:
                        eng.scalar_tensor_tensor(qp[:, ds(h * T + (qoff + (j % 2) * 512), 512)], tmp[:, j, :],
                                                 bias[:, ds(h + B_Q, 1)], qp[:, ds(h * T + (j % 2) * 512, 512)],
                                                 ALU.add, ALU.subtract).then_inc(jl_, 1)

                eng.wait_ge(od_, b * 16)
                for j in range(4):
                    unscale("kkvv"[j], j, j + 1, 0)
                    if j:
                        rest("kkvv"[j - 1], j - 1, j, None)
                rest("v", 3, 4, None)
                with eng.Fori(0, HEADS // 2) as hh:
                    for j in range(4):
                        unscale("q", j, hh * 4 + (4 + j + 1), hh * 4 + (j + 1))
                        if j:
                            rest("q", j - 1, hh * 4 + (4 + j), hh * 2 + (j - 1) // 2)
                    rest("q", 3, hh * 4 + 8, hh * 2 + 1)

                def maxi(h, p):
                    n = (ORDER[p] + 1) * P
                    eng.wait_ge(sc_, b * 64 + h * 8 + (p + 1 + PRIME))
                    eng.tensor_reduce(nmax[:, p % 4:p % 4 + 1], psS[p % 2][:, :, :].rearrange("p a n -> p (a n)")[:, 0:n],
                                      AX.X, ALU.max, negate=True).then_inc(mx_, 1)

                def rec(h, p):
                    eng.wait_ge(ex_, b * 64 + h * 8 + (p + 1 + PRIME))
                    eng.wait_ge(nm_, b * 64 + h * 8 + (p - 3 + PRIME))
                    eng.reciprocal(rrec[:, p % 4:p % 4 + 1], rsum[:, p % 4:p % 4 + 1]).then_inc(rc_, 1)

                def los(h, p):
                    g, qi = ORDER[p] // 4, ORDER[p] % 4
                    for k in range(CHUNKS[p]):
                        c = CUM[p] + k
                        n = min(4, ORDER[p] + 1 - 4 * k)
                        eng.wait_ge(hi_, b * 8 * CH + h * CH + (c + 1 + PRIME))
                        o = pT[g][:, :, 4 * k:4 * k + n, qi * P:(qi + 1) * P]
                        eng.tensor_tensor(o[:, 1], psP[c % 3][:, 0:n, :], o[:, 0], ALU.subtract).then_inc(lo_, 1)

                def outs(h, g):
                    eng.wait_ge(ah_, b * 16 + h * 2 + (g + 1 + PRIME))
                    eng.tensor_tensor(qp[:, ds(h * T + (qoff + g * 512), 512)], psO[g][:, :], qp[:, ds(h * T + g * 512, 512)],
                                      ALU.subtract).then_inc(al_, 1)

                def head(h, first, last):
                    for p in range(8):
                        rec(h, p)
                        if p > 1 or not first:
                            los(*at(h, p - 2))
                        if p < 6 or not last:
                            maxi(*at(h, p + 2))
                        if p in (2, 3) and not first:
                            outs(h - 1, p - 2)

                maxi(0, 0)
                maxi(0, 1)
                head(0, True, False)
                with eng.Fori(1, HEADS - 1) as h:
                    head(h, False, False)
                head(HEADS - 1, False, True)
                los(HEADS - 1, 6)
                los(HEADS - 1, 7)
                outs(HEADS - 1, 0)
                outs(HEADS - 1, 1)
            for n in range(LATE):
                e = EARLY + n
                eng.wait_ge(l_l[n % 2], 16 * (n // 2 + 1))
                if n == LATE_TMP:
                    eng.wait_ge(od_, NB_ * 16)
                    eng.wait_ge(za_, 16)
                    eng.wait_ge(fr_, FREE * 16)
                w = w2_p[:, 2 * e * W2:2 * (e + 1) * W2].rearrange("p (m a w) -> p a m w", a=2, w=WC)
                src = w2st[n % 2].rearrange("p (m w) -> p m w", w=WC)
                eng.tensor_scalar(w[:, 0], src, WS, None, ALU.mult).then_inc(l_h, 1)
                eng.wait_ge(l_h, n + 1)
                eng.scalar_tensor_tensor(w[:, 1], src, WS, w[:, 0], ALU.mult, ALU.subtract).then_inc(l_o, 1)

        def split_piece(eng, wait, buf, done, hi, lo, n):
            wait(w_l[buf], done * 16 + 16)
            eng.tensor_scalar(wst[buf][:, :], wst[buf][:, :], WS, 1.0, ALU.mult, ALU.mult).then_inc(w_c, 1)
            wait(w_c, n * 2 + 1)
            eng.tensor_copy(hi, wst[buf][:, :]).then_inc(w_c, 1)
            wait(w_c, n * 2 + 2)
            eng.tensor_tensor(lo, wst[buf][:, :], hi, ALU.subtract).then_inc(w_u[buf], 1)

        @block.gpsimd
        def _(eng):
            def wait(sem, value):
                eng.wait_ge(sem, value)
                eng.sem_inc(waited, 1)

            prime(eng, (nm_,))
            eng.memset(zrow[:, :, :], 0).then_inc(z_, 1)
            wait(z_, 1)
            for t in range(2):
                eng.iota(zrow[:, t, D:D + 1], [[1, 1]], base=N + t * P, channel_multiplier=1).then_inc(zi_, 1)
            wait(zi_, 2)
            for k in range(FREE):
                eng.indirect_dma_start(rows_d, bass.IndirectOffsetOnAxis(ap=free[:, k:k + 1], axis=0),
                                       zrow[:, k % 2, :], None).then_inc(fr_, 16)
            wait(primed, 4)
            with eng.Fori(0, NB_) as b:
                for k in range(PIECES):
                    buf = k % 2
                    m = b * PIECES + k
                    split_piece(eng, wait, buf, b * USES[buf] + k // 2, w2_p[:, ds(m * (2 * WC), WC)],
                                w2_p[:, ds(m * (2 * WC) + WC, WC)], b * (PIECES + HEADS) + k)
                with eng.Fori(0, HEADS // 2) as hh:
                    for par in range(2):
                        U = b * 64 + hh * 16 + par * 8
                        n = b * HEADS + hh * 2 + par
                        m = b * (HEADS // 2) + hh
                        for p in range(8):
                            w = (ORDER[p] + 1) * P
                            wait(rc_, U + (p + 1 + PRIME))
                            eng.tensor_scalar(pr[p % 4][:, 0:w], pr[p % 4][:, 0:w], rrec[:, p % 4:p % 4 + 1], 1.0,
                                              ALU.mult, ALU.mult).then_inc(nm_, 1)
                            if p == 0:
                                wait(r_s, m * 64 + par * 32)
                                for s in range(2):
                                    eng.tensor_copy(rowb[s][:, D:D + 1], tok[:, ds(n, 1)]).then_inc(r_c, 1)
                                    eng.tensor_copy(rowb[s][:, D + 1:D + 2].bitcast(F32), gate[:, s, ds(n, 1)]).then_inc(r_c, 1)
                                    eng.tensor_copy(idx[s][:, :], pos[:, s, ds(n, 1)]).then_inc(r_c, 1)
                            if p in (2, 4):
                                s = p // 2 - 1
                                wait(r_c, n * 6 + 6)
                                wait(r_l[s], n * 16 + 16)
                                eng.indirect_dma_start(rows_d, bass.IndirectOffsetOnAxis(ap=idx[s][:, 0:1], axis=0),
                                                       rowb[s][:, :], None).then_inc(r_s, 16)
                            if p == 6:
                                split_piece(eng, wait, par, b * USES[par] + hh + (PIECES + 1 - par) // 2, w1_p[:, ds(n * WC, WC)],
                                            w1_p[:, ds(n * WC + E * W1, WC)], b * (PIECES + HEADS) + hh * 2 + (PIECES + par))
            wait(r_s, NT * 32)
            wait(fr_, FREE * 16)

        @block.sync
        def _(eng):
            w1v = w1.rearrange("e (c p) n -> (e c) p n", p=P)
            w2v = w2.rearrange("e (g p) d -> e p g d", p=P)
            w2f = w2.rearrange("e (m g p) d -> (e m) p g d", p=P, g=WC // D)
            eng.wait_ge(zi_, 2)
            eng.dma_start(acc_v, zrow[:, 0, 0:D].bitcast(F32).unsqueeze(1).to_broadcast([P, acc_v.shape[1], D])).then_inc(za_, 16)

            def batch(b, last):
                for k in range(PIECES):
                    buf = k % 2
                    eng.wait_ge(w_u[buf], b * USES[buf] + k // 2)
                    eng.dma_start(wst[buf][:, :].rearrange("p (g d) -> p g d", d=D),
                                  w2f[ds(b * PIECES + k, 1)].squeeze(0)).then_inc(w_l[buf], 16)
                with eng.Fori(0, HEADS // 2) as hh:
                    for par in range(2):
                        n = b * HEADS + hh * 2 + par
                        m = b * (HEADS // 2) + hh
                        eng.wait_ge(r_s, m * 64 + par * 32)
                        for s in range(2):
                            eng.dma_start(rowb[s][:, 0:D].bitcast(F16), xp_v[:, ds(n, 1), :].squeeze(1)).then_inc(r_l[s], 16)
                        eng.wait_ge(w_u[par], b * USES[par] + hh + (PIECES + 1 - par) // 2)
                        eng.dma_start(wst[par][:, :], w1v[:, :, par * WC:(par + 1) * WC][ds(m, 1)].squeeze(0)).then_inc(w_l[par], 16)
                if not last:
                    eng.wait_ge(jm_, b * JOBS + JOBS)
                    eng.dma_start(xTb[:, :, :], xT_d[:, :, ds(b * T + T, T)]).then_inc(xl_, 16)
                else:
                    eng.wait_ge(jm_, b * JOBS + JOBS)
                    for n in range(2):
                        eng.dma_start(w2st[n].rearrange("p (g d) -> p g d", d=D), w2v[EARLY + n]).then_inc(l_l[n], 16)
                eng.wait_ge(oc_, b * 4 + 4)
                eng.dma_start(s_v[:, ds(b * QT, QT), :], tmp[:, :, :].rearrange("p j (i d) -> p (j i) d", d=D)).then_inc(od_, 16)

            with eng.Fori(0, NB_ - 1) as b:
                batch(b, False)
            batch(NB_ - 1, True)
            for n in range(2, LATE):
                eng.wait_ge(l_o, n - 1)
                eng.dma_start(w2st[n % 2].rearrange("p (g d) -> p g d", d=D), w2v[EARLY + n]).then_inc(l_l[n % 2], 16)
            eng.wait_ge(od_, NB_ * 16)
            eng.wait_ge(za_, 16)


def experts(nc, v):
    N, D, DC, E, H, HT, NT, NBLK, ROW = (v[k] for k in ("N", "D", "DC", "E", "H", "HT", "NT", "NBLK", "ROW"))
    blk_e, bias, id16, w1_p, w2_p, b2, rows_v, acc_d, W1, W2 = (v[k] for k in (
        "blk_e", "bias", "id16", "w1_p", "w2_p", "b2", "rows_v", "acc_d", "W1", "W2"))
    R = 3
    UPS = HT // 2
    with ExitStack() as ctx:
        pb, sem = v["tensors"](ctx)
        arena = Arena(nc, v["rest_at"])
        sb = arena.take
        b2b = sb("b2b", [P, E * D], F32)
        rowx = [sb(f"rowx{i}", [P, 2, D], I32) for i in range(R)]
        tag = [sb(f"tag{i}", [P, 2, ROW - D], I32) for i in range(R)]
        bxT = [sb(f"bxT{i}", [P, 2 * DC, BLK], F16) for i in range(R)]
        h32 = [sb(f"h32_{i}", [P, 2, BLK], F32) for i in range(UPS)]
        hp = [sb(f"hp{i}", [P, 2, HT, BLK], F16) for i in range(R)]
        y = [sb(f"y{i}", [P, 2, D], F32) for i in range(R)]
        psX = pb("psX", [P, 2 * DC, BLK], F16)
        psU = [pb(f"psU{i}", [P, 2, BLK], F32) for i in range(UPS)]
        psY = [pb(f"psY{i}", [P, 2, D], F32) for i in range(R)]
        b_l = sem("b_l")
        ld = [sem(f"ld{i}") for i in range(R)]
        lt = [sem(f"lt{i}") for i in range(R)]
        (xt_, xc_, up_, rl_, hh_, hl_, dn_, yb_, yg_, sc_) = map(sem, (
            "e_xt", "e_xc", "e_up", "e_relu", "e_hi", "e_lo", "e_down", "e_yb", "e_yg", "e_add"))
        primed, waited = sem("e_primed"), sem("e_waited")
        PR = 16

        def prime(eng, sems):
            for s in sems:
                eng.sem_inc(s, PR)
            eng.sem_inc(primed, 1)

        ctx2 = ctx.enter_context(ExitStack())
        block = ctx2.enter_context(nc.Block())

        @block.sync
        def _(eng):
            eng.dma_start(b2b[:, :], b2.rearrange("e d -> (e d)").partition_broadcast(P)).then_inc(b_l, 16)
            eng.wait_ge(primed, 4)

            def load(m, j):
                eng.wait_ge(xt_, m * R + (j - 2 + PR))
                eng.sem_inc(waited, 1)
                eng.dma_start(rowx[j][:, :, :], rows_v[:, ds(m * R * 2 + 2 * j, 2), 0:D]).then_inc(ld[j], 16)

            def tags(m, j):
                if not (isinstance(m, int) and m * R + j < R):
                    eng.wait_ge(sc_, m * R * 32 + (j - 2) * 32)
                    eng.sem_inc(waited, 1)
                eng.dma_start(tag[j % R][:, :, :], rows_v[:, ds(m * R * 2 + 2 * j, 2), D:ROW]).then_inc(lt[j % R], 16)

            for j in range(R):
                load(0, j)
                if j:
                    tags(0, j - 1)
            with eng.Fori(1, NBLK // R) as m:
                for j in range(R):
                    load(m, j)
                    tags(m, j - 1)
            tags(NBLK // R - 1, R - 1)

        @block.tensor
        def _(eng):
            prime(eng, (xt_, up_, dn_))
            eng.wait_ge(primed, 4)

            def expert(m, j):
                return eng.value_load(blk_e[0:1, ds(m * R + j, 1)], min_val=0, max_val=E - 1)

            def turn(m, j):
                eng.wait_ge(ld[j % R], m * 16 + 16 * (j // R + 1))
                eng.wait_ge(xc_, m * R + (j + PR))
                for t in range(2):
                    for h in range(2):
                        for c in range(DC):
                            mm = eng.transpose(psX[:, 2 * h + c, t * P:(t + 1) * P],
                                               rowx[j % R][:, t, :].bitcast(F16)[:, h * D + c * P:h * D + (c + 1) * P], id16[:, :])
                mm.then_inc(xt_, 1)

            def up(m, j):
                e = expert(m, j)
                eng.wait_ge(xc_, m * R + (j + 1 + PR))
                for u in range(UPS):
                    eng.wait_ge(rl_, m * R * UPS + ((j - 1) * UPS + u + 1 + PR))
                    for g in range(2):
                        n = 0
                        for a, b in PASSES:
                            for c in range(DC):
                                mm = eng.matmul(psU[u][:, g, :], w1_p[:, ds(e * W1 + (a * E * W1 + c * H + (2 * u + g) * P), P)],
                                                bxT[j][:, 2 * b + c, :], start=(n == 0), stop=(n == 3 * DC - 1))
                                n += 1
                    mm.then_inc(up_, 1)

            def down(m, j):
                e = expert(m, j)
                eng.wait_ge(hl_, m * R * UPS + ((j + 1) * UPS + PR))
                eng.wait_ge(yb_, m * R * 2 + ((j - 2) * 2 + PR))
                for t in range(2):
                    n = 0
                    for g in range(HT):
                        for a, b in PASSES:
                            mm = eng.matmul(psY[j % R][:, t, :], hp[j % R][:, a, g, t * P:(t + 1) * P],
                                            w2_p[:, ds(e * (2 * W2) + ((g // 2 * 2 + b) * (2 * D) + g % 2 * D), D)],
                                            start=(n == 0), stop=(n == 3 * HT - 1))
                            n += 1
                mm.then_inc(dn_, 1)

            def blocks(m, first, last):
                for j in range(R):
                    up(m, j)
                    if not (last and j == R - 1):
                        turn(m, j + 1)
                    if not (first and j == 0):
                        down(m, j - 1)

            turn(0, 0)
            blocks(0, True, False)
            with eng.Fori(1, NBLK // R - 1) as m:
                blocks(m, False, False)
            blocks(NBLK // R - 1, False, True)
            down(NBLK // R - 1, R - 1)

        @block.scalar
        def _(eng):
            prime(eng, (xc_, rl_))
            eng.wait_ge(primed, 4)
            with eng.Fori(0, NBLK // R) as m:
                for j in range(R):
                    e = eng.value_load(blk_e[0:1, ds(m * R + j, 1)], min_val=0, max_val=E - 1)
                    eng.wait_ge(xt_, m * R + (j + 1 + PR))
                    eng.wait_ge(up_, m * R * UPS + ((j - 2) * UPS + PR))
                    eng.activation(bxT[j][:, :, :], psX[:, :, :], ACT.Copy).then_inc(xc_, 1)
                    for u in range(UPS):
                        eng.wait_ge(up_, m * R * UPS + (j * UPS + u + 1 + PR))
                        eng.wait_ge(hl_, m * R * UPS + ((j - 1) * UPS + u + 1 + PR))
                        for g in range(2):
                            a = eng.activation(h32[u][:, g, :], psU[u][:, g, :], ACT.Relu,
                                               bias=bias[:, ds(e * HT + (2 * u + g), 1)], scale=1.0 / WS)
                        a.then_inc(rl_, 1)

        @block.vector
        def _(eng):
            prime(eng, (hh_, hl_, yb_))
            eng.wait_ge(primed, 4)
            eng.wait_ge(b_l, 16)

            def hidden(m, j):
                def hi(u):
                    eng.wait_ge(rl_, m * R * UPS + (j * UPS + u + 1 + PR))
                    if u == 0:
                        eng.wait_ge(dn_, m * R + (j - 2 + PR))
                    eng.tensor_copy(hp[j][:, 0, 2 * u:2 * u + 2, :], h32[u][:, :, :]).then_inc(hh_, 1)

                def lo(u):
                    eng.wait_ge(hh_, m * R * UPS + (j * UPS + u + 1 + PR))
                    eng.tensor_tensor(hp[j][:, 1, 2 * u:2 * u + 2, :], h32[u][:, :, :], hp[j][:, 0, 2 * u:2 * u + 2, :],
                                      ALU.subtract).then_inc(hl_, 1)
                for u in range(UPS):
                    hi(u)
                    if u:
                        lo(u - 1)
                lo(UPS - 1)

            def rows(m, j):
                e = eng.value_load(blk_e[0:1, ds(m * R + j, 1)], min_val=0, max_val=E - 1)
                eng.wait_ge(dn_, m * R + (j + 1 + PR))
                if not isinstance(m, int) or m * R + j > 2:
                    eng.wait_ge(sc_, m * R * 32 + (j - 2) * 32)
                for t in range(2):
                    eng.scalar_tensor_tensor(y[j % R][:, t, :], psY[j % R][:, t, :], 1.0 / WS, b2b[:, ds(e * D, D)],
                                             ALU.mult, ALU.add).then_inc(yb_, 1)

            for j in range(R):
                hidden(0, j)
                if j:
                    rows(0, j - 1)
            with eng.Fori(1, NBLK // R) as m:
                for j in range(R):
                    hidden(m, j)
                    rows(m, j - 1)
            rows(NBLK // R - 1, R - 1)

        @block.gpsimd
        def _(eng):
            def wait(sem, value):
                eng.wait_ge(sem, value)
                eng.sem_inc(waited, 1)

            prime(eng, (yg_,))
            wait(primed, 4)
            with eng.Fori(0, NBLK // R) as m:
                for j in range(R):
                    wait(yb_, m * R * 2 + (2 * j + 2 + PR))
                    wait(lt[j], m * 16 + 16)
                    for t in range(2):
                        eng.tensor_scalar(y[j][:, t, :], y[j][:, t, :], tag[j][:, t, 1:2].bitcast(F32), 1.0,
                                          ALU.mult, ALU.mult).then_inc(yg_, 1)
                    wait(yg_, m * R * 2 + (2 * j + 2 + PR))
                    wait(sc_, m * R * 32 + j * 32)
                    for t in range(2):
                        eng.indirect_dma_start(acc_d, bass.IndirectOffsetOnAxis(ap=tag[j][:, t, 0:1].bitcast(U32), axis=0),
                                               y[j][:, t, :], None, compute_op=ALU.add).then_inc(sc_, 16)
            wait(sc_, NBLK * 32)

    xf, of, s_v, acc_v = (v[k] for k in ("xf", "of", "s_v", "acc_v"))
    G, B = 2, 4
    STEPS = NT // G
    with ExitStack() as ctx:
        pb, sem = v["tensors"](ctx)
        sb = Arena(nc, v["rest_at"]).take
        fb = [sb(f"fb{i}", [P, G, D], F32) for i in range(B)]
        gb = [sb(f"gb{i}", [P, G, D], F32) for i in range(B)]
        sbf = [sb(f"sbf{i}", [P, G, D], F32) for i in range(B)]
        xb = [sb(f"xb{i}", [P, G, D], F32) for i in range(B)]
        f_l = [sem(f"f_ld{i}") for i in range(B)]
        f_o = [sem(f"f_out{i}") for i in range(B)]
        f_g, f_m, f_a, f_w = sem("f_silu"), sem("f_mul"), sem("f_add"), sem("f_waited")
        block = ctx.enter_context(nc.Block())

        @block.sync
        def _(eng):
            with eng.Fori(0, STEPS // B) as m:
                for j in range(B):
                    eng.wait_ge(f_o[j], m * 16)
                    for dst, src in ((fb, acc_v), (sbf, s_v), (xb, xf)):
                        eng.dma_start(dst[j][:, :, :], src[:, ds(m * B * G + j * G, G), :]).then_inc(f_l[j], 16)

        @block.scalar
        def _(eng):
            with eng.Fori(0, STEPS // B) as m:
                for j in range(B):
                    eng.wait_ge(f_l[j], m * 48 + 48)
                    eng.activation(gb[j][:, :, :], fb[j][:, :, :], ACT.Silu).then_inc(f_g, 1)

        @block.vector
        def _(eng):
            with eng.Fori(0, STEPS // B) as m:
                for j in range(B):
                    eng.wait_ge(f_g, m * B + (j + 1))
                    eng.tensor_tensor(gb[j][:, :, :], gb[j][:, :, :], sbf[j][:, :, :], ALU.mult).then_inc(f_m, 1)
                    eng.wait_ge(f_m, m * B + (j + 1))
                    eng.tensor_tensor(xb[j][:, :, :], gb[j][:, :, :], xb[j][:, :, :], ALU.add).then_inc(f_a, 1)

        @block.gpsimd
        def _(eng):
            with eng.Fori(0, STEPS // B) as m:
                for j in range(B):
                    eng.wait_ge(f_a, m * B + (j + 1))
                    eng.sem_inc(f_w, 1)
                    eng.dma_start(of[:, ds(m * B * G + j * G, G), :], xb[j][:, :, :]).then_inc(f_o[j], 16)
            for j in range(B):
                eng.wait_ge(f_o[j], STEPS // B * 16)


_INS = ["L0_attn_x", "L0_attn_Wq", "L0_attn_bq", "L0_attn_Wkv", "L0_attn_bkv", "L0_attn_Wo", "L0_ffn_router_w",
        "L0_ffn_router_b", "L0_ffn_w1", "L0_ffn_b1", "L0_ffn_w2", "L0_ffn_b2"]


def kernel(**inputs):
    import concourse.bacc as _bacc
    from concourse.bass_utils import run_bass_kernel_spmd as _run

    nc = _bacc.Bacc("TRN2", target_bir_lowering=False, num_devices=1)
    arrays, args = {}, []

    def given(name, a):
        arrays[name] = a
        args.append(nc.dram_tensor(name, a.shape, mybir.dt.from_np(a.dtype), kind="ExternalInput").ap())

    for name in _INS:
        given(f"in_{name}", np.ascontiguousarray(inputs[name]))
    shape = tuple(inputs["L0_attn_x"].shape)
    for name, a in zip(("tables", "positions"), constants(shape[0] * shape[1], inputs["L0_ffn_w1"].shape[0], shape[1])):
        given(name, a)
    args.append(nc.dram_tensor("out", shape, F32, kind="ExternalOutput").ap())
    build(nc, *args)
    r = _run(nc, [arrays], core_ids=[0])
    return r.results[0]["out"]
```

```python
from contextlib import ExitStack

import numpy as np
import concourse.bass as bass
from concourse import mybir

F32, F16, BF16, I32, U32 = (mybir.dt.float32, mybir.dt.float16, mybir.dt.bfloat16, mybir.dt.int32,
                            mybir.dt.uint32)
ALU, ACT, AX = mybir.AluOpType, mybir.ActivationFunctionType, mybir.AxisListType
ds = bass.ds

P = 128
WS = 64.0
EPS = 1e-5
MASKED = -3.0e38
FAR = -3.0e38
HEADS, HD = 8, 128
BLK = 256
PASSES = ((0, 0), (0, 1), (1, 0))
C_ID, C_MASK, C_UP, C_E = 0, P, 2 * P, 3 * P


def constants(tokens, experts, seq):
    most = tokens // BLK
    blocks = 2 * tokens // BLK + experts - 1
    q, k = np.arange(P)[:, None], np.arange(P)[None, :]
    c = np.concatenate([
        (q == k), np.where(k > q, MASKED, 0.0), (q < k),
        np.broadcast_to(np.arange(experts), (P, experts)),
        np.broadcast_to(np.arange(most) * BLK, (P, most)),
        np.broadcast_to(np.arange(blocks), (P, blocks)),
        np.arange(blocks * BLK // P - 2 * tokens // P)[None, :] * P + q], axis=1).astype(np.float32)
    pos = np.arange(seq, dtype=np.float32)[:, None]
    inv = np.exp(np.float32(-np.log(10000.0)) * np.arange(0, HD, 2, dtype=np.float32) / np.float32(HD))
    ang = (pos * inv.astype(np.float32)[None, :]).astype(np.float32)
    pe = np.zeros((seq, HD), np.float32)
    pe[:, 0::2], pe[:, 1::2] = np.sin(ang), np.cos(ang)
    return c, np.ascontiguousarray((pe * np.float32(HD ** -0.25)).T.astype(np.float32))


class Arena:

    def __init__(self, nc, at):
        self.nc, self.at = nc, -(-at // 64) * 64

    def take(self, name, shape, dt):
        size = mybir.dt.size(dt)
        for n in shape[1:]:
            size *= n
        assert self.at + size <= self.nc.sbuf_usable_end, (name, self.at, size)
        t = self.nc.alloc_sbuf_tensor_at(name, shape, dt, offset=self.at)
        self.at += -(-size // 64) * 64
        return t


def build(nc, x, wq, bq, wkv, bkv, wo, rw, rb, w1, b1, w2, b2, cst, pe, out):
    NB_, T, D = x.shape
    N = NB_ * T
    NT = N // P
    E, _, H = w1.shape
    DC, HT = D // P, H // P
    QT = T // P
    MOST = N // BLK
    NBLK = 2 * N // BLK + E - 1
    FREE = NBLK * BLK // P - 2 * NT
    C_TH, C_BL, C_FR = C_E + E, C_E + E + MOST, C_E + E + MOST + NBLK
    CW = C_FR + FREE
    SC = float(HD) ** -0.25
    ROW = D + 2
    SLOTS = NBLK * BLK
    EARLY = 4
    W1, W2 = DC * H, HT * D
    assert D == 256 and HD == P and T == 1024 and H == 1024 and E == 8 and NBLK % 3 == 0

    xf = x.rearrange("b t d -> (b t) d").rearrange("(n p) d -> p n d", p=P)
    of = out.rearrange("b t d -> (b t) d").rearrange("(n p) d -> p n d", p=P)
    xp_d = nc.dram_tensor("xn_split", (N, 2 * D), F16, kind="Internal").ap()
    s_d = nc.dram_tensor("attention", (N, D), F32, kind="Internal").ap()
    rows_d = nc.dram_tensor("expert_rows", (SLOTS, ROW), I32, kind="Internal").ap()
    acc_d = nc.dram_tensor("mixture", (N + BLK, D), F32, kind="Internal").ap()
    xp_v = xp_d.rearrange("(n p) d -> p n d", p=P)
    s_v = s_d.rearrange("(n p) d -> p n d", p=P)
    acc_v = acc_d.rearrange("(n p) d -> p n d", p=P)
    rows_v = rows_d.rearrange("(k p) c -> p k c", p=P)
    xT_d = nc.dram_tensor("xn_transposed", (P, 2 * DC, N), F16, kind="Internal").ap()

    def tensors(ctx):
        def pb(name, shape, dt):
            return ctx.enter_context(nc.psum_tensor(name, shape, dt))

        def sem(name):
            return ctx.enter_context(nc.semaphore(name))
        return pb, sem

    kept = Arena(nc, nc.sbuf_base)
    pos = kept.take("pos", [P, 2, NT], U32)
    free = kept.take("free", [P, FREE], U32)
    gate = kept.take("gate", [P, 2, NT], F32)
    tok = kept.take("tok", [P, NT], I32)
    blk_e = kept.take("blk_e", [P, NBLK], I32)
    bias = kept.take("bias", [P, E * HT + HEADS + 2], F32)
    B_Q, B_K = E * HT, E * HT + HEADS
    id16 = kept.take("id16", [P, P], F16)
    w1_p = kept.take("w1_p", [P, 2 * E * W1], F16)
    w2_at = kept.at
    w2_p = kept.take("w2_p", [P, 2 * E * W2], F16)
    rest_at = kept.at

    area = Arena(nc, rest_at)
    pe_sb = area.take("pe_sb", [P, T], F32)
    bv = area.take("bv", [P, HD], F32)
    wkv_p = area.take("wkv_p", [P, 2, DC, 2 * HD], F16)
    used_up = area.at
    id32 = area.take("id32", [P, P], F32)
    idb = area.take("idb", [P, P], BF16)
    maskb = area.take("maskb", [P, P], BF16)
    wq_p = area.take("wq_p", [P, 2 * DC * HEADS * HD], F16)
    wo_p = area.take("wo_p", [P, 2, HEADS, D], F16)
    xTb = area.take("xTb", [P, 2 * DC, T], F16)
    attn_at = area.at

    R = 3
    ahead_of = Arena(nc, rest_at)
    rowx = [ahead_of.take(f"rowx{i}", [P, 2, D], I32) for i in range(R)]
    tag = [ahead_of.take(f"tag{i}", [P, 2, ROW - D], I32) for i in range(R)]
    experts_at = ahead_of.at
    assert experts_at <= used_up
    whole = ExitStack()
    ld = [whole.enter_context(nc.semaphore(f"ld{i}")) for i in range(R)]
    lt = [whole.enter_context(nc.semaphore(f"lt{i}")) for i in range(R)]
    od_ = [whole.enter_context(nc.semaphore(f"o_dma{j}")) for j in range(4)]

    with ExitStack() as ctx:
        pb, sem = tensors(ctx)
        x_sb = w1_p[:, 0:2 * NT * D].bitcast(F32).rearrange("p (n d) -> p n d", d=D)
        xp = w1_p[:, 2 * NT * D:4 * NT * D].rearrange("p (n h d) -> p n h d", h=2, d=D)
        low = Arena(nc, w2_at)
        xT = low.take("xT", [P, 2 * DC, N - T], F16)
        wst = low.take("wst", [P, 2048], F32)
        wst2 = low.take("wst2", [P, 2048], F32)
        kvst = low.take("kvst", [P, DC, 2 * HD], F32)
        high = Arena(nc, attn_at)
        sb = high.take
        c_sb = sb("c_sb", [P, CW], F32)
        up16 = sb("up16", [P, P], F16)
        one16 = sb("one16", [P, P], F16)
        brow = sb("brow", [E * HT + HEADS + 2, P], F32)
        rbb = sb("rbb", [P, E], F32)
        eps = sb("eps", [P, 1], F32)
        rw_s = sb("rw_s", [P, DC, E], F32)
        rw_p = sb("rw_p", [P, 2, DC, E], F16)
        st = sb("st", [P, NT, 6], F32)
        mv = sb("mv", [P, NT, 2], F32)
        rs = sb("rs", [P, 4, NT], F32)
        L = sb("L", [P, NT, E], F32)
        L2 = sb("L2", [P, NT, E], F32)
        cand = sb("cand", [P, NT, E], F32)
        oh = [sb(f"oh{i}", [P, NT, E], F32) for i in range(2)]
        M16 = sb("M16", [P, NT * E], F16)
        m_ = [sb(f"m{i}", [P, NT], F32) for i in range(2)]
        ix = [sb(f"ix{i}", [P, NT], F32) for i in range(2)]
        ex = sb("ex", [P, 3, NT], F32)
        sc = [sb(f"scan{i}", [P, NT, E], F32) for i in range(2)]
        tot = sb("tot", [P, NT, E], F32)
        se = [sb(f"scane{i}", [P, 2, E], F32) for i in range(2)]
        nbl = sb("nbl", [P, 2, E], F32)
        fre = sb("fre", [P, E], F32)
        frs = sb("frs", [P, FREE], F32)
        cmpb = sb("cmpb", [P, max(NBLK, MOST, FREE) * E], F32)
        bf = sb("bf", [P, NBLK], F32)
        psT = [pb(f"psT{i}", [P, 4, 2 * P], F16) for i in range(2)]
        psL = pb("psL", [P, NT * E], F32)
        psR = pb("psR", [P, 2, NT * E], F32)
        psB = pb("psB", [P, P], F32)
        s_x = [sem(f"x_loaded{i}") for i in range(4)]
        (s_c, s_w, s_cc, s_bn, s_var, s_sd, s_xn, s_xh, s_xl, s_z, s_one, s_tr, s_te, s_td, s_wh, s_wl, s_b, s_lg, s_ch,
         s_diff, s_pick, s_cnt, s_e, s_dr) = map(sem, (
             "tables", "weights", "tables_cast", "stats", "variance", "std", "xn", "xn_hi", "xn_lo", "zeroed", "ones",
             "transposed", "copied_act", "copied_dve", "w_hi", "w_lo", "bias_turned", "logits", "chain", "top_diff",
             "picked", "counted", "exp_diff", "stored"))
        block = ctx.enter_context(nc.Block())
        G4 = NT // 4

        def rowsT(job):
            t = job * 2 * P
            return xTb[:, :, t:t + 2 * P] if t < T else xT[:, :, t - T:t - T + 2 * P]

        @block.sync
        def _(eng):
            for g in range(4):
                eng.dma_start(x_sb[:, g * G4:(g + 1) * G4, :], xf[:, g * G4:(g + 1) * G4, :]).then_inc(s_x[g], 16)
            for g in range(4):
                eng.wait_ge(s_xl, g + 1)
                eng.dma_start(xp_v[:, g * G4:(g + 1) * G4, :],
                              xp[:, g * G4:(g + 1) * G4].rearrange("p n h d -> p n (h d)")).then_inc(s_dr, 16)
            eng.wait_ge(s_te, NT // 4)
            eng.wait_ge(s_td, NT // 4)
            eng.dma_start(xT_d[:, :, T:N], xT[:, :, :]).then_inc(s_dr, 16)
            eng.wait_ge(s_dr, 80)

        @block.gpsimd
        def _(eng):
            eng.memset(eps[:, :], EPS).then_inc(s_z, 1)
            eng.memset(one16[:, :], 1.0).then_inc(s_one, 1)
            eng.iota(tok[:, :], [[P, NT]], base=0, channel_multiplier=1)
            for g in range(4):
                eng.wait_ge(s_xh, g + 1)
                sl = slice(g * G4, (g + 1) * G4)
                eng.tensor_tensor(xp[:, sl, 1, :], x_sb[:, sl, :], xp[:, sl, 0, :], ALU.subtract).then_inc(s_xl, 1)

        @block.scalar
        def _(eng):
            for dst, src in ((c_sb[:, :], cst), (rw_s[:, :, :], rw.rearrange("(c p) e -> p c e", p=P)),
                             (rbb[:, :], rb.partition_broadcast(P)),
                             (brow[0:E * HT, :], b1.rearrange("e (h p) -> (e h) p", p=P)),
                             (brow[E * HT:E * HT + HEADS, :], bq.rearrange("(h p) -> h p", p=P)),
                             (brow[E * HT + HEADS:, :], bkv.rearrange("(h p) -> h p", p=P))):
                eng.dma_start(dst, src).then_inc(s_c, 16)
            for dst, src in ((wst[:, :].rearrange("p (c n) -> p c n", c=DC), wq.rearrange("(c p) n -> p c n", p=P)),
                             (kvst[:, :, :], wkv.rearrange("(c p) n -> p c n", p=P)),
                             (wst2[:, :].rearrange("p (h n) -> p h n", h=HEADS), wo.rearrange("(h p) n -> p h n", p=P)),
                             (bv[:, :], bkv[HD:2 * HD].partition_broadcast(P)),
                             (pe_sb[:, :], pe)):
                eng.dma_start(dst, src).then_inc(s_w, 16)
            eng.wait_ge(s_z, 1)

            def std(k, sl):
                eng.wait_ge(s_var, k)
                eng.activation(rs[:, 0, sl], mv[:, sl, 1], ACT.Sqrt, bias=eps[:, :]).then_inc(s_sd, 1)

            std(1, slice(0, G4))
            eng.wait_ge(s_c, 96)
            eng.activation(rw_p[:, 0], rw_s[:, :, :], ACT.Copy, scale=WS).then_inc(s_wh, 1)
            for dst, src in ((id32, C_ID), (id16, C_ID), (idb, C_ID), (maskb, C_MASK), (up16, C_UP)):
                eng.activation(dst[:, :], c_sb[:, src:src + P], ACT.Copy).then_inc(s_cc, 1)

            def his(g):
                sl = slice(g * G4, (g + 1) * G4)
                eng.wait_ge(s_xn, g + 1)
                eng.activation(xp[:, sl, 0, :], x_sb[:, sl, :], ACT.Copy).then_inc(s_xh, 1)

            def weights():
                eng.wait_ge(s_w, 80)
                eng.activation(wkv_p[:, 0], kvst[:, :, :], ACT.Copy, scale=WS).then_inc(s_wh, 1)
                eng.activation(wq_p[:, 0:2048], wst[:, :], ACT.Copy, scale=WS).then_inc(s_wh, 1)
                eng.activation(wo_p[:, 0], wst2[:, :].rearrange("p (h n) -> p h n", h=HEADS), ACT.Copy,
                               scale=WS).then_inc(s_wh, 1)

            def out_of_psum(g):
                for i in range(2 * g, 2 * g + 2):
                    eng.wait_ge(s_tr, 2 * i + 1)
                    eng.activation(rowsT(2 * i), psT[0][:, :, :], ACT.Copy).then_inc(s_te, 1)

            his(0)
            eng.wait_ge(s_b, 1)
            eng.activation(bias[:, 0:E * HT], psB[:, 0:E * HT], ACT.Copy)
            eng.activation(bias[:, E * HT:], psB[:, E * HT:E * HT + HEADS + 2], ACT.Copy, scale=SC)
            std(2, slice(G4, NT))
            his(1)
            out_of_psum(0)
            weights()
            his(2)
            out_of_psum(1)
            his(3)
            out_of_psum(2)
            out_of_psum(3)
            eng.wait_ge(s_diff, 1)
            eng.activation(ex[:, 0, :], ex[:, 2, :], ACT.Exp).then_inc(s_e, 1)

        @block.tensor
        def _(eng):
            eng.wait_ge(s_cc, 5)
            eng.transpose(psB[:, 0:E * HT + HEADS + 2], brow[:, :], id32[0:E * HT + HEADS + 2, 0:E * HT + HEADS + 2]).then_inc(s_b, 1)

            def turn(g):
                eng.wait_ge(s_xl, g + 1)
                for j in range(4):
                    q = j % 2
                    eng.wait_ge((s_te, s_td)[q], g * 2 + j // 2)
                    for t in range(2):
                        for h in range(2):
                            for c in range(DC):
                                mm = eng.transpose(psT[q][:, 2 * h + c, t * P:(t + 1) * P],
                                                   xp[:, g * G4 + 2 * j + t, h, c * P:(c + 1) * P], id16[:, :])
                    mm.then_inc(s_tr, 1)

            def logits(g):
                eng.wait_ge(s_te, g * 2 + 2)
                eng.wait_ge(s_td, g * 2 + 2)
                src, at = (xTb, 0) if g == 0 else (xT, (g - 1) * T)
                for t in range(G4):
                    k = 0
                    for a, b in PASSES:
                        for c in range(DC):
                            mm = eng.matmul(psL[:, (g * G4 + t) * E:(g * G4 + t + 1) * E],
                                            src[:, 2 * a + c, at + t * P:at + (t + 1) * P],
                                            rw_p[:, b, c, :], start=(k == 0), stop=(k == 3 * DC - 1))
                            k += 1
                mm.then_inc(s_lg, 1)

            turn(0)
            eng.wait_ge(s_wl, 1)
            for g in range(1, 4):
                turn(g)
                logits(g - 1)
            logits(3)
            eng.wait_ge(s_one, 1)
            eng.wait_ge(s_pick, 1)
            eng.matmul(psR[:, 0, :], up16[:, :], M16[:, :], start=True, stop=True)
            eng.matmul(psR[:, 1, :], one16[:, :], M16[:, :], start=True, stop=True).then_inc(s_cnt, 1)

        @block.vector
        def _(eng):
            n_ch = [0]

            def step(ins):
                n_ch[0] += 1
                ins.then_inc(s_ch, 1)

            def link(ins):
                step(ins)
                eng.wait_ge(s_ch, n_ch[0])

            def stats(g):
                eng.wait_ge(s_x[g], 16)
                for n in range(g * G4, (g + 1) * G4):
                    eng.bn_stats(st[:, n, :], x_sb[:, n, :]).then_inc(s_bn, 1)

            def variance(g, sl):
                eng.wait_ge(s_bn, g * G4)
                step(eng.tensor_tensor(mv[:, sl, 0], st[:, sl, 1], st[:, sl, 4], ALU.add))
                step(eng.tensor_tensor(rs[:, 1, sl], st[:, sl, 1], st[:, sl, 4], ALU.subtract))
                link(eng.tensor_tensor(rs[:, 2, sl], st[:, sl, 2], st[:, sl, 5], ALU.add))
                step(eng.tensor_scalar(mv[:, sl, 0], mv[:, sl, 0], 0.5, None, ALU.mult))
                link(eng.tensor_tensor(rs[:, 1, sl], rs[:, 1, sl], rs[:, 1, sl], ALU.mult))
                link(eng.tensor_scalar(rs[:, 1, sl], rs[:, 1, sl], 0.25, None, ALU.mult))
                eng.scalar_tensor_tensor(mv[:, sl, 1], rs[:, 2, sl], 1.0 / D, rs[:, 1, sl], ALU.mult, ALU.add).then_inc(s_var, 1)

            def rstd(k, sl):
                eng.wait_ge(s_sd, k)
                step(eng.tensor_scalar(rs[:, 1, sl], mv[:, sl, 1], EPS, None, ALU.add))
                link(eng.reciprocal(rs[:, 2, sl], rs[:, 0, sl]))
                link(eng.tensor_tensor(rs[:, 3, sl], rs[:, 2, sl], rs[:, 2, sl], ALU.mult))
                link(eng.tensor_tensor(rs[:, 3, sl], rs[:, 3, sl], rs[:, 1, sl], ALU.mult))
                link(eng.tensor_scalar(rs[:, 3, sl], rs[:, 3, sl], -0.5, 1.5, ALU.mult, ALU.add))
                link(eng.tensor_tensor(rs[:, 0, sl], rs[:, 2, sl], rs[:, 3, sl], ALU.mult))

            def normalise(g):
                for n in range(g * G4, (g + 1) * G4):
                    a = eng.tensor_scalar(x_sb[:, n, :], x_sb[:, n, :], mv[:, n, 0:1], rs[:, 0, n:n + 1], ALU.subtract, ALU.mult)
                a.then_inc(s_xn, 1)

            stats(0)
            variance(1, slice(0, G4))
            stats(1)
            rstd(1, slice(0, G4))
            normalise(0)
            stats(2)
            stats(3)
            variance(4, slice(G4, NT))
            rstd(2, slice(G4, NT))

            def out_of_psum(g):
                for i in range(2 * g, 2 * g + 2):
                    eng.wait_ge(s_tr, 2 * i + 2)
                    eng.tensor_copy(rowsT(2 * i + 1), psT[1][:, :, :]).then_inc(s_td, 1)

            normalise(1)
            eng.wait_ge(s_wh, 1)
            eng.scalar_tensor_tensor(rw_p[:, 1], rw_s[:, :, :], WS, rw_p[:, 0], ALU.mult, ALU.subtract).then_inc(s_wl, 1)
            out_of_psum(0)
            normalise(2)
            normalise(3)
            out_of_psum(1)
            eng.wait_ge(s_wh, 4)
            for dst, src, hi in ((wkv_p[:, 1], kvst[:, :, :], wkv_p[:, 0]),
                                 (wq_p[:, 2048:], wst[:, :], wq_p[:, 0:2048]),
                                 (wo_p[:, 1], wst2[:, :].rearrange("p (h n) -> p h n", h=HEADS), wo_p[:, 0])):
                eng.scalar_tensor_tensor(dst, src, WS, hi, ALU.mult, ALU.subtract).then_inc(s_wl, 1)
            out_of_psum(2)
            out_of_psum(3)

            ids = c_sb[:, C_E:C_E + E].unsqueeze(1).to_broadcast([P, NT, E])
            eng.wait_ge(s_c, 96)
            eng.wait_ge(s_lg, 4)

            def wide(a):
                return a.unsqueeze(2).to_broadcast([P, NT, E])

            link(eng.scalar_tensor_tensor(L[:, :, :], psL[:, :].rearrange("p (n e) -> p n e", e=E), 1.0 / WS,
                                          rbb[:, :].unsqueeze(1).to_broadcast([P, NT, E]), ALU.mult, ALU.add))
            src = L
            for i in range(2):
                link(eng.tensor_reduce(m_[i][:, :], src[:, :, :], AX.X, ALU.max))
                link(eng.tensor_tensor(cand[:, :, :], src[:, :, :], wide(m_[i][:, :]), ALU.is_lt))
                link(eng.scalar_tensor_tensor(cand[:, :, :], cand[:, :, :], float(E), ids, ALU.mult, ALU.add))
                link(eng.tensor_reduce(ix[i][:, :], cand[:, :, :], AX.X, ALU.min))
                link(eng.tensor_tensor(oh[i][:, :, :], ids, wide(ix[i][:, :]), ALU.is_equal))
                if i == 0:
                    link(eng.scalar_tensor_tensor(L2[:, :, :], oh[0][:, :, :], FAR, L[:, :, :], ALU.mult, ALU.add))
                    src = L2
            eng.tensor_tensor(M16[:, :].rearrange("p (n e) -> p n e", e=E), oh[0][:, :, :], oh[1][:, :, :],
                              ALU.add).then_inc(s_pick, 1)
            eng.tensor_tensor(ex[:, 2, :], m_[1][:, :], m_[0][:, :], ALU.subtract).then_inc(s_diff, 1)
            eng.wait_ge(s_e, 1)
            link(eng.tensor_scalar(ex[:, 1, :], ex[:, 0, :], 1.0, None, ALU.add))
            link(eng.reciprocal(gate[:, 0, :], ex[:, 1, :]))
            step(eng.tensor_tensor(gate[:, 1, :], ex[:, 0, :], gate[:, 0, :], ALU.mult))
            eng.wait_ge(s_cnt, 1)
            step(eng.tensor_copy(tot[:, :, :], psR[:, 1, :].rearrange("p (n e) -> p n e", e=E)))
            link(eng.tensor_copy(sc[0][:, :, :], psR[:, 1, :].rearrange("p (n e) -> p n e", e=E)))
            cur, by = 0, 1
            while by < NT:
                a, b = sc[cur], sc[1 - cur]
                step(eng.tensor_copy(b[:, 0:by, :], a[:, 0:by, :]))
                link(eng.tensor_tensor(b[:, by:, :], a[:, by:, :], a[:, 0:NT - by, :], ALU.add))
                cur, by = 1 - cur, 2 * by
            cnt = sc[cur][:, NT - 1, :]
            cm = cmpb[:, 0:MOST * E].rearrange("p (e k) -> p e k", e=E)
            step(eng.tensor_copy(nbl[:, 1, :], cnt))
            link(eng.tensor_tensor(cm, c_sb[:, C_TH:C_TH + MOST].unsqueeze(1).to_broadcast([P, E, MOST]),
                                   cnt.unsqueeze(2).to_broadcast([P, E, MOST]), ALU.is_lt))
            link(eng.tensor_reduce(nbl[:, 0, :], cm, AX.X, ALU.add))
            link(eng.tensor_copy(se[0][:, :, :], nbl[:, :, :]))
            ce, by = 0, 1
            while by < E:
                a, b = se[ce], se[1 - ce]
                step(eng.tensor_copy(b[:, :, 0:by], a[:, :, 0:by]))
                link(eng.tensor_tensor(b[:, :, by:], a[:, :, by:], a[:, :, 0:E - by], ALU.add))
                ce, by = 1 - ce, 2 * by
            ends = se[ce][:, 0, :]
            first = se[1 - ce]
            link(eng.tensor_tensor(first[:, :, :], se[ce][:, :, :], nbl[:, :, :], ALU.subtract))
            rank = sc[1 - cur]
            link(eng.tensor_tensor(rank[:, :, :], sc[cur][:, :, :], tot[:, :, :], ALU.subtract))
            link(eng.tensor_tensor(rank[:, :, :], rank[:, :, :], psR[:, 0, :].rearrange("p (n e) -> p n e", e=E), ALU.add))
            link(eng.scalar_tensor_tensor(rank[:, :, :], first[:, 0, :].unsqueeze(1).to_broadcast([P, NT, E]), float(BLK),
                                          rank[:, :, :], ALU.mult, ALU.add))
            for i in range(2):
                link(eng.tensor_tensor(cand[:, :, :], oh[i][:, :, :], rank[:, :, :], ALU.mult))
                link(eng.tensor_reduce(ix[i][:, :], cand[:, :, :], AX.X, ALU.add))
                step(eng.tensor_copy(pos[:, i, :], ix[i][:, :]))
            cb = cmpb[:, 0:NBLK * E].rearrange("p (k e) -> p k e", e=E)
            link(eng.tensor_tensor(cb, c_sb[:, C_BL:C_BL + NBLK].unsqueeze(2).to_broadcast([P, NBLK, E]),
                                   ends.unsqueeze(1).to_broadcast([P, NBLK, E]), ALU.is_ge))
            link(eng.tensor_reduce(bf[:, :], cb, AX.X, ALU.add))
            step(eng.tensor_scalar(blk_e[:, :], bf[:, :], float(E - 1), None, ALU.min))
            link(eng.scalar_tensor_tensor(fre[:, :], first[:, 0, :], float(BLK), first[:, 1, :], ALU.mult, ALU.subtract))
            jj = c_sb[:, C_FR:C_FR + FREE]
            cf = cmpb[:, 0:FREE * E].rearrange("p (k e) -> p k e", e=E)
            link(eng.tensor_tensor(cf, jj.unsqueeze(2).to_broadcast([P, FREE, E]), fre[:, :].unsqueeze(1).to_broadcast([P, FREE, E]),
                                   ALU.is_ge))
            link(eng.tensor_tensor(cf, cf, nbl[:, 1, :].unsqueeze(1).to_broadcast([P, FREE, E]), ALU.mult))
            link(eng.tensor_reduce(frs[:, :], cf, AX.X, ALU.add))
            step(eng.tensor_tensor(free[:, :], frs[:, :], jj, ALU.add))

    with whole:
        attention(nc, locals())
        experts(nc, locals())


def attention(nc, v):
    NB_, T, QT, N, D, DC, E, H = (v[k] for k in ("NB_", "T", "QT", "N", "D", "DC", "E", "H"))
    NT, HT, SC, ROW, B_Q, B_K, FREE, EARLY, W1, W2 = (v[k] for k in (
        "NT", "HT", "SC", "ROW", "B_Q", "B_K", "FREE", "EARLY", "W1", "W2"))
    pos, free, gate, tok, bias, id32, idb, maskb, pe_sb, bv = (v[k] for k in (
        "pos", "free", "gate", "tok", "bias", "id32", "idb", "maskb", "pe_sb", "bv"))
    wq_p, wkv_p, wo_p, xTb, w1_p, w2_p, xT_d = (v[k] for k in ("wq_p", "wkv_p", "wo_p", "xTb", "w1_p", "w2_p", "xT_d"))
    xp_v, s_v, rows_d, acc_v, w1, w2 = (v[k] for k in ("xp_v", "s_v", "rows_d", "acc_v", "w1", "w2"))
    PRIME = 16
    ORDER = (0, 4, 1, 5, 2, 6, 3, 7)
    CHUNKS = [1 if u < 4 else 2 for u in ORDER]
    CUM = [sum(CHUNKS[:p]) for p in range(9)]
    CH = CUM[8]
    AHEAD_S = (2, 4)
    AHEAD_E = 1
    WC = E * W1 // NT
    LATE = E - EARLY
    PAIRS = sorted(range(QT // 2), key=lambda g: max(ORDER.index(2 * g), ORDER.index(2 * g + 1)))
    ENDS = [max(ORDER.index(2 * g), ORDER.index(2 * g + 1)) for g in PAIRS]
    V = len(PAIRS)
    assert WC == 512 and T == 2 * WC and EARLY * W2 == NT * D
    with ExitStack() as ctx:
        pb, sem = v["tensors"](ctx)
        low = Arena(nc, v["attn_at"])
        sb = low.take
        qp = sb("qp", [P, 2 * HEADS * T], F16)
        kp_at = low.at
        kp = sb("kp", [P, 2, T], F16)
        vp = sb("vp", [P, 2, QT, HD], F16)
        orow = Arena(nc, kp_at).take("orow", [P, 4, 512], F32)
        nmax = sb("nmax", [P, 4], F32)
        rsum = sb("rsum", [P, 4], F32)
        rrec = sb("rrec", [P, 4], F32)
        wst = sb("wpiece", [P, WC + D], F32)
        zrow = sb("rows", [P, 2, ROW], I32)
        rowb = [zrow[:, i, :] for i in range(2)]
        idx = [sb(f"idx{i}", [P, 1], U32) for i in range(2)]
        over = Arena(nc, v["w2_at"] + EARLY * 2 * W2 * 2)
        pT = [over.take(f"pT{g}", [P, 2, 2 * (g + 1), 2 * P], F16) for g in range(4)]
        tmp_at = over.at - 2 * 2 * QT * 2 * P
        wide = [max(ORDER[p], ORDER[p + 4]) + 1 for p in range(4)]
        pr = [over.take(f"pr{i}", [P, wide[i] * P], F32) for i in range(4)]
        assert over.at <= v["rest_at"]
        tmp = Arena(nc, tmp_at).take("tmp", [P, 4, 512], F32)
        w2st = [xTb[:, :, :].rearrange("p c t -> p (c t)").bitcast(F32), wq_p[:, :].bitcast(F32)]
        short = pb("psS0", [P, 1, 512], F32)
        long = [pb(f"psS{i}", [P, 2, 512], F32) for i in (1, 2)]
        psS = [short, long[0], short, long[1]]
        AGO = [2, 4, 2, 4]
        psP = [pb(f"psP{i}", [P, 4, P], F32) for i in range(2)]
        psO = pb("psO", [P, 512], F32)
        bank = [short[:, 0, :], long[0][:, 0, :], long[0][:, 1, :], long[1][:, 0, :]]
        names = ("a_sc", "a_max", "a_exp", "a_rec", "a_nrm", "a_tr", "a_hi", "a_lo", "a_pv", "a_ah", "a_al",
                 "j_mm", "j_t", "j_hi", "j_lo", "o_mm", "o_cp", "a_pr", "a_waited")
        (sc_, mx_, ex_, rc_, nm_, tr_, hi_, lo_, pv_, ah_, al_, jm_, jt_, jh_, jl_, om_, oc_, primed, waited) = map(sem, names)
        od_ = v["od_"]
        xl_, z_, zi_, fr_, za_ = map(sem, ("x_next", "zero_rows", "zero_ids", "free_rows", "zero_acc"))
        w_l, w_h, w_c, w_u = sem("w_ld"), sem("w_hi"), sem("w_scaled"), sem("w_used")
        l_l = [sem(f"late_ld{i}") for i in range(2)]
        l_h, l_o = sem("late_hi"), sem("late_lo")
        r_l = [sem(f"r_ld{i}") for i in range(2)]
        r_c, r_s = sem("r_copy"), sem("r_scatter")
        JOBS = 4 + 2 * HEADS
        block = ctx.enter_context(nc.Block())
        qoff = HEADS * T

        def prime(eng, sems):
            for s in sems:
                eng.sem_inc(s, PRIME)
            eng.sem_inc(primed, 1)

        def at(h, p):
            return h + p // 8, p % 8

        def piece(n, part):
            return ((w1_p[:, ds(n * WC + part * E * W1, WC)], wst[:, 0:WC]),
                    (w2_p[:, ds(n * (2 * D) + part * D, D)], wst[:, WC:]))

        def ahead(p):
            return [p + a for par, a in enumerate(AHEAD_S) if (p + a) % 2 == par]

        NTH = [p + (1 - 2 * (p % 2)) * (AHEAD_S[1] - AHEAD_S[0] == 2) for p in range(8)]
        AT_FIRST = sorted((p for p in range(max(AHEAD_S)) if p < AHEAD_S[p % 2]), key=lambda p: NTH[p])

        @block.tensor
        def _(eng):
            prime(eng, (sc_, tr_, pv_))
            eng.wait_ge(primed, 4)

            def proj(out, lhs, rhs):
                k = 0
                for a, b in PASSES:
                    for c in range(DC):
                        mm = eng.matmul(out, lhs(a, c), rhs(b, c), start=(k == 0), stop=(k == 3 * DC - 1))
                        k += 1
                return mm

            with eng.Fori(0, NB_) as b:
                eng.wait_ge(xl_, b * 16)
                for j in range(2):
                    eng.wait_ge(oc_, b * 4 + (j - 3 + PRIME))
                    proj(bank[j], lambda a, c: wkv_p[:, a, c, 0:HD],
                         lambda a, c: xTb[:, 2 * a + c, j * 512:(j + 1) * 512]).then_inc(jm_, 1)
                for j in range(2):
                    eng.wait_ge(oc_, b * 4 + (j - 1 + PRIME))
                    for t in range(4):
                        mm = proj(bank[2 + j][:, t * P:(t + 1) * P],
                                  lambda a, c: xTb[:, 2 * a + c, (4 * j + t) * P:(4 * j + t + 1) * P],
                                  lambda a, c: wkv_p[:, a, c, HD:2 * HD])
                    mm.then_inc(jm_, 1)
                with eng.Fori(0, HEADS // 2) as hh:
                    for j in range(4):
                        eng.wait_ge(jt_, b * JOBS + hh * 4 + (j + 1))
                        proj(bank[j], lambda a, c: wq_p[:, ds(hh * 2 * HD + ((2 * a + c) * HEADS * HD + (j // 2) * HD), HD)],
                             lambda a, c: xTb[:, 2 * a + c, (j % 2) * 512:(j % 2 + 1) * 512]).then_inc(jm_, 1)

                def scores(h, p):
                    u = ORDER[p]
                    eng.wait_ge(ex_, b * 64 + h * 8 + (p + 1 - AGO[p % 4] + PRIME))
                    n = (u + 1) * P
                    for lo in range(0, n, 512):
                        w = min(512, n - lo)
                        last = lo + w == n
                        o = psS[p % 4][:, lo // 512, 0:w]
                        for k, (a, c) in enumerate(PASSES):
                            mm = eng.matmul(o, qp[:, ds(h * T + (a * qoff + u * P), P)], kp[:, c, lo:lo + w],
                                            start=(k == 0), stop=(k == 2 and not last))
                        if last:
                            mm = eng.matmul(o[:, w - P:w], idb[:, :], maskb[:, :], start=False, stop=True)
                    mm.then_inc(sc_, 1)

                def turn(h, p):
                    u = ORDER[p]
                    eng.wait_ge(nm_, b * 64 + h * 8 + (p + 1 + PRIME))
                    for k in range(CHUNKS[p]):
                        c = CUM[p] + k
                        eng.wait_ge(lo_, b * 8 * CH + h * CH + (c - 1 + PRIME))
                        for t in range(min(4, u + 1 - 4 * k)):
                            mm = eng.transpose(psP[c % 2][:, t, :], pr[p % 4][:, (4 * k + t) * P:(4 * k + t + 1) * P], id32[:, :])
                        mm.then_inc(tr_, 1)

                def values(h, n):
                    g = PAIRS[n]
                    eng.wait_ge(lo_, b * 8 * CH + h * CH + (CUM[ENDS[n] + 1] + PRIME))
                    eng.wait_ge(al_, b * 8 * V + h * V + (n + PRIME))
                    last = 2 * g + 1
                    for j in range(last + 1):
                        q0 = max(0, j - 2 * g) * P
                        for k, (a, c) in enumerate(PASSES):
                            mm = eng.matmul(psO[:, q0:2 * P], vp[:, a, j, :], pT[g][:, c, j, q0:2 * P],
                                            start=(j == 0 and k == 0), stop=(j == last and k == 2))
                    mm.then_inc(pv_, 1)

                def rows_out(j, h0, h1):
                    for i in (2 * j, 2 * j + 1):
                        o = bank[j][:, (i % 2) * D:(i % 2 + 1) * D]
                        for h in range(h0, h1):
                            for k, (a, c) in enumerate(PASSES):
                                mm = eng.matmul(o, qp[:, a * qoff + h * T + i * P:a * qoff + h * T + (i + 1) * P], wo_p[:, c, h, :],
                                                start=(i == 2 * j and h == 0 and k == 0),
                                                stop=(i == 2 * j + 1 and h == HEADS - 1 and k == 2))
                    if h1 == HEADS:
                        mm.then_inc(om_, 1)

                def head(h, first, last):
                    for p in range(8):
                        if p > 1 or not first:
                            turn(*at(h, p - 2))
                        if p == 1 and not first:
                            values(h - 1, 2)
                        if p == 5:
                            values(h, 0)
                        for q in ahead(p):
                            if q < 8 or not last:
                                scores(*at(h, q))
                        if p == 2 and not first:
                            values(h - 1, 3)
                        if p == 6:
                            values(h, 1)

                eng.wait_ge(jl_, b * JOBS + (JOBS - 8))
                for p in AT_FIRST:
                    eng.wait_ge(jt_, b * JOBS + JOBS - (p < 2))
                    scores(0, p)
                head(0, True, False)
                with eng.Fori(1, HEADS - 1) as h:
                    head(h, False, False)
                head(HEADS - 1, False, True)
                eng.wait_ge(ex_, b * 64 + (64 + PRIME))
                turn(HEADS - 1, 6)
                rows_out(0, 0, HEADS - 1)
                turn(HEADS - 1, 7)
                values(HEADS - 1, 2)
                rows_out(1, 0, HEADS - 1)
                values(HEADS - 1, 3)
                rows_out(2, 0, HEADS - 1)
                rows_out(3, 0, HEADS - 1)
                eng.wait_ge(al_, b * 8 * V + (8 * V + PRIME))
                for j in range(4):
                    rows_out(j, HEADS - 1, HEADS)

        @block.scalar
        def _(eng):
            prime(eng, (ex_, hi_, ah_, oc_))
            eng.wait_ge(primed, 4)
            with eng.Fori(0, NB_) as b:
                def job(kind, j, jj, h):
                    eng.wait_ge(jt_, b * JOBS + jj)
                    if kind == "v":
                        eng.activation(vp[:, 0, 4 * (j % 2):4 * (j % 2) + 4, :],
                                       tmp[:, j, :].rearrange("p (t n) -> p t n", n=P), ACT.Copy).then_inc(jh_, 1)
                    elif kind == "k":
                        eng.activation(kp[:, 0, j * 512:(j + 1) * 512], tmp[:, j, :], ACT.Identity,
                                       bias=bias[:, B_K:B_K + 1]).then_inc(jh_, 1)
                    else:
                        eng.activation(qp[:, ds(h * T + (j % 2) * 512, 512)], tmp[:, j, :], ACT.Identity,
                                       bias=bias[:, ds(h + B_Q, 1)]).then_inc(jh_, 1)

                for j in range(4):
                    if j % 2 == 0:
                        eng.wait_ge(od_[j], b * 16)
                    job("kkvv"[j], j, j + 1, None)
                with eng.Fori(0, HEADS // 2) as hh:
                    for j in range(4):
                        job("q", j, hh * 4 + (4 + j + 1), hh * 2 + j // 2)

                def expo(h, p):
                    n = (ORDER[p] + 1) * P
                    eng.wait_ge(mx_, b * 64 + h * 8 + (NTH[p] + 1 + PRIME))
                    eng.wait_ge(tr_, b * 8 * CH + h * CH + ((CUM[p - 3] if p > 3 else CUM[p + 5] - CH) + PRIME))
                    eng.activation(pr[p % 4][:, 0:n], psS[p % 4][:, :, :].rearrange("p a n -> p (a n)")[:, 0:n], ACT.Exp,
                                   bias=nmax[:, p % 4:p % 4 + 1], accum_out=rsum[:, p % 4:p % 4 + 1]).then_inc(ex_, 1)

                def his(h, p):
                    g, qi = ORDER[p] // 2, ORDER[p] % 2
                    eng.wait_ge(pv_, b * 8 * V + h * V + (PAIRS.index(g) + 1 - V + PRIME))
                    for k in range(CHUNKS[p]):
                        c = CUM[p] + k
                        n = min(4, ORDER[p] + 1 - 4 * k)
                        eng.wait_ge(tr_, b * 8 * CH + h * CH + (c + 1 + PRIME))
                        eng.activation(pT[g][:, 0, 4 * k:4 * k + n, qi * P:(qi + 1) * P], psP[c % 2][:, 0:n, :], ACT.Copy).then_inc(hi_, 1)

                def outs(h, n):
                    eng.wait_ge(pv_, b * 8 * V + h * V + (n + 1 + PRIME))
                    eng.activation(qp[:, ds(h * T + PAIRS[n] * 2 * P, 2 * P)], psO[:, 0:2 * P], ACT.Copy).then_inc(ah_, 1)

                def head(h, first, last):
                    for p in range(8):
                        if p > 1 or not first:
                            his(*at(h, p - 2))
                        if p in (1, 3) and not first:
                            outs(h - 1, 2 + p // 2)
                        if p in (5, 7):
                            outs(h, p // 2 - 2)
                        if p + AHEAD_E < 8 or not last:
                            expo(*at(h, p + AHEAD_E))
                        if p == 4:
                            n = b * HEADS + h
                            eng.wait_ge(w_l, n * 32 + 32)
                            for dst, src in piece(n, 0):
                                a = eng.activation(dst, src, ACT.Copy, scale=WS)
                            a.then_inc(w_h, 1)

                for p in range(AHEAD_E):
                    expo(0, p)
                head(0, True, False)
                with eng.Fori(1, HEADS - 1) as h:
                    head(h, False, False)
                head(HEADS - 1, False, True)
                his(HEADS - 1, 6)
                his(HEADS - 1, 7)
                outs(HEADS - 1, 2)
                outs(HEADS - 1, 3)
                for j in range(4):
                    eng.wait_ge(om_, b * 4 + (j + 1))
                    eng.activation(orow[:, j, :], bank[j], ACT.Copy, scale=1.0 / WS).then_inc(oc_, 1)

        @block.vector
        def _(eng):
            prime(eng, (mx_, rc_, lo_, al_))
            eng.wait_ge(primed, 4)
            with eng.Fori(0, NB_) as b:
                def unscale(kind, j, jj, lojj):
                    eng.wait_ge(jm_, b * JOBS + jj)
                    eng.wait_ge(jl_, b * JOBS + lojj)
                    if kind == "v":
                        eng.scalar_tensor_tensor(tmp[:, j, :].rearrange("p (t n) -> p t n", n=P),
                                                 bank[j].rearrange("p (t n) -> p t n", n=P), 1.0 / WS,
                                                 bv[:, :].unsqueeze(1).to_broadcast([P, 4, P]), ALU.mult, ALU.add).then_inc(jt_, 1)
                    else:
                        eng.scalar_tensor_tensor(tmp[:, j, :], bank[j], SC / WS, pe_sb[:, (j % 2) * 512:(j % 2 + 1) * 512],
                                                 ALU.mult, ALU.add).then_inc(jt_, 1)

                def rest(kind, j, jj, h):
                    eng.wait_ge(jh_, b * JOBS + jj)
                    if kind != "q":
                        eng.wait_ge(od_[1 if kind == "k" else 3], b * 16)
                    if kind == "v":
                        sl = slice(4 * (j % 2), 4 * (j % 2) + 4)
                        eng.tensor_tensor(vp[:, 1, sl, :], tmp[:, j, :].rearrange("p (t n) -> p t n", n=P), vp[:, 0, sl, :],
                                          ALU.subtract).then_inc(jl_, 1)
                    elif kind == "k":
                        eng.scalar_tensor_tensor(kp[:, 1, j * 512:(j + 1) * 512], tmp[:, j, :], bias[:, B_K:B_K + 1],
                                                 kp[:, 0, j * 512:(j + 1) * 512], ALU.add, ALU.subtract).then_inc(jl_, 1)
                    else:
                        eng.scalar_tensor_tensor(qp[:, ds(h * T + (qoff + (j % 2) * 512), 512)], tmp[:, j, :],
                                                 bias[:, ds(h + B_Q, 1)], qp[:, ds(h * T + (j % 2) * 512, 512)],
                                                 ALU.add, ALU.subtract).then_inc(jl_, 1)

                for j in range(4):
                    unscale("kkvv"[j], j, j + 1, 0)
                    if j:
                        rest("kkvv"[j - 1], j - 1, j, None)

                def q_jobs(hh, first):
                    for j in range(4):
                        unscale("q", j, hh * 4 + (4 + j + 1), hh * 4 + (j + 1))
                        if j or not first:
                            rest("q", (j - 1) % 4, hh * 4 + (4 + j), hh * 2 + (j - 1) // 2)
                        else:
                            rest("v", 3, 4, None)
                q_jobs(0, True)
                with eng.Fori(1, HEADS // 2) as hh:
                    q_jobs(hh, False)
                rest("q", 3, JOBS, HEADS - 1)

                def maxi(h, p):
                    n = (ORDER[p] + 1) * P
                    eng.wait_ge(sc_, b * 64 + h * 8 + (NTH[p] + 1 + PRIME))
                    eng.tensor_reduce(nmax[:, p % 4:p % 4 + 1], psS[p % 4][:, :, :].rearrange("p a n -> p (a n)")[:, 0:n],
                                      AX.X, ALU.max, negate=True).then_inc(mx_, 1)

                def rec(h, p):
                    eng.wait_ge(ex_, b * 64 + h * 8 + (p + 1 + PRIME))
                    eng.wait_ge(nm_, b * 64 + h * 8 + (p - 3 + PRIME))
                    eng.reciprocal(rrec[:, p % 4:p % 4 + 1], rsum[:, p % 4:p % 4 + 1]).then_inc(rc_, 1)

                def los(h, p):
                    g, qi = ORDER[p] // 2, ORDER[p] % 2
                    for k in range(CHUNKS[p]):
                        c = CUM[p] + k
                        n = min(4, ORDER[p] + 1 - 4 * k)
                        eng.wait_ge(hi_, b * 8 * CH + h * CH + (c + 1 + PRIME))
                        o = pT[g][:, :, 4 * k:4 * k + n, qi * P:(qi + 1) * P]
                        eng.tensor_tensor(o[:, 1], psP[c % 2][:, 0:n, :], o[:, 0], ALU.subtract).then_inc(lo_, 1)

                def outs(h, n):
                    eng.wait_ge(ah_, b * 8 * V + h * V + (n + 1 + PRIME))
                    at_ = PAIRS[n] * 2 * P
                    eng.tensor_tensor(qp[:, ds(h * T + (qoff + at_), 2 * P)], psO[:, 0:2 * P], qp[:, ds(h * T + at_, 2 * P)],
                                      ALU.subtract).then_inc(al_, 1)

                def head(h, first, last):
                    for p in range(8):
                        rec(h, p)
                        if p > 1 or not first:
                            los(*at(h, p - 2))
                        if p in (1, 3) and not first:
                            outs(h - 1, 2 + p // 2)
                        if p in (5, 7):
                            outs(h, p // 2 - 2)
                        for q in ahead(p):
                            if q < 8 or not last:
                                maxi(*at(h, q))

                for p in AT_FIRST:
                    maxi(0, p)
                head(0, True, False)
                with eng.Fori(1, HEADS - 1) as h:
                    head(h, False, False)
                head(HEADS - 1, False, True)
                los(HEADS - 1, 6)
                los(HEADS - 1, 7)
                outs(HEADS - 1, 2)
                outs(HEADS - 1, 3)
            for n in range(LATE):
                e = EARLY + n
                eng.wait_ge(l_l[n % 2], 16 * (n // 2 + 1))
                w = w2_p[:, 2 * e * W2:2 * (e + 1) * W2].rearrange("p (m a w) -> p a m w", a=2, w=D)
                src = w2st[n % 2].rearrange("p (m w) -> p m w", w=D)
                eng.tensor_scalar(w[:, 0], src, WS, None, ALU.mult).then_inc(l_h, 1)
                eng.wait_ge(l_h, n + 1)
                eng.scalar_tensor_tensor(w[:, 1], src, WS, w[:, 0], ALU.mult, ALU.subtract).then_inc(l_o, 1)

        @block.gpsimd
        def _(eng):
            def wait(sem, value):
                eng.wait_ge(sem, value)
                eng.sem_inc(waited, 1)

            prime(eng, (nm_,))
            eng.memset(zrow[:, :, :], 0).then_inc(z_, 1)
            wait(z_, 1)
            for t in range(2):
                eng.iota(zrow[:, t, D:D + 1], [[1, 1]], base=N + t * P, channel_multiplier=1).then_inc(zi_, 1)
            wait(zi_, 2)
            for k in range(FREE):
                eng.indirect_dma_start(rows_d, bass.IndirectOffsetOnAxis(ap=free[:, k:k + 1], axis=0),
                                       zrow[:, k % 2, :], None).then_inc(fr_, 16)
            wait(primed, 4)
            wait(fr_, FREE * 16)
            wait(za_, 16)
            with eng.Fori(0, NB_) as b:
                with eng.Fori(0, HEADS) as h:
                    n = b * HEADS + h
                    for p in range(8):
                        w = (ORDER[p] + 1) * P
                        wait(rc_, b * 64 + h * 8 + (p + 1 + PRIME))
                        eng.tensor_scalar(pr[p % 4][:, 0:w], pr[p % 4][:, 0:w], rrec[:, p % 4:p % 4 + 1], 1.0,
                                          ALU.mult, ALU.mult).then_inc(nm_, 1)
                        if p == 0:
                            wait(r_s, n * 32)
                            for s in range(2):
                                eng.tensor_copy(rowb[s][:, D:D + 1], tok[:, ds(n, 1)]).then_inc(r_c, 1)
                                eng.tensor_copy(rowb[s][:, D + 1:D + 2].bitcast(F32), gate[:, s, ds(n, 1)]).then_inc(r_c, 1)
                                eng.tensor_copy(idx[s][:, :], pos[:, s, ds(n, 1)]).then_inc(r_c, 1)
                        if p in (2, 4):
                            s = p // 2 - 1
                            wait(r_c, n * 6 + 6)
                            wait(r_l[s], n * 16 + 16)
                            eng.indirect_dma_start(rows_d, bass.IndirectOffsetOnAxis(ap=idx[s][:, 0:1], axis=0),
                                                   rowb[s], None).then_inc(r_s, 16)
                        if p == 5:
                            wait(w_h, n + 1)
                            eng.tensor_scalar(wst[:, :], wst[:, :], WS, 1.0, ALU.mult, ALU.mult).then_inc(w_c, 1)
                        if p == 7:
                            wait(w_c, n + 1)
                            for (lo, src), (hi, _) in zip(piece(n, 1), piece(n, 0)):
                                a = eng.tensor_tensor(lo, src, hi, ALU.subtract)
                            a.then_inc(w_u, 1)
            wait(r_s, NT * 32)
        @block.sync
        def _(eng):
            w1v = w1.rearrange("e (c p) n -> (e c) p n", p=P)
            w2v = w2.rearrange("e (g p) d -> e p g d", p=P)
            w2f = w2.rearrange("e (g p) d -> (e g) p d", p=P)
            eng.wait_ge(zi_, 2)
            eng.dma_start(acc_v, zrow[:, 0, 0:D].bitcast(F32).unsqueeze(1).to_broadcast([P, acc_v.shape[1], D])).then_inc(za_, 16)

            def batch(b, last):
                with eng.Fori(0, HEADS // 2) as hh:
                    for par in range(2):
                        n = b * HEADS + hh * 2 + par
                        m = b * (HEADS // 2) + hh
                        eng.wait_ge(r_s, m * 64 + par * 32)
                        for s in range(2):
                            eng.dma_start(rowb[s][:, 0:D].bitcast(F16), xp_v[:, ds(n, 1), :].squeeze(1)).then_inc(r_l[s], 16)
                        eng.wait_ge(w_u, n)
                        eng.dma_start(wst[:, 0:WC], w1v[:, :, par * WC:(par + 1) * WC][ds(m, 1)].squeeze(0)).then_inc(w_l, 16)
                        eng.dma_start(wst[:, WC:], w2f[ds(n, 1)].squeeze(0)).then_inc(w_l, 16)
                if not last:
                    eng.wait_ge(jm_, b * JOBS + JOBS)
                    eng.dma_start(xTb[:, :, :], xT_d[:, :, ds(b * T + T, T)]).then_inc(xl_, 16)
                else:
                    eng.wait_ge(jm_, b * JOBS + JOBS)
                    for n in range(LATE):
                        if n >= 2:
                            eng.wait_ge(l_o, n - 1)
                        eng.dma_start(w2st[n % 2].rearrange("p (g d) -> p g d", d=D), w2v[EARLY + n]).then_inc(l_l[n % 2], 16)
                    eng.wait_ge(r_s, NT * 32)
                    eng.wait_ge(jt_, NB_ * JOBS)
                    for j in range(v["R"]):
                        eng.dma_start(v["rowx"][j][:, :, :], v["rows_v"][:, 2 * j:2 * j + 2, 0:D]).then_inc(v["ld"][j], 16)
                        eng.dma_start(v["tag"][j][:, :, :], v["rows_v"][:, 2 * j:2 * j + 2, D:ROW]).then_inc(v["lt"][j], 16)
                for j in range(4):
                    eng.wait_ge(oc_, b * 4 + (j + 1 + PRIME))
                    eng.dma_start(s_v[:, ds(b * QT + 2 * j, 2), :], orow[:, j, :].rearrange("p (i d) -> p i d", d=D)).then_inc(od_[j], 16)

            eng.wait_ge(fr_, FREE * 16)
            eng.wait_ge(za_, 16)
            with eng.Fori(0, NB_ - 1) as b:
                batch(b, False)
            batch(NB_ - 1, True)


def experts(nc, v):
    N, D, DC, E, H, HT, NT, NBLK, ROW = (v[k] for k in ("N", "D", "DC", "E", "H", "HT", "NT", "NBLK", "ROW"))
    blk_e, bias, id16, w1_p, w2_p, b2, rows_v, acc_d, W1, W2 = (v[k] for k in (
        "blk_e", "bias", "id16", "w1_p", "w2_p", "b2", "rows_v", "acc_d", "W1", "W2"))
    R, rowx, tag, ld, lt = (v[k] for k in ("R", "rowx", "tag", "ld", "lt"))
    UPS = HT // 2
    G, B = 2, 4
    with ExitStack() as ctx:
        pb, sem = v["tensors"](ctx)
        arena = Arena(nc, v["experts_at"])
        sb = arena.take
        b2b = sb("b2b", [P, E * D], F32)
        bxT = [sb(f"bxT{i}", [P, 2 * DC, BLK], F16) for i in range(R)]
        h32 = [sb(f"h32_{i}", [P, 2, BLK], F32) for i in range(UPS)]
        hp = [sb(f"hp{i}", [P, 2, HT, BLK], F16) for i in range(R)]
        y = [sb(f"y{i}", [P, 2, D], F32) for i in range(R)]
        pre = [sb(f"pre{i}", [P, B * G, D], F32) for i in range(2)]
        psX = pb("psX", [P, 2 * DC, BLK], F16)
        psU = [pb(f"psU{i}", [P, 2, BLK], F32) for i in range(UPS)]
        psY = [pb(f"psY{i}", [P, 2, D], F32) for i in range(R)]
        b_l, p_l = sem("b_l"), sem("pre_ld")
        (xt_, xc_, up_, rl_, hh_, hl_, dn_, yb_, yg_, sc_) = map(sem, (
            "e_xt", "e_xc", "e_up", "e_relu", "e_hi", "e_lo", "e_down", "e_yb", "e_yg", "e_add"))
        primed, waited = sem("e_primed"), sem("e_waited")
        PR = 16

        def prime(eng, sems):
            for s in sems:
                eng.sem_inc(s, PR)
            eng.sem_inc(primed, 1)

        ctx2 = ctx.enter_context(ExitStack())
        block = ctx2.enter_context(nc.Block())

        @block.sync
        def _(eng):
            eng.dma_start(b2b[:, :], b2.rearrange("e d -> (e d)").partition_broadcast(P)).then_inc(b_l, 16)
            eng.wait_ge(primed, 4)

            def load(m, j):
                eng.wait_ge(xt_, m * R + (j - 2 + PR))
                eng.sem_inc(waited, 1)
                eng.dma_start(rowx[j][:, :, :], rows_v[:, ds(m * R * 2 + 2 * j, 2), 0:D]).then_inc(ld[j], 16)

            def tags(m, j):
                eng.wait_ge(sc_, m * R * 32 + (j - 2) * 32)
                eng.sem_inc(waited, 1)
                eng.dma_start(tag[j % R][:, :, :], rows_v[:, ds(m * R * 2 + 2 * j, 2), D:ROW]).then_inc(lt[j % R], 16)

            load(1, 0)
            load(1, 1)
            tags(1, 0)
            load(1, 2)
            tags(1, 1)
            for o in v["od_"]:
                eng.wait_ge(o, v["NB_"] * 16)
            for dst, src in zip(pre, (v["s_v"], v["xf"])):
                eng.dma_start(dst[:, :, :], src[:, 0:B * G, :]).then_inc(p_l, 16)
            with eng.Fori(2, NBLK // R) as m:
                for j in range(R):
                    load(m, j)
                    tags(m, j - 1)
            tags(NBLK // R - 1, R - 1)
            eng.wait_ge(p_l, 32)

        @block.tensor
        def _(eng):
            prime(eng, (xt_, up_, dn_))
            eng.wait_ge(primed, 4)

            def expert(m, j):
                return eng.value_load(blk_e[0:1, ds(m * R + j, 1)], min_val=0, max_val=E - 1)

            def turn(m, j):
                eng.wait_ge(ld[j % R], m * 16 + 16 * (j // R + 1))
                eng.wait_ge(xc_, m * R + (j + PR))
                for t in range(2):
                    for h in range(2):
                        for c in range(DC):
                            mm = eng.transpose(psX[:, 2 * h + c, t * P:(t + 1) * P],
                                               rowx[j % R][:, t, :].bitcast(F16)[:, h * D + c * P:h * D + (c + 1) * P], id16[:, :])
                mm.then_inc(xt_, 1)

            def up(m, j):
                e = expert(m, j)
                eng.wait_ge(xc_, m * R + (j + 1 + PR))
                for u in range(UPS):
                    eng.wait_ge(rl_, m * R * UPS + ((j - 1) * UPS + u + 1 + PR))
                    for g in range(2):
                        n = 0
                        for a, b in PASSES:
                            for c in range(DC):
                                mm = eng.matmul(psU[u][:, g, :], w1_p[:, ds(e * W1 + (a * E * W1 + c * H + (2 * u + g) * P), P)],
                                                bxT[j][:, 2 * b + c, :], start=(n == 0), stop=(n == 3 * DC - 1))
                                n += 1
                    mm.then_inc(up_, 1)

            def down(m, j):
                e = expert(m, j)
                eng.wait_ge(hl_, m * R * UPS + ((j + 1) * UPS + PR))
                eng.wait_ge(yb_, m * R * 2 + ((j - 2) * 2 + PR))
                for t in range(2):
                    n = 0
                    for g in range(HT):
                        for a, b in PASSES:
                            mm = eng.matmul(psY[j % R][:, t, :], hp[j % R][:, a, g, t * P:(t + 1) * P],
                                            w2_p[:, ds(e * (2 * W2) + ((2 * g + b) * D), D)],
                                            start=(n == 0), stop=(n == 3 * HT - 1))
                            n += 1
                mm.then_inc(dn_, 1)

            def blocks(m, first, last):
                for j in range(R):
                    up(m, j)
                    if not (last and j == R - 1):
                        turn(m, j + 1)
                    if not (first and j == 0):
                        down(m, j - 1)

            turn(0, 0)
            blocks(0, True, False)
            with eng.Fori(1, NBLK // R - 1) as m:
                blocks(m, False, False)
            blocks(NBLK // R - 1, False, True)
            down(NBLK // R - 1, R - 1)

        @block.scalar
        def _(eng):
            prime(eng, (xc_, rl_))
            eng.wait_ge(primed, 4)
            with eng.Fori(0, NBLK // R) as m:
                for j in range(R):
                    e = eng.value_load(blk_e[0:1, ds(m * R + j, 1)], min_val=0, max_val=E - 1)
                    eng.wait_ge(xt_, m * R + (j + 1 + PR))
                    eng.wait_ge(up_, m * R * UPS + ((j - 2) * UPS + PR))
                    eng.activation(bxT[j][:, :, :], psX[:, :, :], ACT.Copy).then_inc(xc_, 1)
                    for u in range(UPS):
                        eng.wait_ge(up_, m * R * UPS + (j * UPS + u + 1 + PR))
                        eng.wait_ge(hl_, m * R * UPS + ((j - 1) * UPS + u + 1 + PR))
                        for g in range(2):
                            a = eng.activation(h32[u][:, g, :], psU[u][:, g, :], ACT.Relu,
                                               bias=bias[:, ds(e * HT + (2 * u + g), 1)], scale=1.0 / WS)
                        a.then_inc(rl_, 1)

        @block.vector
        def _(eng):
            prime(eng, (hh_, hl_, yb_))
            eng.wait_ge(primed, 4)
            eng.wait_ge(b_l, 16)

            def hidden(m, j):
                def hi(u):
                    eng.wait_ge(rl_, m * R * UPS + (j * UPS + u + 1 + PR))
                    if u == 0:
                        eng.wait_ge(dn_, m * R + (j - 2 + PR))
                    eng.tensor_copy(hp[j][:, 0, 2 * u:2 * u + 2, :], h32[u][:, :, :]).then_inc(hh_, 1)

                def lo(u):
                    eng.wait_ge(hh_, m * R * UPS + (j * UPS + u + 1 + PR))
                    eng.tensor_tensor(hp[j][:, 1, 2 * u:2 * u + 2, :], h32[u][:, :, :], hp[j][:, 0, 2 * u:2 * u + 2, :],
                                      ALU.subtract).then_inc(hl_, 1)
                for u in range(UPS):
                    hi(u)
                    if u:
                        lo(u - 1)
                lo(UPS - 1)

            def rows(m, j):
                e = eng.value_load(blk_e[0:1, ds(m * R + j, 1)], min_val=0, max_val=E - 1)
                eng.wait_ge(dn_, m * R + (j + 1 + PR))
                if not isinstance(m, int) or m * R + j > 2:
                    eng.wait_ge(sc_, m * R * 32 + (j - 2) * 32)
                for t in range(2):
                    eng.scalar_tensor_tensor(y[j % R][:, t, :], psY[j % R][:, t, :], 1.0 / WS, b2b[:, ds(e * D, D)],
                                             ALU.mult, ALU.add).then_inc(yb_, 1)

            for j in range(R):
                hidden(0, j)
                if j:
                    rows(0, j - 1)
            with eng.Fori(1, NBLK // R) as m:
                for j in range(R):
                    hidden(m, j)
                    rows(m, j - 1)
            rows(NBLK // R - 1, R - 1)

        @block.gpsimd
        def _(eng):
            def wait(sem, value):
                eng.wait_ge(sem, value)
                eng.sem_inc(waited, 1)

            prime(eng, (yg_,))
            wait(primed, 4)
            with eng.Fori(0, NBLK // R) as m:
                for j in range(R):
                    wait(yb_, m * R * 2 + (2 * j + 2 + PR))
                    wait(lt[j], m * 16 + 16)
                    for t in range(2):
                        eng.tensor_scalar(y[j][:, t, :], y[j][:, t, :], tag[j][:, t, 1:2].bitcast(F32), 1.0,
                                          ALU.mult, ALU.mult).then_inc(yg_, 1)
                    wait(yg_, m * R * 2 + (2 * j + 2 + PR))
                    wait(sc_, m * R * 32 + j * 32)
                    for t in range(2):
                        eng.indirect_dma_start(acc_d, bass.IndirectOffsetOnAxis(ap=tag[j][:, t, 0:1].bitcast(U32), axis=0),
                                               y[j][:, t, :], None, compute_op=ALU.add).then_inc(sc_, 16)
            wait(sc_, NBLK * 32)

    xf, of, s_v, acc_v = (v[k] for k in ("xf", "of", "s_v", "acc_v"))
    STEPS = NT // G
    with ExitStack() as ctx:
        pb, sem = v["tensors"](ctx)
        sb = Arena(nc, v["rest_at"]).take
        fb = [sb(f"fb{i}", [P, G, D], F32) for i in range(B)]
        gb = [sb(f"gb{i}", [P, G, D], F32) for i in range(B)]
        sbf = [sb(f"sbf{i}", [P, G, D], F32) for i in range(B)]
        xb = [sb(f"xb{i}", [P, G, D], F32) for i in range(B)]
        f_l = [sem(f"f_ld{i}") for i in range(B)]
        f_o = [sem(f"f_out{i}") for i in range(B)]
        f_g, f_m, f_a, f_w, f_p = map(sem, ("f_silu", "f_mul", "f_add", "f_waited", "f_first_out"))
        block = ctx.enter_context(nc.Block())

        @block.sync
        def _(eng):
            for j in range(B):
                eng.dma_start(fb[j][:, :, :], acc_v[:, j * G:(j + 1) * G, :]).then_inc(f_l[j], 16)
            with eng.Fori(1, STEPS // B) as m:
                for j in range(B):
                    eng.wait_ge(f_g, m * B + (j + 1 - B))
                    eng.wait_ge(f_m, m * B + (j + 1 - B))
                    eng.wait_ge(f_o[j], m * 16 - 16)
                    for dst, src in ((fb, acc_v), (sbf, s_v), (xb, xf)):
                        eng.dma_start(dst[j][:, :, :], src[:, ds(m * B * G + j * G, G), :]).then_inc(f_l[j], 16)

        @block.scalar
        def _(eng):
            def silu(m, j):
                eng.wait_ge(f_l[j], m * 48 + 16)
                eng.activation(gb[j][:, :, :], fb[j][:, :, :], ACT.Silu).then_inc(f_g, 1)

            for j in range(B):
                silu(0, j)
            with eng.Fori(1, STEPS // B) as m:
                for j in range(B):
                    eng.wait_ge(f_a, m * B + (j + 1 - B))
                    silu(m, j)

        @block.vector
        def _(eng):
            def step(m, j, att, inp):
                eng.wait_ge(f_g, m * B + (j + 1))
                eng.tensor_tensor(gb[j][:, :, :], gb[j][:, :, :], att, ALU.mult).then_inc(f_m, 1)
                eng.wait_ge(f_m, m * B + (j + 1))
                eng.tensor_tensor(inp, gb[j][:, :, :], inp, ALU.add).then_inc(f_a, 1)

            for j in range(B):
                step(0, j, *(t[:, j * G:(j + 1) * G, :] for t in pre))
            with eng.Fori(1, STEPS // B) as m:
                for j in range(B):
                    step(m, j, sbf[j][:, :, :], xb[j][:, :, :])

        @block.gpsimd
        def _(eng):
            def store(m, j, src, done):
                eng.wait_ge(f_a, m * B + (j + 1))
                eng.sem_inc(f_w, 1)
                eng.dma_start(of[:, ds(m * B * G + j * G, G), :], src).then_inc(done, 16)

            for j in range(B):
                store(0, j, pre[1][:, j * G:(j + 1) * G, :], f_p)
            with eng.Fori(1, STEPS // B) as m:
                for j in range(B):
                    store(m, j, xb[j][:, :, :], f_o[j])
            eng.wait_ge(f_p, B * 16)
            for j in range(B):
                eng.wait_ge(f_o[j], (STEPS // B - 1) * 16)


_INS = ["L0_attn_x", "L0_attn_Wq", "L0_attn_bq", "L0_attn_Wkv", "L0_attn_bkv", "L0_attn_Wo", "L0_ffn_router_w",
        "L0_ffn_router_b", "L0_ffn_w1", "L0_ffn_b1", "L0_ffn_w2", "L0_ffn_b2"]


def kernel(**inputs):
    import concourse.bacc as _bacc
    from concourse.bass_utils import run_bass_kernel_spmd as _run

    nc = _bacc.Bacc("TRN2", target_bir_lowering=False, num_devices=1)
    arrays, args = {}, []

    def given(name, a):
        arrays[name] = a
        args.append(nc.dram_tensor(name, a.shape, mybir.dt.from_np(a.dtype), kind="ExternalInput").ap())

    for name in _INS:
        given(f"in_{name}", np.ascontiguousarray(inputs[name]))
    shape = tuple(inputs["L0_attn_x"].shape)
    for name, a in zip(("tables", "positions"), constants(shape[0] * shape[1], inputs["L0_ffn_w1"].shape[0], shape[1])):
        given(name, a)
    args.append(nc.dram_tensor("out", shape, F32, kind="ExternalOutput").ap())
    build(nc, *args)
    r = _run(nc, [arrays], core_ids=[0])
    return r.results[0]["out"]
```
